# Optimizing a Trainium2 kernel written in Bass

```python
import numpy as np
import jax
import jax.numpy as jnp

def _softmax(x, axis=-1):
    return jax.nn.softmax(x, axis=axis)

def _gelu(x):
    return jax.nn.gelu(x, approximate=True)

def _silu(x):
    return jax.nn.silu(x)

def _sigmoid(x):
    return jax.nn.sigmoid(x)

def _layernorm(x, axis=-1, eps=1e-05):
    m = jnp.mean(x, axis=axis, keepdims=True)
    v = jnp.var(x, axis=axis, keepdims=True)
    return (x - m) / jnp.sqrt(v + eps)

def _scatter_add(tgt, idx, src, axis=0):
    return tgt.at[idx].add(src)

def _segment_sum(src, seg, n):
    return jax.ops.segment_sum(src, seg, n)
kernel_name = 'mk_flamingo_gated_d1_seqx_r8_f7473f'

def setup_inputs(seed: int=0):
    np.random.seed(seed)
    _w = jnp.asarray

    def _rec_inputs():
        import jax
        import jax.numpy as jnp
        _rk = jax.random.key(seed)
        x = -0.0002928 + 1 * jax.random.normal(jax.random.fold_in(_rk, 1), (8, 256, 128), jnp.float32)
        _lenS = 256 - jax.random.randint(jax.random.fold_in(_rk, 7), (8,), 0, max(1, 256 // 4) + 1, jnp.int32)
        _lenS2 = 64 - jax.random.randint(jax.random.fold_in(_rk, 8), (8,), 0, max(1, 64 // 4) + 1, jnp.int32)
        _ctx_512P = jax.random.normal(jax.random.fold_in(_rk, 11), (8, 16, 64), jnp.float32)
        _ctx_512c = jax.random.dirichlet(jax.random.fold_in(_rk, 511), 0.3 * jnp.ones((16,), jnp.float32), (8, 64))
        _ctx_512t = jnp.einsum('bsk,bkd->bsd', _ctx_512c, _ctx_512P)
        _ctx_512t = _ctx_512t * jax.lax.rsqrt(jnp.mean(jnp.square(_ctx_512t)) + 1e-12) * 0.953939
        ctx_512 = 0.00222621 + 0.99962 * (_ctx_512t + 0.3 * jax.random.normal(jax.random.fold_in(_rk, 611), (8, 64, 64), jnp.float32))
        _g = jax.random.normal(jax.random.fold_in(_rk, 9001), (2, 1), jnp.float32)
        _g = jnp.sign(_g) * jnp.maximum(jnp.abs(_g), 1.0) + (_g == 0) * 1.0
        g_xattn = _g[0]
        g_ffn = _g[1]
        return (x, ctx_512, g_xattn, g_ffn)
    x, ctx_512, g_xattn, g_ffn = _rec_inputs()

    def _L0_xattn_setup():
        import jax, jax.numpy as jnp
        import numpy as np
        B, T, TC, C, CC, H = (2, 256, 64, 128, 64, 16)
        D = C // H

        def _heads(t):
            b, l, _ = t.shape
            return t.reshape(b, l, H, D).transpose(0, 2, 1, 3)
        key = jax.random.key(seed)
        ks = jax.random.split(key, 18)
        w = lambda k, i, o: jax.random.normal(k, (i, o), jnp.float32) / np.sqrt(i).astype(np.float32)
        return {'x': jax.random.normal(ks[0], (B, T, C), jnp.float32), 'cross_input': jax.random.normal(ks[1], (B, TC, CC), jnp.float32), 'Wk': w(ks[2], C, C), 'bk': jnp.zeros((C,), jnp.float32), 'Wq': w(ks[3], C, C), 'bq': jnp.zeros((C,), jnp.float32), 'Wv': w(ks[4], C, C), 'bv': jnp.zeros((C,), jnp.float32), 'Wck': w(ks[5], CC, C), 'bck': jnp.zeros((C,), jnp.float32), 'Wcq': w(ks[6], C, C), 'bcq': jnp.zeros((C,), jnp.float32), 'Wcv': w(ks[7], CC, C), 'bcv': jnp.zeros((C,), jnp.float32), 'Wp': w(ks[8], C, C), 'bp': jnp.zeros((C,), jnp.float32)}
    _L0_xattn_all = _L0_xattn_setup()
    _L0_xattn_in = {k: v for k, v in _L0_xattn_all.items() if k in ('Wk', 'bk', 'Wq', 'bq', 'Wv', 'bv', 'Wck', 'bck', 'Wcq', 'bcq', 'Wcv', 'bcv', 'Wp', 'bp')}
    del _L0_xattn_all

    def _L0_ffn_setup():
        import jax, jax.numpy as jnp
        import numpy as np
        B, S, D, F, E = (4, 256, 128, 512, 8)
        LN_EPS = 1e-05
        key = jax.random.key(seed)
        ks = jax.random.split(key, 6)
        sc = 0.02
        return {'x': jax.random.normal(ks[0], (B, S, D), dtype=jnp.float32), 'Wr': jax.random.normal(ks[1], (D, E), dtype=jnp.float32) * sc, 'br': jnp.zeros((E,), jnp.float32), 'ln_g': jnp.ones((D,), jnp.float32), 'ln_b': jnp.zeros((D,), jnp.float32), 'W1': jax.random.normal(ks[2], (E, D, F), dtype=jnp.float32) * sc, 'b1': jnp.zeros((E, F), jnp.float32), 'W2': jax.random.normal(ks[3], (E, F, D), dtype=jnp.float32) * sc, 'b2': jnp.zeros((E, D), jnp.float32)}
    _L0_ffn_all = _L0_ffn_setup()
    _L0_ffn_in = {k: v for k, v in _L0_ffn_all.items() if k in ('Wr', 'br', 'ln_g', 'ln_b', 'W1', 'b1', 'W2', 'b2')}
    del _L0_ffn_all
    return {'x': x, 'ctx_512': ctx_512, 'g_xattn': g_xattn, 'g_ffn': g_ffn, 'L0_xattn_Wk': _L0_xattn_in['Wk'], 'L0_xattn_bk': _L0_xattn_in['bk'], 'L0_xattn_Wq': _L0_xattn_in['Wq'], 'L0_xattn_bq': _L0_xattn_in['bq'], 'L0_xattn_Wv': _L0_xattn_in['Wv'], 'L0_xattn_bv': _L0_xattn_in['bv'], 'L0_xattn_Wck': _L0_xattn_in['Wck'], 'L0_xattn_bck': _L0_xattn_in['bck'], 'L0_xattn_Wcq': _L0_xattn_in['Wcq'], 'L0_xattn_bcq': _L0_xattn_in['bcq'], 'L0_xattn_Wcv': _L0_xattn_in['Wcv'], 'L0_xattn_bcv': _L0_xattn_in['bcv'], 'L0_xattn_Wp': _L0_xattn_in['Wp'], 'L0_xattn_bp': _L0_xattn_in['bp'], 'L0_ffn_Wr': _L0_ffn_in['Wr'], 'L0_ffn_br': _L0_ffn_in['br'], 'L0_ffn_ln_g': _L0_ffn_in['ln_g'], 'L0_ffn_ln_b': _L0_ffn_in['ln_b'], 'L0_ffn_W1': _L0_ffn_in['W1'], 'L0_ffn_b1': _L0_ffn_in['b1'], 'L0_ffn_W2': _L0_ffn_in['W2'], 'L0_ffn_b2': _L0_ffn_in['b2']}

def reference(x, ctx_512, g_xattn, g_ffn, L0_xattn_Wk, L0_xattn_bk, L0_xattn_Wq, L0_xattn_bq, L0_xattn_Wv, L0_xattn_bv, L0_xattn_Wck, L0_xattn_bck, L0_xattn_Wcq, L0_xattn_bcq, L0_xattn_Wcv, L0_xattn_bcv, L0_xattn_Wp, L0_xattn_bp, L0_ffn_Wr, L0_ffn_br, L0_ffn_ln_g, L0_ffn_ln_b, L0_ffn_W1, L0_ffn_b1, L0_ffn_W2, L0_ffn_b2):
    import jax
    import jax.numpy as jnp

    def _L0_xattn_ref(x, cross_input, Wk, bk, Wq, bq, Wv, bv, Wck, bck, Wcq, bcq, Wcv, bcv, Wp, bp):
        import jax, jax.numpy as jnp
        import numpy as np
        B, T, TC, C, CC, H = (2, 256, 64, 128, 64, 16)
        D = C // H

        def _heads(t):
            b, l, _ = t.shape
            return t.reshape(b, l, H, D).transpose(0, 2, 1, 3)
        scale = np.float32(1.0 / np.sqrt(D))
        q = _heads(x @ Wq + bq)
        k = _heads(x @ Wk + bk)
        v = _heads(x @ Wv + bv)
        att = jnp.einsum('bhqd,bhkd->bhqk', q, k) * scale
        causal = jnp.tril(jnp.ones((T, T), bool))
        att = jnp.where(causal[None, None], att, -jnp.inf)
        y = jnp.einsum('bhqk,bhkd->bhqd', jax.nn.softmax(att, axis=-1), v)
        qc = _heads(x @ Wcq + bcq)
        kc = _heads(cross_input @ Wck + bck)
        vc = _heads(cross_input @ Wcv + bcv)
        attc = jnp.einsum('bhqd,bhkd->bhqk', qc, kc) * scale
        y = y + jnp.einsum('bhqk,bhkd->bhqd', jax.nn.softmax(attc, axis=-1), vc)
        y = y.transpose(0, 2, 1, 3).reshape(x.shape[0], T, C)
        return y @ Wp + bp

    def _L0_ffn_ref(x, Wr, br, ln_g, ln_b, W1, b1, W2, b2):
        import jax, jax.numpy as jnp
        import numpy as np
        B, S, D, F, E = (4, 256, 128, 512, 8)
        LN_EPS = 1e-05
        tokens_shape = x.shape[:-1]
        xt = x.reshape(-1, x.shape[-1])
        router_logits = xt @ Wr + br
        router_probs = jax.nn.softmax(router_logits, axis=-1)
        gates = jnp.max(router_probs, axis=-1, keepdims=True)
        idx = jnp.argmax(router_probs, axis=-1)
        onehot = jax.nn.one_hot(idx, E, dtype=xt.dtype)
        mu = jnp.mean(xt, axis=-1, keepdims=True)
        var = jnp.mean(jnp.square(xt - mu), axis=-1, keepdims=True)
        xn = (xt - mu) * jax.lax.rsqrt(var + LN_EPS) * ln_g + ln_b
        h = jnp.einsum('te,td,edf->tf', onehot, xn, W1) + b1[idx]
        h = jax.nn.relu(h)
        y = jnp.einsum('te,tf,efd->td', onehot, h, W2) + b2[idx]
        y = y * gates
        return y.reshape(tokens_shape + (y.shape[-1],))
    x = x + jnp.tanh(g_xattn[0]) * _L0_xattn_ref(_layernorm(x, axis=-1), ctx_512, L0_xattn_Wk, L0_xattn_bk, L0_xattn_Wq, L0_xattn_bq, L0_xattn_Wv, L0_xattn_bv, L0_xattn_Wck, L0_xattn_bck, L0_xattn_Wcq, L0_xattn_bcq, L0_xattn_Wcv, L0_xattn_bcv, L0_xattn_Wp, L0_xattn_bp)
    x = x + jnp.tanh(g_ffn[0]) * _L0_ffn_ref(_layernorm(x, axis=-1), L0_ffn_Wr, L0_ffn_br, L0_ffn_ln_g, L0_ffn_ln_b, L0_ffn_W1, L0_ffn_b1, L0_ffn_W2, L0_ffn_b2)
    return x

_drawn_inputs = setup_inputs


def setup_inputs(seed=0):
    import zlib

    import numpy as np

    out = dict(_drawn_inputs(seed))
    spreads = {'L0_xattn_bk': (0.0, 0.8),
     'L0_xattn_bq': (0.0, 0.557),
     'L0_xattn_bv': (0.0, 0.1),
     'L0_xattn_bck': (0.0, 0.8),
     'L0_xattn_bcq': (0.0, 0.455),
     'L0_xattn_bcv': (0.0, 0.1),
     'L0_xattn_bp': (0.0, 0.1),
     'L0_ffn_br': (0.0, 0.431),
     'L0_ffn_ln_g': (1.0, 0.6),
     'L0_ffn_ln_b': (0.0, 0.8),
     'L0_ffn_b1': (0.0, 0.8),
     'L0_ffn_b2': (0.0, 0.538)}
    factors = {'L0_ffn_Wr': 3.111, 'L0_ffn_W1': 5.548, 'L0_ffn_W2': 4.436}
    for name, (base, spread) in spreads.items():
        noise = np.random.default_rng([zlib.crc32(name.encode()), seed]).standard_normal(out[name].shape)
        drawn = base * np.exp(spread * noise) if base else spread * noise
        out[name] = jnp.asarray(drawn.astype(out[name].dtype))
    for name, factor in factors.items():
        out[name] = (out[name] * factor).astype(out[name].dtype)
    return out
```

```python
from contextlib import ExitStack

import concourse.bass as bass
from concourse import mybir

ALU = mybir.AluOpType
ACT = mybir.ActivationFunctionType
AX_X = mybir.AxisListType.X
F32 = mybir.dt.float32
BF16 = mybir.dt.bfloat16
I32 = mybir.dt.int32
U32 = mybir.dt.uint32

P = 128
B = 8
T = 256
TC = 64
C = 128
H = 16
D = C // H
NP = H // 2
NT = B * T // P
E = 8
F = 512
FC = F // P
SCALE = float(D) ** -0.5
EPS = 1e-5
NEG = -1e30

SH = 24
NS = 2
ROWS = SH + NS
RUNS = {False: [(0, 0, ROWS), (ROWS, 0, 2 * D), (ROWS + 2 * D, 0, D)],
        True: [(0, 0, ROWS), (ROWS, D, 2 * D), (ROWS + 2 * D, 2 * D, D)]}
RING = 3
VW = 48
GB = 4
NG = -(-(NT + E - 1) // GB)
NBLK = NG * GB
NSLOT = NBLK * P


def build(nc, a, out):
    nchunk = 4
    CT = 4
    with ExitStack() as ctx:
        def sb(name, shape, dt=F32):
            return ctx.enter_context(nc.sbuf_tensor(name, shape, dt))

        def sem(name):
            return ctx.enter_context(nc.semaphore(name))

        def dram(name, shape, dt):
            return nc.dram_tensor(name, shape, dt, kind="Internal").ap()

        ps_all = ctx.enter_context(nc.psum_tensor("ps_all", [P, 8 * 512], F32))

        def pb(i, n=1):
            return ps_all[:, 512 * i:512 * (i + n)]

        q_scr = dram("q_scr", [B, 2, ROWS, NP, T], BF16)
        k_scr = dram("k_scr", [B, 2, ROWS, NP, T], BF16)
        qc_scr = dram("qc_scr", [B, 2, ROWS, NP, T], BF16)
        kc_scr = dram("kc_scr", [2, ROWS, NP, B * TC], BF16)
        m_scr = dram("m_scr", [2 * B, 32, NS, P], BF16)
        xs_scr = dram("xs_scr", [NSLOT, C], F32)
        ys_scr = dram("ys_scr", [NSLOT, C], F32)

        x_sb = sb("x_sb", [P, NT, C])
        xn = sb("xn", [P, NT, C])
        v_all = sb("v_all", [P, NT, C])
        vc_all = sb("vc_all", [P, B, C])
        K = sb("K", [P, RING, NP, 2, T], BF16)
        Q = sb("Q", [P, RING, NP, T], BF16)
        Qc = sb("Qc", [P, RING, NP, T], BF16)
        Kc = sb("Kc", [P, NP * B, 2, TC], BF16)
        probs = sb("probs", [P, NP, 1024])
        Vz = sb("Vz", [P, 2, 2, H // 2, VW])
        Vcz = sb("Vcz", [P, 2, NP // 2, 32])
        ident = sb("ident", [P, P])
        ident_bf = sb("ident_bf", [P, P], BF16)
        causal = sb("causal", [P, P], BF16)
        before = sb("before", [P, P], BF16)
        ones_bf = sb("ones_bf", [P, P], BF16)
        zeros_bf = sb("zeros_bf", [B, T], BF16)
        kones = sb("kones", [NS * NP, 2 * T], BF16)
        half_neg = sb("half_neg", [P, 2 * NT])
        w_q = sb("w_q", [P, 3, C])
        w_v = sb("w_v", [P, C])
        w_ck = sb("w_ck", [TC, C])
        w_cv = sb("w_cv", [TC, C])
        w_p = sb("w_p", [P, C])
        b_col = sb("b_col", [P, 4])
        bv_col = sb("bv_col", [P, 2])
        bvs = sb("bvs", [P, 1])
        bvs_w = sb("bvs_w", [P, P])
        bp_bc = sb("bp_bc", [P, C])
        att_bias = sb("att_bias", [P, C])
        gate_x = sb("gate_x", [P, 2])
        tanh_g = sb("tanh_g", [P, 2])
        ctx_sb = sb("ctx_sb", [P, 4, TC])
        ctxT = sb("ctxT", [TC, B * TC])
        ctxT2 = sb("ctxT2", [TC, B, 2, TC])
        st6 = sb("st6", [P, NT, 6])
        mv = sb("mv", [P, NT, 2])
        rstd = sb("rstd", [P, NT])
        xh = sb("xh", [P, CT, C])
        xT = sb("xT", [P, CT * P])
        flat = probs[:].rearrange("p n q -> p (n q)")
        full = flat[:, 0:1536].rearrange("p (j t) -> p j t", j=3)
        rest = flat[:, 1536:3072].rearrange("p (j t) -> p j t", j=3)
        piece = flat[:, 3072:5376].bitcast(BF16).rearrange("p (j i t) -> p j i t", j=3, i=3)
        cfull = flat[:, 5376:5888]
        cpiece = flat[:, 5888:6656].bitcast(BF16).rearrange("p (i t) -> p i t", i=3)

        top = sb("top", [P, NP // 2, 16])
        M = sb("M", [P, P])
        shift = sb("shift", [32, NS, P], BF16)
        o_sb = sb("o_sb", [P, 512])
        rec = sb("rec", [P, 32])
        yn = sb("yn", [P, 2, 2, 64])
        y_sb = sb("y_sb", [P, 2, C])
        yT = sb("yT", [P, T])
        xb = sb("xb", [P, 2, C])

        w1 = sb("w1", [P, E, F])
        w2 = sb("w2", [P, E, FC, C])
        w_r = sb("w_r", [P, E])
        br_bc = sb("br_bc", [P, E])
        ln_g = sb("ln_g", [P, 1])
        ln_b = sb("ln_b", [P, 1])
        kflat = K[:].rearrange("p r n h t -> p (r n h t)").bitcast(F32)
        b1_bc = kflat[:, 0:E * F].rearrange("p (e f) -> p e f", e=E)
        b2_bc = kflat[:, E * F:E * F + E * C].rearrange("p (e c) -> p e c", e=E)
        zrow = sb("zrow", [P, C])
        iota_i = sb("iota_i", [P, 32], I32)
        iota = sb("iota", [P, 32])
        st6z = sb("st6z", [P, CT, 6])
        mvz = sb("mvz", [P, CT, 2])
        rstdz = sb("rstdz", [P, CT])
        logit = sb("logit", [P, NT, E])
        top1 = sb("top1", [P, NT])
        work = sb("work", [P, NT, E])
        onehot = sb("onehot", [P, NT, E])
        cum = [sb("cum_a", [P, NT, E]), sb("cum_b", [P, NT, E])]
        gate = sb("gate", [P, NT])
        rows_bf = sb("rows_bf", [P, E], BF16)
        base = sb("base", [P, 2 * E])
        over = sb("over", [P, E, NT])
        nb = [sb("nb_a", [P, E]), sb("nb_b", [P, E])]
        start = sb("start", [P, E])
        slot_f = sb("slot_f", [P, NT])
        slot = sb("slot", [P, NT], I32)
        passed = sb("passed", [P, NBLK, E])
        own_f = sb("own_f", [P, NBLK])
        owner = sb("owner", [P, NBLK], I32)
        pflat = flat
        xg = [pflat[:, 512 * i:512 * i + 512].rearrange("p (g c) -> p g c", g=GB) for i in range(2)]
        xnT = [pflat[:, 1024 + 512 * i:1536 + 512 * i] for i in range(2)]
        hid = [pflat[:, 2048 + 512 * i:2560 + 512 * i] for i in range(2)]
        hidT = [pflat[:, 3072 + 512 * i:3584 + 512 * i] for i in range(2)]
        yg = [pflat[:, 4096 + 512 * i:4608 + 512 * i].rearrange("p (g c) -> p g c", g=GB) for i in range(2)]
        y_all = pflat[:, 5120:7168].rearrange("p (t c) -> p t c", t=NT)

        s_stand_sp = sem("sp_wait_stands_alone")
        s_stand_pool = sem("pool_wait_stands_alone")
        s_w = sem("weights_loaded")
        s_x = sem("x_loaded")
        s_cst = sem("constants_made")
        s_zero = sem("operands_zeroed")
        s_zk = sem("k_ring_zeroed")
        s_init = sem("scratch_rows_written")
        s_tanh = sem("tanh_done")
        s_wp = sem("wp_scaled")
        s_bvs = sem("value_bias_summed")
        s_bmm = sem("bias_product_done")
        s_abias = sem("attention_bias_done")
        s_ctxT = sem("context_transposed")
        s_ctxs = sem("context_copied")
        s_kcps = sem("context_keys_projected")
        s_kcf = sem("context_keys_full")
        s_kcp = sem("context_pieces_step")
        s_kcw = sem("context_pieces_written")
        s_kcl = sem("context_keys_loaded")
        s_vcps = sem("context_values_projected")
        s_vc = sem("context_values_copied")
        s_st = sem("stats_step")
        s_rstd = sem("rstd_done")
        s_xh = sem("xhat_done")
        s_xTp = sem("xhat_transposed")
        s_xT = sem("xT_copied")
        s_pr = sem("projections_done")
        s_full = sem("projections_copied")
        s_pc = sem("pieces_step")
        s_v = sem("values_copied")
        s_pw = sem("pieces_written")

        s_ld = sem("operands_loaded")
        s_s = sem("scores_ready")
        s_red = sem("scores_reduced")
        s_m = sem("maxima_step")
        s_mt = sem("maxima_transposed")
        s_n1 = sem("shift1_done")
        s_n2 = sem("shift2_done")
        s_mw = sem("shift_written")
        s_mr = sem("shift_rows_loaded")
        s_stt = sem("scoresT_ready")
        s_exp = sem("exp_done")
        s_sel = sem("probs_masked")
        s_vz = sem("v_blocks_ready")
        s_vcz = sem("vc_blocks_ready")
        s_pv = sem("pv_done")
        s_osb = sem("o_copied")
        s_ot = sem("o_transposed")
        s_rec = sem("reciprocal_done")
        s_yn = sem("heads_normalised")
        s_y = sem("y_summed")
        s_yt = sem("y_transposed")
        s_yts = sem("yT_copied")
        s_xb = sem("x_plus_bias")
        s_att = sem("attention_projected")
        s_x1 = sem("x1_done")
        s_ew = sem("expert_weights_loaded")
        s_eb = sem("expert_biases_loaded")
        s_xsz = sem("slots_zeroed")
        s_io = sem("iota_made")
        s_zst = sem("ffn_stats_step")
        s_zr = sem("ffn_rstd_done")
        s_z = sem("z_done")
        s_zTp = sem("z_transposed")
        s_zT = sem("zT_copied")
        s_lgp = sem("logits_projected")
        s_lg = sem("logits_done")
        s_rt = sem("routing_step")
        s_ge = sem("gate_exp_done")
        s_rkp = sem("ranks_counted")
        s_slot = sem("slots_done")
        s_sc = sem("tokens_scattered")
        s_xg = [sem("group_loaded_a"), sem("group_loaded_b")]
        s_gT = sem("group_transposed")
        s_gTc = sem("group_copied")
        s_h = sem("hidden_projected")
        s_hc = sem("hidden_biased")
        s_hT = sem("hidden_transposed")
        s_hTc = sem("hidden_activated")
        s_yp = sem("expert_output_projected")
        s_yc = sem("expert_output_biased")
        s_yw = [sem("group_written_a"), sem("group_written_b")]
        s_ga = [sem(f"tokens_gathered_{c}") for c in range(4)]
        s_fin = sem("output_done")
        s_out = sem("out_written")

        block = ctx.enter_context(nc.Block())
        weights = [
            (w_q[:, 0, :], a["wq"]), (w_q[:, 1, :], a["wk"]), (w_q[:, 2, :], a["wcq"]),
            (w_v[:], a["wv"]), (w_ck[:], a["wck"]), (w_cv[:], a["wcv"]), (w_p[:], a["wp"]),
            (b_col[:, 0:1], a["bq"]), (b_col[:, 1:2], a["bk"]), (b_col[:, 2:3], a["bcq"]), (b_col[:, 3:4], a["bck"]),
            (bv_col[:, 0:1], a["bv"]), (bv_col[:, 1:2], a["bcv"]),
            (bp_bc[:], a["bp"].partition_broadcast(P)),
            (gate_x[:, 0:1], a["gx"].partition_broadcast(P)), (gate_x[:, 1:2], a["gf"].partition_broadcast(P)),
            (ctx_sb[:], a["ctx"].rearrange("(t p) c -> p t c", p=P)),
        ]
        NLD = 18

        def rows_of(hh, run):
            return slice(64 * hh + run[0], 64 * hh + run[0] + run[2])

        @block.sync
        def _(sp):
            sp.dma_start(x_sb[:], a["x"].rearrange("(t p) c -> p t c", p=P)).then_inc(s_x, 16)
            for dst, src in weights:
                sp.dma_start(dst, src).then_inc(s_w, 16)
            sp.wait_ge(s_cst, 8)
            for dst, src in ((w1[:], a["w1"].rearrange("e p f -> p e f")),
                             (w2[:], a["w2"].rearrange("e (k p) c -> p e k c", p=P)), (w_r[:], a["wr"]),
                             (br_bc[:], a["br"].partition_broadcast(P)), (ln_g[:], a["lng"]), (ln_b[:], a["lnb"])):
                sp.dma_start(dst, src).then_inc(s_ew, 16)
            sp.wait_ge(s_io, 3)
            sp.dma_start(xs_scr.rearrange("(n p) c -> p n c", p=P),
                         zrow[:].unsqueeze(1).to_broadcast([P, NBLK, C])).then_inc(s_xsz, 16)
            for hh in range(2):
                for scr in (q_scr, qc_scr):
                    sp.dma_start(scr[:, hh, SH:ROWS].rearrange("b r n t -> b (r n) t"),
                                 zeros_bf[:].unsqueeze(1).to_broadcast([B, NS * NP, T])).then_inc(s_init, 16)
                sp.dma_start(k_scr[:, hh, SH:ROWS].rearrange("b r n t -> b (r n) t"),
                             kones[0:B, 0:T].unsqueeze(1).to_broadcast([B, NS * NP, T])).then_inc(s_init, 16)
                sp.dma_start(kc_scr[hh, SH:ROWS].rearrange("r n t -> (r n) t"),
                             kones[0:NS * NP, 0:B * TC]).then_inc(s_init, 16)
            sp.wait_ge(s_kcp, 4)
            for hh in range(2):
                for i in range(3):
                    sp.dma_start(kc_scr[hh, i * D:(i + 1) * D].rearrange("d n t -> (d n) t"),
                                 cpiece[64 * hh:64 * hh + 64, i, :]).then_inc(s_kcw, 16)
            sp.wait_ge(s_kcw, 16 * 6)
            sp.wait_ge(s_init, 16 * 8)
            sp.wait_ge(s_zero, 9)
            for hh in range(2):
                for run in RUNS[True]:
                    sp.dma_start(Kc[rows_of(hh, run), :, hh, :],
                                 kc_scr[hh, run[1]:run[1] + run[2]].rearrange("r n (b t) -> r (n b) t", t=TC)).then_inc(s_kcl, 16)
            for c in range(nchunk):
                sp.wait_ge(s_pc, 4 * (c + 1) * 3)
                for j, scr in enumerate((q_scr, k_scr, qc_scr)):
                    for hh in range(2):
                        for bb in range(2):
                            for i in range(3):
                                sp.dma_start(
                                    scr[2 * c + bb, hh, i * D:(i + 1) * D].rearrange("d n t -> (d n) t"),
                                    piece[64 * hh:64 * hh + 64, j, i, bb * T:(bb + 1) * T]).then_inc(s_pw, 16)
                sp.wait_ge(s_pw, 16 * 36 * (c + 1))

            def load(b):
                for scr, dst, isk in ((q_scr, Q, False), (k_scr, K, True), (qc_scr, Qc, False)):
                    for hh in range(2):
                        for run in RUNS[isk]:
                            d = dst[rows_of(hh, run), bass.ds(b % RING, 1)]
                            s = scr[bass.ds(b, 1), hh, run[1]:run[1] + run[2]]
                            if isk:
                                d = d[:, :, :, hh, :]
                            sp.dma_start(d.rearrange("r o n t -> r (o n) t"),
                                         s.rearrange("o r n t -> r (o n) t")).then_inc(s_ld, 16)
                sp.wait_ge(s_ld, 16 * NLD * (b + 1))
                sp.sem_inc(s_stand_sp, 1)

            def shifts(hf, b, half):
                sp.wait_ge(s_n2, hf + 1)
                sp.sem_inc(s_stand_sp, 1)
                sp.dma_start(m_scr[bass.ds(hf, 1)].rearrange("o r i q -> r (o i) q"), shift[:]).then_inc(s_mw, 16)
                sp.wait_ge(s_mw, 16 * (hf + 1))
                sp.sem_inc(s_stand_sp, 1)
                for ty, dst in enumerate((Q, Qc)):
                    for hh in range(2):
                        row = 16 * ty + 8 * hh
                        sp.dma_start(
                            dst[64 * hh + SH:64 * hh + ROWS, bass.ds(b % RING, 1), 4 * half:4 * half + 4, :]
                            .rearrange("i o n (u q) -> i (o n u) q", u=2),
                            m_scr[bass.ds(hf, 1), row:row + 8].rearrange("o r i q -> i (o r) q")).then_inc(s_mr, 16)
                sp.wait_ge(s_mr, 64 * (hf + 1))
                sp.sem_inc(s_stand_sp, 1)

            sp.wait_ge(s_zk, 1)
            for b in range(2):
                load(b)
            shifts(0, 0, 0)
            shifts(1, 0, 1)

            def body(b, ld, m0, m1):
                if ld:
                    sp.wait_ge(s_stt, 8 * b)
                    sp.sem_inc(s_stand_sp, 1)
                    load(b + 2)
                if m0:
                    shifts(2 * b + 2, b + 1, 0)
                if m1:
                    shifts(2 * b + 3, b + 1, 1)

            body(0, True, True, True)
            with sp.Fori(1, 6) as b:
                body(b, True, True, True)
            body(6, False, True, True)
            sp.wait_ge(s_stt, 8 * B)
            sp.dma_start(b1_bc, a["b1"].rearrange("e f -> (e f)").partition_broadcast(P)
                         .rearrange("p (e f) -> p e f", e=E)).then_inc(s_eb, 16)
            sp.dma_start(b2_bc, a["b2"].rearrange("e c -> (e c)").partition_broadcast(P)
                         .rearrange("p (e c) -> p e c", e=E)).then_inc(s_eb, 16)

            def load_group(g, u):
                if not isinstance(g, int) or g >= 2:
                    sp.wait_ge(s_gT, g - 1)
                    sp.sem_inc(s_stand_sp, 1)
                sp.dma_start(xg[u], xs_scr[bass.ds(g * GB * P, GB * P)]
                             .rearrange("(g p) c -> p g c", p=P)).then_inc(s_xg[u], 16)

            def write_group(g, u):
                sp.wait_ge(s_yc, GB * (g + 1))
                sp.sem_inc(s_stand_sp, 1)
                sp.dma_start(ys_scr[bass.ds(g * GB * P, GB * P)].rearrange("(g p) c -> p g c", p=P),
                             yg[u]).then_inc(s_yw[u], 16)

            sp.wait_ge(s_sc, 16 * NT)
            sp.wait_ge(s_y, 2 * B)
            load_group(0, 0)
            load_group(1, 1)
            load_group(2, 0)
            write_group(0, 0)
            load_group(3, 1)
            write_group(1, 1)
            with sp.Fori(1, NG // 2 - 1) as i:
                load_group(2 * i + 2, 0)
                write_group(2 * i, 0)
                load_group(2 * i + 3, 1)
                write_group(2 * i + 1, 1)
            write_group(NG - 2, 0)
            write_group(NG - 1, 1)
            for c in range(nchunk):
                sp.wait_ge(s_fin, CT * (c + 1))
                sp.dma_start(out[c * CT * P:(c + 1) * CT * P].rearrange("(t p) c -> p t c", p=P),
                             y_all[:, CT * c:CT * c + CT, :]).then_inc(s_out, 16)
            sp.wait_ge(s_out, 16 * nchunk)

        @block.gpsimd
        def _(pool):
            pool.memset(ident[:], 0.0).then_inc(s_cst, 1)
            pool.memset(causal[:], 0.0).then_inc(s_cst, 1)
            pool.memset(before[:], 1.0).then_inc(s_cst, 1)
            pool.memset(zeros_bf[:], 0.0).then_inc(s_cst, 1)
            pool.memset(kones[:], 1.0).then_inc(s_cst, 1)
            pool.wait_ge(s_cst, 5)
            pool.affine_select(out=ident[:], in_=ident[:], compare_op=ALU.not_equal, fill=1.0, base=0,
                               pattern=[[-1, P]], channel_multiplier=1).then_inc(s_cst, 1)
            pool.affine_select(out=causal[:], in_=causal[:], compare_op=ALU.is_ge, fill=NEG, base=0,
                               pattern=[[-1, P]], channel_multiplier=1).then_inc(s_cst, 1)
            pool.affine_select(out=before[:], in_=before[:], compare_op=ALU.is_gt, fill=0.0, base=0,
                               pattern=[[1, P]], channel_multiplier=-1).then_inc(s_cst, 1)
            pool.memset(half_neg[:], -0.5).then_inc(s_cst, 1)
            pool.memset(ones_bf[:], 1.0).then_inc(s_cst, 1)
            pool.wait_ge(s_cst, 10)
            pool.tensor_copy(ident_bf[:], ident[:]).then_inc(s_cst, 1)
            pool.iota(iota_i[:], pattern=[[1, 32]], base=0, channel_multiplier=0).then_inc(s_io, 1)
            pool.memset(zrow[:], 0.0).then_inc(s_io, 1)
            pool.wait_ge(s_io, 2)
            pool.tensor_copy(iota[:], iota_i[:]).then_inc(s_io, 1)
            for c in range(nchunk):
                pool.wait_ge(s_st, 3 * (c + 1))
                sl = slice(CT * c, CT * c + CT)
                pool.tensor_tensor(rstd[:, sl], rstd[:, sl], half_neg[:, 0:CT], ALU.pow).then_inc(s_rstd, 1)
                if c == 0:
                    pool.memset(Kc[:].rearrange("p n h t -> p (n h t)").bitcast(F32), 0.0).then_inc(s_zero, 1)
                    pool.memset(Q[:].rearrange("p r n t -> p (r n t)").bitcast(F32), 0.0).then_inc(s_zero, 1)
                    pool.memset(Qc[:].rearrange("p r n t -> p (r n t)").bitcast(F32), 0.0).then_inc(s_zero, 1)
                    pool.memset(M[:], 0.0).then_inc(s_zero, 1)
                    pool.memset(Vz[:], 0.0).then_inc(s_zero, 1)
                    pool.memset(Vcz[:], 0.0).then_inc(s_zero, 1)
                    pool.wait_ge(s_zero, 6)
                    pool.memset(Vz[:, :, :, :, 24:25], 1.0).then_inc(s_zero, 1)
                    pool.memset(Vcz[0:64, :, :, 8:9], 1.0).then_inc(s_zero, 1)
                    pool.wait_ge(s_zero, 8)
                    pool.memset(Vcz[64:128, :, :, 24:25], 1.0).then_inc(s_zero, 1)
                    pool.wait_ge(s_zero, 9)

            def v_blocks(hf, b, half):
                if not isinstance(hf, int) or hf >= 2:
                    pool.wait_ge(s_pv, hf - 1)
                pool.tensor_copy(Vz[:, half, :, :, 16:24],
                                 v_all[:, bass.ds(2 * b, 2), 64 * half:64 * half + 64]
                                 .rearrange("p k (h d) -> p k h d", d=D)).then_inc(s_vz, 1)

            def select(b, k):
                pool.wait_ge(s_exp, 8 * b + k + 1)
                pool.sem_inc(s_stand_pool, 1)
                v = probs[:, k, :].rearrange("p (g q) -> p g q", q=256)[:, :, 0:128]
                pool.affine_select(out=v, in_=v, compare_op=ALU.is_ge, fill=0.0, base=0,
                                   pattern=[[0, 4], [1, P]], channel_multiplier=-1).then_inc(s_sel, 1)

            def y_sum(hf, half):
                pool.wait_ge(s_yn, hf + 1)
                if half == 0 and (not isinstance(hf, int) or hf >= 2):
                    pool.wait_ge(s_yt, bass_half(hf))
                pool.tensor_tensor(y_sb[:, :, 64 * half:64 * half + 64], yn[:, 0], yn[:, 1], ALU.add).then_inc(s_y, 1)

            def bass_half(hf):
                return hf // 2

            def body(b, prev, cur):
                for k in range(NP):
                    if cur:
                        if k == 0:
                            v_blocks(2 * b, b, 0)
                        if k == 4:
                            v_blocks(2 * b + 1, b, 1)
                        select(b, k)
                    if prev:
                        if k == 0:
                            y_sum(2 * b - 2, 0)
                        if k == 3:
                            y_sum(2 * b - 1, 1)
                        if k == 4:
                            if not isinstance(b, int) or b >= 2:
                                pool.wait_ge(s_x1, b - 1)
                            pool.tensor_tensor(
                                xb[:], x_sb[:, bass.ds(2 * b - 2, 2), :],
                                att_bias[:].unsqueeze(1).to_broadcast([P, 2, C]), ALU.add).then_inc(s_xb, 1)

            pool.wait_ge(s_zero, 9)
            pool.wait_ge(s_v, nchunk)
            pool.wait_ge(s_vc, 2)
            body(0, False, True)
            pool.wait_ge(s_abias, 1)
            body(1, True, True)
            with pool.Fori(2, B) as b:
                body(b, True, True)
            body(B, True, False)

            for n in range(2 * nchunk):
                pool.wait_ge(s_zst, 3 * (n + 1))
                pool.tensor_tensor(rstdz[:], rstdz[:], half_neg[:, 0:CT], ALU.pow).then_inc(s_zr, 1)
            pool.wait_ge(s_slot, 1)
            pool.wait_ge(s_xsz, 16)
            pool.wait_ge(s_z, 2 * nchunk)
            for t in range(NT):
                pool.indirect_dma_start(out=xs_scr, out_offset=bass.IndirectOffsetOnAxis(
                    ap=slot[:, t:t + 1].bitcast(U32), axis=0), in_=xn[:, t, :], in_offset=None).then_inc(s_sc, 16)
            pool.wait_ge(s_yw[0], 16 * NG // 2)
            pool.wait_ge(s_yw[1], 16 * NG // 2)
            for t in range(NT):
                pool.indirect_dma_start(out=y_all[:, t, :], out_offset=None, in_=ys_scr,
                                        in_offset=bass.IndirectOffsetOnAxis(
                                            ap=slot[:, t:t + 1].bitcast(U32), axis=0)).then_inc(s_ga[t // CT], 16)

        @block.scalar
        def _(act):
            act.wait_ge(s_w, 16 * len(weights))
            act.activation(tanh_g[:], gate_x[:], ACT.Tanh).then_inc(s_tanh, 1)
            act.wait_ge(s_ctxT, 1)
            act.copy(ctxT[:], pb(5)[0:TC, :]).then_inc(s_ctxs, 1)
            act.copy(ctxT2[:, :, 0, :], pb(5)[0:TC, :].rearrange("p (b t) -> p b t", b=B)).then_inc(s_ctxs, 1)
            act.copy(ctxT2[:, :, 1, :], pb(5)[0:TC, :].rearrange("p (b t) -> p b t", b=B)).then_inc(s_ctxs, 1)
            act.wait_ge(s_kcps, 1)
            act.activation(cfull, pb(6), ACT.Identity, bias=b_col[:, 3:4]).then_inc(s_kcf, 1)
            act.wait_ge(s_wp, 2)
            for c in range(nchunk):
                act.wait_ge(s_xTp, c + 1)
                if c:
                    act.wait_ge(s_pr, 4 * c)
                act.copy(xT[:], pb(0)).then_inc(s_xT, 1)
                for j in range(3):
                    act.wait_ge(s_pr, 4 * c + j + 1)
                    if c:
                        act.wait_ge(s_pc, 12 * c)
                    act.activation(full[:, j, :], pb(1 + j), ACT.Identity, bias=b_col[:, j:j + 1],
                                   scale=1.0 if j == 1 else SCALE).then_inc(s_full, 1)

            def exp(b, k):
                act.wait_ge(s_stt, 8 * b + k + 1)
                if not isinstance(b, int) or b >= 1:
                    act.wait_ge(s_pv, 2 * b - 1 + k // 4)
                act.activation(probs[:, k, :], pb(2 + 2 * (k % 2), 2), ACT.Exp).then_inc(s_exp, 1)

            def vc_blocks(hf, b, half):
                if not isinstance(hf, int) or hf >= 2:
                    act.wait_ge(s_pv, hf - 1)
                for hh in range(2):
                    pr = slice(64 * hh, 64 * hh + 64)
                    act.copy(
                        Vcz[pr, half, :, 16 * hh:16 * hh + 8],
                        vc_all[pr, bass.ds(b, 1), 64 * half:64 * half + 64]
                        .rearrange("p o (n s d) -> p (o n) s d", s=2, d=D)[:, :, hh, :]).then_inc(s_vcz, 1)

            def shift1(hf):
                act.wait_ge(s_mt, hf + 1)
                if not isinstance(hf, int) or hf >= 1:
                    act.wait_ge(s_mw, 16 * hf)
                act.activation(shift[:, 0, :], pb(7)[0:32, 0:P], ACT.Copy, scale=-1.0).then_inc(s_n1, 1)

            def o_copy(hf):
                act.wait_ge(s_pv, hf + 1)
                if not isinstance(hf, int) or hf >= 1:
                    act.wait_ge(s_ot, hf)
                act.copy(o_sb[:], pb(6)).then_inc(s_osb, 1)

            def yT_copy(b):
                act.wait_ge(s_yt, b + 1)
                act.copy(yT[:], pb(7)[:, 0:T]).then_inc(s_yts, 1)

            def body(b, prev, cur, m):
                for k in range(NP):
                    if cur:
                        if k == 2:
                            vc_blocks(2 * b, b, 0)
                        if k == 6:
                            vc_blocks(2 * b + 1, b, 1)
                        exp(b, k)
                    if prev and k == 1:
                        o_copy(2 * b - 1)
                    if m and k == 1:
                        shift1(2 * b + 2)
                    if cur and k == 5:
                        o_copy(2 * b)
                    if m and k == 5:
                        shift1(2 * b + 3)
                    if prev and k == 6:
                        yT_copy(b - 1)

            act.wait_ge(s_zero, 9)
            act.wait_ge(s_vc, 2)
            shift1(0)
            shift1(1)
            body(0, False, True, True)
            with act.Fori(1, 7) as b:
                body(b, True, True, True)
            body(7, True, True, False)
            body(8, True, False, False)

            for c in range(nchunk):
                act.wait_ge(s_zTp, c + 1)
                if c:
                    act.wait_ge(s_lgp, c)
                act.copy(xT[:], pb(0)).then_inc(s_zT, 1)
            act.wait_ge(s_rt, 2)
            act.activation(work[:], work[:], ACT.Exp).then_inc(s_ge, 1)

            def group_T(g, u):
                act.wait_ge(s_gT, g + 1)
                if not isinstance(g, int) or g >= 2:
                    act.wait_ge(s_h, GB * (g - 1))
                act.activation(xnT[u], pb(6), ACT.Identity, bias=ln_b[:], scale=ln_g[:]).then_inc(s_gTc, 1)

            def hidden_T(j, v):
                act.wait_ge(s_hT, j + 1)
                if not isinstance(j, int) or j >= 2:
                    act.wait_ge(s_yp, j - 1)
                act.activation(hidT[v], pb(2 + v), ACT.Relu).then_inc(s_hTc, 1)

            act.wait_ge(s_ew, 16 * 6)
            group_T(0, 0)

            def blocks(i, last):
                for u in range(2):
                    for n in range(GB):
                        if n == 2 and not (last and u == 1):
                            group_T(2 * i + u + 1, 1 - u)
                        hidden_T(GB * (2 * i + u) + n, n % 2)

            blocks(0, False)
            with act.Fori(1, NG // 2 - 1) as i:
                blocks(i, False)
            blocks(NG // 2 - 1, True)

        @block.vector
        def _(dve):
            dve.memset(K[:].rearrange("p r n h t -> p (r n h t)").bitcast(F32), 0.0).then_inc(s_zk, 1)
            dve.wait_ge(s_x, 16)
            for c in range(nchunk):
                sl = slice(CT * c, CT * c + CT)
                for t in range(CT * c, CT * c + CT):
                    ins = dve.bn_stats(st6[:, t, :], x_sb[:, t, :])
                ins.then_inc(s_st, 1)
                dve.wait_ge(s_st, 3 * c + 1)
                for t in range(CT * c, CT * c + CT):
                    ins = dve.bn_aggr(mv[:, t, :], st6[:, t, :])
                ins.then_inc(s_st, 1)
                dve.wait_ge(s_st, 3 * c + 2)
                dve.tensor_scalar(rstd[:, sl], mv[:, sl, 1], EPS, None, ALU.add).then_inc(s_st, 1)
                if c == 0:
                    dve.wait_ge(s_w, 16 * len(weights))
                    dve.wait_ge(s_tanh, 1)
                    dve.tensor_tensor(bvs[:], bv_col[:, 0:1], bv_col[:, 1:2], ALU.add).then_inc(s_bvs, 1)
                    dve.tensor_scalar(b_col[:, 0:1], b_col[:, 0:1], SCALE, None, ALU.mult).then_inc(s_wp, 1)
                    dve.tensor_scalar(b_col[:, 2:3], b_col[:, 2:3], SCALE, None, ALU.mult).then_inc(s_wp, 1)
                    dve.tensor_scalar(w_p[:], w_p[:], tanh_g[:, 0:1], None, ALU.mult).then_inc(s_wp, 1)
                    dve.tensor_scalar(bp_bc[:], bp_bc[:], tanh_g[:, 0:1], None, ALU.mult).then_inc(s_wp, 1)
                    dve.wait_ge(s_bvs, 1)
                    dve.tensor_copy(bvs_w[:], bvs[:, 0:1].to_broadcast([P, P])).then_inc(s_bvs, 1)
                dve.wait_ge(s_rstd, c + 1)
                if c:
                    dve.wait_ge(s_xTp, c)
                for i in range(CT):
                    t = CT * c + i
                    ins = dve.tensor_scalar(xh[:, i, :], x_sb[:, t, :], mv[:, t, 0:1], rstd[:, t:t + 1],
                                            ALU.subtract, ALU.mult)
                ins.then_inc(s_xh, 1)
                if c == 0:
                    dve.wait_ge(s_bmm, 1)
                    dve.tensor_tensor(att_bias[:], pb(7)[:, 0:C], bp_bc[:], ALU.add).then_inc(s_abias, 1)
                    dve.wait_ge(s_kcf, 1)
                    dve.tensor_copy(cpiece[:, 2, :], cfull).then_inc(s_kcp, 1)
                    dve.wait_ge(s_kcp, 1)
                    dve.tensor_tensor(cfull, cfull, cpiece[:, 2, :], ALU.subtract).then_inc(s_kcp, 1)
                    dve.wait_ge(s_kcp, 2)
                    dve.tensor_copy(cpiece[:, 1, :], cfull).then_inc(s_kcp, 1)
                    dve.wait_ge(s_kcp, 3)
                    dve.tensor_tensor(cpiece[:, 0, :], cfull, cpiece[:, 1, :], ALU.subtract).then_inc(s_kcp, 1)
                    for i in range(2):
                        dve.wait_ge(s_vcps, i + 1)
                        dve.tensor_copy(vc_all[:, 4 * i:4 * i + 4, :], pb(4 if i == 0 else 5)
                                        .rearrange("p (b c) -> p b c", b=4)).then_inc(s_vc, 1)
                dve.wait_ge(s_pr, 4 * c + 4)
                dve.tensor_copy(v_all[:, CT * c:CT * c + CT, :],
                                pb(4).rearrange("p (t c) -> p t c", t=CT)).then_inc(s_v, 1)
                if c:
                    dve.wait_ge(s_pw, 16 * 36 * c)
                for j in range(3):
                    first, last = (2, 0) if j == 1 else (0, 2)
                    at = 4 * (3 * c + j)
                    dve.wait_ge(s_full, 3 * c + j + 1)
                    dve.tensor_copy(piece[:, j, first, :], full[:, j, :]).then_inc(s_pc, 1)
                    dve.wait_ge(s_pc, at + 1)
                    dve.tensor_tensor(rest[:, j, :], full[:, j, :], piece[:, j, first, :], ALU.subtract).then_inc(s_pc, 1)
                    dve.wait_ge(s_pc, at + 2)
                    dve.tensor_copy(piece[:, j, 1, :], rest[:, j, :]).then_inc(s_pc, 1)
                    dve.wait_ge(s_pc, at + 3)
                    dve.tensor_tensor(piece[:, j, last, :], rest[:, j, :], piece[:, j, 1, :], ALU.subtract).then_inc(s_pc, 1)

            def reduce(hf, j):
                dve.wait_ge(s_s, 4 * hf + j + 1)
                dve.tensor_reduce(top[:, j, :], pb(0, 2).rearrange("p (g k) -> p g k", k=64), AX_X,
                                  ALU.max).then_inc(s_red, 1)

            def maxima(hf):
                Mv = M[:, 0:32].rearrange("p (y h n u) -> p y h n u", y=2, h=2, n=4)
                dve.wait_ge(s_red, 4 * hf + 4)
                if not isinstance(hf, int) or hf >= 1:
                    dve.wait_ge(s_mt, hf)
                dve.tensor_reduce(Mv[:, 0, :, :, 1].rearrange("p h n -> p n h"),
                                  top[:, :, 0:8].rearrange("p n (h g) -> p n h g", h=2), AX_X, ALU.max).then_inc(s_m, 1)
                dve.tensor_reduce(Mv[:, 0, :, :, 0].rearrange("p h n -> p n h"),
                                  top[:, :, 8:12].rearrange("p n (h g) -> p n h g", h=2), AX_X, ALU.max).then_inc(s_m, 1)
                for u in range(2):
                    dve.tensor_copy(Mv[:, 1, :, :, u].rearrange("p h n -> p n h"),
                                    top[:, :, 12 + 2 * u:14 + 2 * u]).then_inc(s_m, 1)
                dve.wait_ge(s_m, 4 * hf + 4)

            def shift2(hf):
                dve.wait_ge(s_n1, hf + 1)
                dve.scalar_tensor_tensor(out=shift[:, 1, :], in0=pb(7)[0:32, 0:P], scalar=-1.0,
                                         in1=shift[:, 0, :], op0=ALU.mult, op1=ALU.subtract).then_inc(s_n2, 1)

            def normalise(hf):
                O = pb(7).rearrange("p (g r) -> p g r", r=16)
                dve.wait_ge(s_ot, hf + 1)
                dve.reciprocal(rec[:], O[:, :, 8]).then_inc(s_rec, 1)
                dve.wait_ge(s_rec, hf + 1)
                if not isinstance(hf, int) or hf >= 1:
                    dve.wait_ge(s_y, hf)
                dve.tensor_tensor(yn[:].rearrange("p y u (g d) -> p (y u g) d", d=D), O[:, :, 0:8],
                                  rec[:].unsqueeze(2).to_broadcast([P, 32, D]), ALU.mult).then_inc(s_yn, 1)

            def x1(b):
                dve.wait_ge(s_att, b + 1)
                dve.wait_ge(s_xb, b + 1)
                dve.tensor_tensor(x_sb[:, bass.ds(2 * b, 2), :], pb(7)[:, 0:2 * C]
                                  .rearrange("p (u c) -> p u c", u=2), xb[:], ALU.add).then_inc(s_x1, 1)

            def body(b, prev, p1a, p1b):
                for k in range(NP):
                    if (p1a and k < 4) or (p1b and k >= 4):
                        reduce(2 * b + 3 + k // 4, k % 4)
                        if k % 4 == 3:
                            maxima(2 * b + 3 + k // 4)
                    if prev and k == 0:
                        normalise(2 * b - 2)
                    if p1a and k == 1:
                        shift2(2 * b + 2)
                    if prev and k == 3:
                        normalise(2 * b - 1)
                    if p1a and k == 5:
                        shift2(2 * b + 3)
                    if prev and k == 7:
                        x1(b - 1)

            for hf in range(3):
                for j in range(4):
                    reduce(hf, j)
                maxima(hf)
                if hf:
                    shift2(hf - 1)
            body(0, False, True, True)
            body(1, True, True, True)
            with dve.Fori(2, 6) as b:
                body(b, True, True, True)
            body(6, True, True, False)
            body(7, True, False, False)
            body(8, True, False, False)

            dve.wait_ge(s_ew, 16 * 6)
            for c in range(nchunk):
                src = [x_sb[:, CT * c + i, :] for i in range(CT)]
                dst = [xh[:, i, :] for i in range(CT)]
                for n in range(2):
                    at = 3 * (2 * c + n)
                    if n == 0 and c:
                        dve.wait_ge(s_zTp, c)
                    if n:
                        dve.wait_ge(s_z, 2 * c + 1)
                    for i in range(CT):
                        ins = dve.bn_stats(st6z[:, i, :], src[i])
                    ins.then_inc(s_zst, 1)
                    dve.wait_ge(s_zst, at + 1)
                    for i in range(CT):
                        ins = dve.bn_aggr(mvz[:, i, :], st6z[:, i, :])
                    ins.then_inc(s_zst, 1)
                    dve.wait_ge(s_zst, at + 2)
                    dve.tensor_scalar(rstdz[:], mvz[:, :, 1], EPS, None, ALU.add).then_inc(s_zst, 1)
                    dve.wait_ge(s_zr, 2 * c + n + 1)
                    for i in range(CT):
                        ins = dve.tensor_scalar(dst[i], src[i], mvz[:, i, 0:1], rstdz[:, i:i + 1],
                                                ALU.subtract, ALU.mult)
                    ins.then_inc(s_z, 1)
                    src, dst = dst, [xn[:, CT * c + i, :] for i in range(CT)]
                dve.wait_ge(s_z, 2 * c + 2)
                dve.wait_ge(s_lgp, c + 1)
                dve.tensor_tensor(logit[:, CT * c:CT * c + CT, :],
                                  pb(1)[:, 0:CT * E].rearrange("p (t e) -> p t e", t=CT),
                                  br_bc[:].unsqueeze(1).to_broadcast([P, CT, E]), ALU.add).then_inc(s_lg, 1)
            step = [0]

            def did(ins):
                step[0] += 1
                ins.then_inc(s_rt, 1)
                dve.wait_ge(s_rt, step[0])

            all_e = [P, NT, E]
            over_e = lambda v: v.unsqueeze(2).to_broadcast(all_e)
            over_t = lambda v: v.unsqueeze(1).to_broadcast(all_e)
            dve.wait_ge(s_lg, nchunk)
            dve.wait_ge(s_io, 3)
            did(dve.tensor_reduce(top1[:], logit[:], AX_X, ALU.max))
            did(dve.tensor_tensor(work[:], logit[:], over_e(top1[:]), ALU.subtract))
            did(dve.tensor_tensor(onehot[:], logit[:], over_e(top1[:]), ALU.is_equal))
            did(dve.tensor_scalar(nb[0][:], iota[:, 0:E], -1.0, float(E), ALU.mult, ALU.add))
            did(dve.tensor_tensor(onehot[:], onehot[:], over_t(nb[0][:]), ALU.mult))
            did(dve.tensor_reduce(top1[:], onehot[:], AX_X, ALU.max))
            did(dve.tensor_tensor(onehot[:], over_t(nb[0][:]), over_e(top1[:]), ALU.is_equal))
            dve.wait_ge(s_ge, 1)
            did(dve.tensor_reduce(gate[:], work[:], AX_X, ALU.add))
            did(dve.reciprocal(gate[:], gate[:]))
            did(dve.tensor_scalar(gate[:], gate[:], tanh_g[:, 1:2], None, ALU.mult))
            src, dst = onehot, cum[0]
            for sh in (1, 2, 4, 8):
                did(dve.tensor_copy(dst[:, 0:sh, :], src[:, 0:sh, :]))
                did(dve.tensor_tensor(dst[:, sh:NT, :], src[:, sh:NT, :], src[:, 0:NT - sh, :], ALU.add))
                src, dst = dst, cum[1] if dst is cum[0] else cum[0]
            did(dve.tensor_copy(rows_bf[:], src[:, NT - 1, :]))
            dve.wait_ge(s_rkp, 1)
            did(dve.tensor_copy(base[:], pb(1)[:, 0:2 * E]))
            did(dve.tensor_scalar(own_f[:, 0:NT], iota[:, 0:NT], float(P), None, ALU.mult))
            did(dve.tensor_tensor(over[:], base[:, E:2 * E].unsqueeze(2).to_broadcast([P, E, NT]),
                                  own_f[:, 0:NT].unsqueeze(1).to_broadcast([P, E, NT]), ALU.is_gt))
            did(dve.tensor_reduce(nb[0][:], over[:], AX_X, ALU.add))
            did(dve.tensor_copy(start[:], nb[0][:]))
            a_, b_ = nb
            for sh in (1, 2, 4):
                did(dve.tensor_copy(b_[:, 0:sh], a_[:, 0:sh]))
                did(dve.tensor_tensor(b_[:, sh:E], a_[:, sh:E], a_[:, 0:E - sh], ALU.add))
                a_, b_ = b_, a_
            did(dve.tensor_tensor(start[:], a_[:], start[:], ALU.subtract))
            did(dve.tensor_scalar(start[:], start[:], float(P), -1.0, ALU.mult, ALU.add))
            did(dve.tensor_tensor(start[:], start[:], base[:, 0:E], ALU.add))
            did(dve.tensor_tensor(src[:], src[:], over_t(start[:]), ALU.add))
            did(dve.tensor_tensor(src[:], src[:], onehot[:], ALU.mult))
            did(dve.tensor_reduce(slot_f[:], src[:], AX_X, ALU.add))
            did(dve.tensor_tensor(passed[:], iota[:, 0:NBLK].unsqueeze(2).to_broadcast([P, NBLK, E]),
                                  a_[:].unsqueeze(1).to_broadcast([P, NBLK, E]), ALU.is_ge))
            did(dve.tensor_reduce(own_f[:], passed[:], AX_X, ALU.add))
            did(dve.tensor_scalar(own_f[:], own_f[:], float(E - 1), None, ALU.min))
            did(dve.tensor_copy(owner[:], own_f[:]))
            dve.tensor_copy(slot[:], slot_f[:]).then_inc(s_slot, 1)

            def bias1(j, v):
                e = dve.value_load(owner[0:1, bass.ds(j, 1)], min_val=0, max_val=E - 1)
                dve.wait_ge(s_h, j + 1)
                if not isinstance(j, int) or j >= 2:
                    dve.wait_ge(s_hT, j - 1)
                dve.tensor_tensor(hid[v], pb(v), b1_bc[:, bass.ds(e, 1), :].rearrange("p o f -> p (o f)"),
                                  ALU.add).then_inc(s_hc, 1)
                return e

            def bias2(j, g, u, n, v):
                e = dve.value_load(owner[0:1, bass.ds(j, 1)], min_val=0, max_val=E - 1)
                dve.wait_ge(s_yp, j + 1)
                if n == 0 and (not isinstance(g, int) or g >= 2):
                    dve.wait_ge(s_yw[u], 16 * (g // 2))
                dve.tensor_tensor(yg[u][:, n, :], pb(4 + v)[:, 0:C], b2_bc[:, bass.ds(e, 1), :]
                                  .rearrange("p o f -> p (o f)"), ALU.add).then_inc(s_yc, 1)

            dve.wait_ge(s_eb, 32)
            bias1(0, 0)
            bias1(1, 1)
            bias2(0, 0, 0, 0, 0)
            for j in range(2, 8):
                bias1(j, j % 2)
                bias2(j - 1, (j - 1) // 4, (j - 1) // 4, (j - 1) % 4, (j - 1) % 2)
            with dve.Fori(1, NG // 2) as i:
                for n in range(8):
                    bias1(8 * i + n, n % 2)
                    if n == 0:
                        bias2(8 * i - 1, 2 * i - 1, 1, 3, 1)
                    else:
                        bias2(8 * i + n - 1, 2 * i + (n - 1) // 4, (n - 1) // 4, (n - 1) % 4, (n - 1) % 2)
            bias2(NBLK - 1, NG - 1, 1, 3, 1)
            for t in range(NT):
                if t % CT == 0:
                    dve.wait_ge(s_ga[t // CT], 16 * CT)
                dve.scalar_tensor_tensor(out=y_all[:, t, :], in0=y_all[:, t, :], scalar=gate[:, t:t + 1],
                                         in1=x_sb[:, t, :], op0=ALU.mult, op1=ALU.add).then_inc(s_fin, 1)

        @block.tensor
        def _(pe):
            pe.wait_ge(s_cst, 11)
            pe.wait_ge(s_w, 16 * len(weights))
            for i in range(4):
                ins = pe.transpose(pb(5)[0:TC, P * i:P * i + P], ctx_sb[:, i, :], ident[:])
            ins.then_inc(s_ctxT, 1)
            pe.wait_ge(s_ctxs, 3)
            pe.matmul(pb(6), w_ck[:], ctxT[:], start=True, stop=True).then_inc(s_kcps, 1)
            for i in range(2):
                for j in range(4):
                    ins = pe.matmul(pb(4 + i)[:, C * j:C * j + C],
                                    ctxT2[:, 4 * i + j].rearrange("p u t -> p (u t)"), w_cv[:], start=True, stop=True)
                ins.then_inc(s_vcps, 1)
            pe.wait_ge(s_bvs, 2)
            pe.wait_ge(s_wp, 4)
            pe.matmul(pb(7)[:, 0:C], bvs_w[:], w_p[:], start=True, stop=True).then_inc(s_bmm, 1)
            for c in range(nchunk):
                pe.wait_ge(s_xh, c + 1)
                if c:
                    pe.wait_ge(s_xT, c)
                for i in range(CT):
                    ins = pe.transpose(pb(0)[:, P * i:P * i + P], xh[:, i, :], ident[:])
                ins.then_inc(s_xTp, 1)
                pe.wait_ge(s_xT, c + 1)
                for j in range(3):
                    if c:
                        pe.wait_ge(s_full, 3 * (c - 1) + j + 1)
                    pe.matmul(pb(1 + j), w_q[:, j, :], xT[:], start=True, stop=True).then_inc(s_pr, 1)
                if c == 0:
                    pe.wait_ge(s_vc, 1)
                else:
                    pe.wait_ge(s_v, c)
                for i in range(CT):
                    ins = pe.matmul(pb(4)[:, C * i:C * i + C], xT[:, P * i:P * i + P], w_v[:], start=True, stop=True)
                ins.then_inc(s_pr, 1)

            def pass1(hf, b, half, j):
                hp = 4 * half + j
                g = 4 * hf + j
                if not isinstance(hf, int) or g >= 1:
                    pe.wait_ge(s_red, g)
                slot = bass.ds(b % RING, 1)
                k2 = K[:, slot, hp].rearrange("p o h t -> p (o h) t")
                q2 = Q[:, slot, hp].rearrange("p o t -> p (o t)")
                qc2 = Qc[:, slot, hp].rearrange("p o t -> p (o t)")
                kc2 = Kc[:, bass.ds(hp * B + b, 1)].rearrange("p o h t -> p (o h t)")
                mask = causal[:].unsqueeze(1).to_broadcast([P, 2, P])
                b0, b1 = pb(0), pb(1)
                pe.matmul(b0, q2[:, P:T], k2, start=True, stop=True)
                pe.matmul(b0.rearrange("p (h t) -> p h t", h=2)[:, :, P:T], ident_bf[:], mask, start=False, stop=True,
                          skip_group_check=True)
                pe.matmul(b1[:, 0:256], q2[:, 0:P], k2[:, :, 0:P], start=True, stop=False)
                pe.matmul(b1[:, 0:256].rearrange("p (h t) -> p h t", h=2), ident_bf[:], mask, start=False, stop=True)
                pe.matmul(b1[:, 256:384], qc2[:, 0:P], kc2, start=True, stop=True)
                pe.matmul(b1[:, 384:512], qc2[:, P:T], kc2, start=True, stop=True).then_inc(s_s, 1)

            def pass2(b, k):
                g = 8 * b + k
                if not isinstance(b, int) or g >= 2:
                    pe.wait_ge(s_exp, g - 1)
                if k % 4 == 0:
                    pe.wait_ge(s_mr, 64 * (2 * b + k // 4 + 1))
                slot = bass.ds(b % RING, 1)
                k2 = K[:, slot, k].rearrange("p o h t -> p (o h) t")
                q2 = Q[:, slot, k].rearrange("p o t -> p (o t)")
                qc2 = Qc[:, slot, k].rearrange("p o t -> p (o t)")
                b0, b1 = pb(2 + 2 * (k % 2)), pb(3 + 2 * (k % 2))
                for hh in range(2):
                    pe.matmul(b0[:, T * hh:T * hh + T], k2[:, hh, 0:P], q2, start=True, stop=True)
                    pe.matmul(b1[:, T * hh:T * hh + P], k2[:, hh, P:T], q2[:, P:T], start=True, stop=True)
                pe.matmul(b1.rearrange("p (g q) -> p g q", q=256)[:, :, P:256], Kc[:, bass.ds(k * B + b, 1)].rearrange("p o h t -> p (o h t)"),
                          qc2.rearrange("p (g q) -> p g q", q=P), start=True, stop=True).then_inc(s_stt, 1)

            def pv(hf, half):
                pe.wait_ge(s_sel, 4 * hf + 4)
                pe.wait_ge(s_vz, hf + 1)
                pe.wait_ge(s_vcz, 2 * hf + 2)
                if not isinstance(hf, int) or hf >= 1:
                    pe.wait_ge(s_osb, hf)
                O = pb(6)
                for step in range(5):
                    for q in range(4):
                        rows = slice(32 * q, 32 * q + 32)
                        pr = probs[:, 4 * half + q, :]
                        hh, kb = ((0, 0), (0, 1), (1, 1), (1, 0), (0, 0))[step]
                        if step == 4:
                            ins = pe.matmul(O[rows, 256:512].rearrange("p (g q) -> p g q", q=P), Vcz[:, half, q, :],
                                            pr[:, 512:1024].rearrange("p (g q) -> p g q", q=256)[:, :, P:256],
                                            start=True, stop=True)
                            continue
                        win = slice(16, 48) if hh == 0 else slice(0, 32)
                        lhs = Vz[:, half, kb, 2 * q + hh, win]
                        if kb == 0:
                            pe.matmul(O[rows, 0:T], lhs, pr[:, T * hh:T * hh + T], start=(hh == 0),
                                      stop=(hh == 1))
                        else:
                            pe.matmul(O[rows, P:T], lhs, pr[:, 512 + T * hh:512 + T * hh + P], start=False,
                                      stop=False)
                ins.then_inc(s_pv, 1)

            def max_T(hf):
                pe.wait_ge(s_m, 4 * hf + 4)
                pe.transpose(pb(7)[:, 0:P], M[:], ident[:]).then_inc(s_mt, 1)

            def o_T(hf):
                pe.wait_ge(s_osb, hf + 1)
                for i in range(4):
                    ins = pe.transpose(pb(7)[:, P * i:P * i + P], o_sb[:, P * i:P * i + P], ident[:])
                ins.then_inc(s_ot, 1)

            def y_T(b):
                pe.wait_ge(s_y, 2 * b + 2)
                for i in range(2):
                    ins = pe.transpose(pb(7)[:, P * i:P * i + P], y_sb[:, i, :], ident[:])
                ins.then_inc(s_yt, 1)

            def project(b):
                pe.wait_ge(s_yts, b + 1)
                for i in range(2):
                    ins = pe.matmul(pb(7)[:, C * i:C * i + C], yT[:, P * i:P * i + P], w_p[:], start=True, stop=True)
                ins.then_inc(s_att, 1)

            def body(b, prev, cur, p1a, p1b):
                for k in range(NP):
                    if cur:
                        pass2(b, k)
                    if p1a and k < 4:
                        pass1(2 * b + 3, b + 1, 1, k)
                    if p1b and k >= 4:
                        if k == 4:
                            pe.wait_ge(s_ld, 16 * NLD * (b + 3))
                        pass1(2 * b + 4, b + 2, 0, k - 4)
                    if prev and k == 0:
                        if not isinstance(b, int) or b >= 2:
                            pe.wait_ge(s_x1, b - 1)
                        o_T(2 * b - 2)
                    if prev and k == 1:
                        pv(2 * b - 1, 1)
                    if p1a and k == 1:
                        if prev:
                            pe.wait_ge(s_yn, 2 * b - 1)
                        max_T(2 * b + 2)
                    if prev and k == 3:
                        if p1a:
                            pe.wait_ge(s_n2, 2 * b + 3)
                        else:
                            pe.wait_ge(s_yn, 2 * b - 1)
                        o_T(2 * b - 1)
                    if cur and k == 5:
                        pv(2 * b, 0)
                    if p1a and k == 5:
                        if prev:
                            pe.wait_ge(s_yn, 2 * b)
                        else:
                            pe.wait_ge(s_n2, 3)
                        max_T(2 * b + 3)
                    if prev and k == 6:
                        if p1a:
                            pe.wait_ge(s_n2, 2 * b + 4)
                        else:
                            pe.wait_ge(s_yn, 2 * b)
                        y_T(b - 1)
                    if prev and k == 7:
                        project(b - 1)

            pe.wait_ge(s_full, 3 * nchunk)
            pe.wait_ge(s_v, nchunk)
            pe.wait_ge(s_vc, 2)
            pe.wait_ge(s_abias, 1)
            pe.wait_ge(s_kcl, 16 * 6)
            pe.wait_ge(s_ld, 16 * NLD)
            for hf in range(3):
                if hf == 2:
                    pe.wait_ge(s_ld, 16 * NLD * 2)
                for j in range(4):
                    pass1(hf, hf // 2, hf % 2, j)
                if hf:
                    if hf == 2:
                        pe.wait_ge(s_n2, 1)
                    max_T(hf - 1)
            pe.wait_ge(s_n2, 2)
            body(0, False, True, True, True)
            body(1, True, True, True, True)
            with pe.Fori(2, 6) as b:
                body(b, True, True, True, True)
            body(6, True, True, True, False)
            body(7, True, True, False, False)
            body(8, True, False, False, False)

            pe.wait_ge(s_ew, 16 * 6)
            for c in range(nchunk):
                pe.wait_ge(s_z, 2 * c + 1)
                if c:
                    pe.wait_ge(s_zT, c)
                for i in range(CT):
                    ins = pe.transpose(pb(0)[:, P * i:P * i + P], xh[:, i, :], ident[:])
                ins.then_inc(s_zTp, 1)
                pe.wait_ge(s_zT, c + 1)
                if c:
                    pe.wait_ge(s_lg, c)
                for i in range(CT):
                    ins = pe.matmul(pb(1)[:, E * i:E * i + E], xT[:, P * i:P * i + P], w_r[:], start=True, stop=True)
                ins.then_inc(s_lgp, 1)
            pe.wait_ge(s_lg, nchunk)
            pe.wait_ge(s_rt, 19)
            pe.matmul(pb(1)[:, 0:E], before[:], rows_bf[:], start=True, stop=True)
            pe.matmul(pb(1)[:, E:2 * E], ones_bf[:], rows_bf[:], start=True, stop=True).then_inc(s_rkp, 1)

            def group_T(g, u):
                pe.wait_ge(s_xg[u], 16 * (g // 2 + 1))
                if not isinstance(g, int) or g >= 1:
                    pe.wait_ge(s_gTc, g)
                for i in range(GB):
                    ins = pe.transpose(pb(6)[:, P * i:P * i + P], xg[u][:, i, :], ident[:])
                ins.then_inc(s_gT, 1)

            def hidden(j, g, u, n):
                e = pe.value_load(owner[0:1, bass.ds(j, 1)], min_val=0, max_val=E - 1)
                if n == 0:
                    pe.wait_ge(s_gTc, g + 1)
                if not isinstance(j, int) or j >= 2:
                    pe.wait_ge(s_hc, j - 1)
                pe.matmul(pb(n % 2), xnT[u][:, P * n:P * n + P], w1[:, bass.ds(e, 1), :].rearrange("p o f -> p (o f)"),
                          start=True, stop=True).then_inc(s_h, 1)

            def hidden_T(j, v):
                pe.wait_ge(s_hc, j + 1)
                if not isinstance(j, int) or j >= 2:
                    pe.wait_ge(s_hTc, j - 1)
                for k in range(FC):
                    ins = pe.transpose(pb(2 + v)[:, P * k:P * k + P], hid[v][:, P * k:P * k + P], ident[:])
                ins.then_inc(s_hT, 1)

            def outp(j, v):
                e = pe.value_load(owner[0:1, bass.ds(j, 1)], min_val=0, max_val=E - 1)
                pe.wait_ge(s_hTc, j + 1)
                if not isinstance(j, int) or j >= 2:
                    pe.wait_ge(s_yc, j - 1)
                for k in range(FC):
                    ins = pe.matmul(pb(4 + v)[:, 0:C], hidT[v][:, P * k:P * k + P],
                                    w2[:, bass.ds(e, 1), k, :].rearrange("p o c -> p (o c)"),
                                    start=(k == 0), stop=(k == FC - 1))
                ins.then_inc(s_yp, 1)

            def blocks(i, first, last):
                for u in range(2):
                    for n in range(GB):
                        j = 8 * i + GB * u + n
                        hidden(j, 2 * i + u, u, n)
                        if n == 1 and not (last and u == 1):
                            group_T(2 * i + u + 1, 1 - u)
                        if not (first and u == 0 and n < 1):
                            hidden_T(j - 1, (n + 1) % 2)
                        if not (first and u == 0 and n < 2):
                            outp(j - 2, n % 2)

            pe.wait_ge(s_slot, 1)
            group_T(0, 0)
            blocks(0, True, False)
            with pe.Fori(1, NG // 2 - 1) as i:
                blocks(i, False, False)
            blocks(NG // 2 - 1, False, True)
            hidden_T(NBLK - 1, 1)
            outp(NBLK - 2, 0)
            outp(NBLK - 1, 1)


_PERM = lambda w: w.reshape(w.shape[0], NP, 2, D).transpose(0, 2, 3, 1).reshape(w.shape[0], C)


def kernel(**inputs):
    import numpy as np
    import concourse.bacc as bacc
    from concourse.bass_utils import run_bass_kernel_spmd as run

    inp = {k: np.ascontiguousarray(v) for k, v in inputs.items()}
    g = lambda n: inp["L0_" + n]
    col = lambda v: np.ascontiguousarray(v.reshape(-1, 1))
    arrays = {
        "x": inp["x"].reshape(B * T, C), "ctx": inp["ctx_512"].reshape(B * TC, TC),
        "gx": inp["g_xattn"].reshape(1), "gf": inp["g_ffn"].reshape(1),
        "wq": _PERM(g("xattn_Wq")), "wk": _PERM(g("xattn_Wk")), "wcq": _PERM(g("xattn_Wcq")),
        "wck": _PERM(g("xattn_Wck")), "wv": g("xattn_Wv"), "wcv": g("xattn_Wcv"), "wp": g("xattn_Wp"),
        "bq": col(_PERM(g("xattn_bq").reshape(1, C))), "bk": col(_PERM(g("xattn_bk").reshape(1, C))),
        "bcq": col(_PERM(g("xattn_bcq").reshape(1, C))), "bck": col(_PERM(g("xattn_bck").reshape(1, C))),
        "bv": col(g("xattn_bv")), "bcv": col(g("xattn_bcv")), "bp": g("xattn_bp"),
        "w1": g("ffn_W1"), "b1": g("ffn_b1"), "w2": g("ffn_W2"), "b2": g("ffn_b2"),
        "wr": g("ffn_Wr"), "br": g("ffn_br"), "lng": col(g("ffn_ln_g")), "lnb": col(g("ffn_ln_b")),
    }
    arrays = {k: np.ascontiguousarray(v) for k, v in arrays.items()}
    nc = bacc.Bacc("TRN2", target_bir_lowering=False, num_devices=1)
    aps = {k: nc.dram_tensor("in_" + k, v.shape, mybir.dt.from_np(v.dtype), kind="ExternalInput").ap()
           for k, v in arrays.items()}
    out = nc.dram_tensor("out", [B * T, C], F32, kind="ExternalOutput").ap()
    build(nc, aps, out)
    r = run(nc, [{"in_" + k: v for k, v in arrays.items()}], core_ids=[0])
    return r.results[0]["out"].reshape(B, T, C)
```

```python
from contextlib import ExitStack

import concourse.bass as bass
from concourse import mybir

ALU = mybir.AluOpType
ACT = mybir.ActivationFunctionType
AX_X = mybir.AxisListType.X
F32 = mybir.dt.float32
BF16 = mybir.dt.bfloat16
I32 = mybir.dt.int32
U32 = mybir.dt.uint32

P = 128
B = 8
T = 256
TC = 64
C = 128
H = 16
D = C // H
NP = H // 2
NT = B * T // P
E = 8
F = 512
FC = F // P
SCALE = float(D) ** -0.5
EPS = 1e-5
NEG = -1e30

R = 2 * D
NS = 2
SHIFT = 3 * R
QROWS, KROWS = 4 * R, 3 * R
QRUNS = [(0, 0, 4 * R), (4 * R, 0, 2 * R), (6 * R, 0, R)]
KRUNS = [(0, 0, 3 * R), (4 * R, R, 2 * R), (6 * R, 2 * R, R)]
XW = 2 * C + 2
DEAD = 1 << 20
RING = 3
VW = 48
GB = 4
NG = -(-(NT + E - 1) // GB)
NBLK = NG * GB
NSLOT = NBLK * P


def build(nc, a, out):
    nchunk = 4
    CT = 4
    with ExitStack() as ctx:
        def sb(name, shape, dt=F32):
            return ctx.enter_context(nc.sbuf_tensor(name, shape, dt))

        def sem(name):
            return ctx.enter_context(nc.semaphore(name))

        def dram(name, shape, dt):
            return nc.dram_tensor(name, shape, dt, kind="Internal").ap()

        ps_all = ctx.enter_context(nc.psum_tensor("ps_all", [P, 8 * 512], F32))

        def pb(i, n=1):
            return ps_all[:, 512 * i:512 * (i + n)]

        q_scr = dram("q_scr", [B, 2, QROWS, NP * T], BF16)
        k_scr = dram("k_scr", [B, KROWS, NP * T], BF16)
        kc_scr = dram("kc_scr", [KROWS, NP * B * TC], BF16)
        m_scr = dram("m_scr", [2 * B, NS, 32, P], BF16)
        xs_scr = dram("xs_scr", [NSLOT, XW], F32)

        xp = sb("xp", [P, NT, XW])
        x_sb = xp[:, :, C:2 * C]
        v_all = sb("v_all", [P, NT, C])
        vc_all = sb("vc_all", [P, B, C])
        K = sb("K", [P, RING, NP, 2, T], BF16)
        K0 = sb("K0", [P, NP * T], BF16)
        QQ = sb("QQ", [P, RING, 2, NP, T], BF16)
        Kc = sb("Kc", [P, NP * B, 2, TC], BF16)
        probs = sb("probs", [P, NP, 1024])
        Vz = sb("Vz", [P, 2, 2, H // 2, VW])
        Vcz = sb("Vcz", [P, 2, NP // 2, 32])
        ident = sb("ident", [P, P])
        ident_bf = sb("ident_bf", [P, P], BF16)
        causal = sb("causal", [P, P], BF16)
        before = sb("before", [P, P], BF16)
        ones_bf = sb("ones_bf", [P, P], BF16)
        half_neg = sb("half_neg", [P, 2 * NT])
        eps2 = sb("eps2", [P, 2])
        wpack = sb("wpack", [P, 5 * C + E])
        w_q = wpack[:, 0:3 * C].rearrange("p (j c) -> p j c", j=3)
        w_v = wpack[:, 3 * C:4 * C]
        w_p = wpack[:, 4 * C:5 * C]
        w_r = wpack[:, 5 * C:5 * C + E]
        cpack = sb("cpack", [TC, 2 * C])
        w_ck, w_cv = cpack[:, 0:C], cpack[:, C:2 * C]
        cols = sb("cols", [P, 12])
        b_col = cols[:, 0:4]
        bv_col = cols[:, 4:6]
        ln_g, ln_b = cols[:, 6:7], cols[:, 7:8]
        own_rows = cols[:, 8:10]
        one_rows = cols[:, 10:12]
        rpack = sb("rpack", [P, C + E + 2])
        bp_bc = rpack[:, 0:C]
        br_bc = rpack[:, C:C + E]
        gate_x = rpack[:, C + E:C + E + 2]
        bvs = sb("bvs", [P, 1])
        bvs_w = sb("bvs_w", [P, P])
        att_bias = sb("att_bias", [P, C])
        tanh_g = sb("tanh_g", [P, 2])
        ctx_sb = sb("ctx_sb", [P, 4, TC])
        ctxT = sb("ctxT", [TC, B * TC])
        ctxT2 = sb("ctxT2", [TC, B, 2, TC])
        st6 = sb("st6", [P, NT, 6])
        mv = sb("mv", [P, NT, 2])
        rstd = sb("rstd", [P, NT])
        xh = sb("xh", [P, 2, CT, C])
        xT = sb("xT", [P, 2, CT * P])
        flat = probs[:].rearrange("p n q -> p (n q)")
        full = flat[:, 0:1536].rearrange("p (j t) -> p j t", j=3)
        rest = flat[:, 1536:3072].rearrange("p (j t) -> p j t", j=3)
        piece = [flat[:, 3072 + 2304 * i:5376 + 2304 * i].bitcast(BF16).rearrange("p (j i t) -> p j i t", j=3, i=3)
                 for i in range(2)]
        kflat = K[:].rearrange("p r n h t -> p (r n h t)").bitcast(F32)
        cfull = kflat[:, 2048:2560]
        cpiece = kflat[:, 2560:3328].bitcast(BF16).rearrange("p (i t) -> p i t", i=3)
        zrows = kflat[:, 0:NP * T // 2].bitcast(BF16)
        Kc0 = kflat[:, 4096:6144].bitcast(BF16)
        top = sb("top", [P, NP // 2, 16])
        M = sb("M", [P, P])
        shift = sb("shift", [32, NS, P], BF16)
        o_sb = sb("o_sb", [P, 512])
        rec = sb("rec", [P, 32])
        yn = sb("yn", [P, 2, 2, 64])
        y_sb = sb("y_sb", [P, 2, C])
        yT = sb("yT", [P, T])
        xb = sb("xb", [P, 2, C])

        w1 = sb("w1", [P, E, F])
        w2 = sb("w2", [P, E, FC, C])
        b1_bc = kflat[:, 0:E * F].rearrange("p (e f) -> p e f", e=E)
        b2_bc = kflat[:, E * F:E * F + E * C].rearrange("p (e c) -> p e c", e=E)
        zrow = sb("zrow", [P, XW])
        iota_i = sb("iota_i", [P, 32], I32)
        iota = sb("iota", [P, 32])
        st6z = sb("st6z", [P, 2, 6])
        mvz = sb("mvz", [P, 2, 2])
        rs = sb("rs", [P, 4, 2])
        z = sb("z", [P, 2, C])
        zT = sb("zT", [P, T])
        logit = sb("logit", [P, NT, E])
        top1 = sb("top1", [P, NT])
        work = sb("work", [P, NT, E])
        onehot = sb("onehot", [P, NT, E])
        cum = [sb("cum_a", [P, NT, E]), sb("cum_b", [P, NT, E])]
        gate = sb("gate", [P, NT])
        rows_bf = sb("rows_bf", [P, E], BF16)
        base = sb("base", [P, 2 * E])
        over = sb("over", [P, E, NT])
        nb = [sb("nb_a", [P, E]), sb("nb_b", [P, E])]
        start = sb("start", [P, E])
        slot_f = sb("slot_f", [P, NT])
        slot = sb("slot", [P, NT], I32)
        passed = sb("passed", [P, NBLK, E])
        own_f = sb("own_f", [P, NBLK])
        owner = sb("owner", [P, NBLK], I32)
        pflat = flat
        xg = [pflat[:, 512 * i:512 * i + 512].rearrange("p (g c) -> p g c", g=GB) for i in range(2)]
        xr = [v[:, 0:GB * (C + 2)].rearrange("p (g c) -> p g c", g=GB)
              for v in (xh[:].rearrange("p u t c -> p (u t c)"), xT[:].rearrange("p u t -> p (u t)"))]
        xnT = [pflat[:, 1024 + 512 * i:1536 + 512 * i] for i in range(2)]
        hid = [pflat[:, 2048 + 512 * i:2560 + 512 * i] for i in range(2)]
        hidT = [pflat[:, 3072 + 512 * i:3584 + 512 * i] for i in range(2)]
        yg = [pflat[:, 4096 + 512 * i:4608 + 512 * i].rearrange("p (g c) -> p g c", g=GB) for i in range(2)]
        yb = [pflat[:, 5120 + P * i:5120 + P * i + P] for i in range(2)]

        s_stand_sp = sem("sp_wait_stands_alone")
        s_stand_pool = sem("pool_wait_stands_alone")
        s_stand_act = sem("act_wait_stands_alone")
        s_stand_dve = sem("dve_wait_stands_alone")
        s_w = sem("weights_loaded")
        s_x = [sem(f"x_loaded_{c}") for c in range(4)]
        s_cst = sem("constants_made")
        s_zero = sem("operands_zeroed")
        s_init = sem("scratch_rows_written")
        s_tanh = sem("tanh_done")
        s_wp = sem("wp_scaled")
        s_bvs = sem("value_bias_summed")
        s_bmm = sem("bias_product_done")
        s_abias = sem("attention_bias_done")
        s_ctxT = sem("context_transposed")
        s_ctxs = sem("context_copied")
        s_kcps = sem("context_keys_projected")
        s_kcf = sem("context_keys_full")
        s_kcp = sem("context_pieces_step")
        s_kcw = sem("context_pieces_written")
        s_kcl = sem("context_keys_loaded")
        s_vcps = sem("context_values_projected")
        s_vc = sem("context_values_copied")
        s_st = sem("stats_step")
        s_rstd = sem("rstd_done")
        s_xh = sem("xhat_done")
        s_xTp = sem("xhat_transposed")
        s_xT = sem("xT_copied")
        s_pr = sem("projections_done")
        s_full = sem("projections_copied")
        s_v = sem("values_copied")
        s_pw = [sem(f"pieces_written_{c}") for c in range(4)]
        s_p1 = sem("first_piece_done")
        s_p2 = sem("rest_done")
        s_p2b = sem("second_piece_done")
        s_p3 = sem("third_piece_done")
        s_kcpad = sem("context_keys_padded")

        s_ldq = sem("queries_loaded")
        s_ldk = sem("keys_loaded")
        s_pad = sem("keys_padded")
        s_s = sem("scores_ready")
        s_red = sem("scores_reduced")
        s_m = sem("maxima_step")
        s_mt = sem("maxima_transposed")
        s_n1 = sem("shift1_done")
        s_n2 = sem("shift2_done")
        s_mw = sem("shift_written")
        s_mr = sem("shift_rows_loaded")
        s_stt = sem("scoresT_ready")
        s_exp = sem("exp_done")
        s_sel = sem("probs_masked")
        s_vz = sem("v_blocks_ready")
        s_vcz = sem("vc_blocks_ready")
        s_pv = sem("pv_done")
        s_osb = sem("o_copied")
        s_ot = sem("o_transposed")
        s_rec = sem("reciprocal_done")
        s_yn = sem("heads_normalised")
        s_y = sem("y_summed")
        s_yt = sem("y_transposed")
        s_yts = sem("yT_copied")
        s_xb = sem("x_plus_bias")
        s_att = sem("attention_projected")
        s_x1 = sem("x1_done")
        s_ew = sem("expert_weights_loaded")
        s_eb = sem("expert_biases_loaded")
        s_xsz = sem("slots_zeroed")
        s_io = sem("iota_made")
        s_zst = sem("ffn_stats_step")
        s_zr = sem("ffn_rstd_step")
        s_z = sem("z_done")
        s_zTp = sem("z_transposed")
        s_zT = sem("zT_copied")
        s_lgp = sem("logits_projected")
        s_lg = sem("logits_done")
        s_xn = sem("expert_input_done")
        s_rt = sem("routing_step")
        s_ge = sem("gate_exp_done")
        s_rkp = sem("ranks_counted")
        s_slot = sem("slots_done")
        s_sc = sem("tokens_scattered")
        s_xg = [sem("group_loaded_a"), sem("group_loaded_b")]
        s_xr = [sem("records_loaded_a"), sem("records_loaded_b")]
        s_gT = sem("group_transposed")
        s_gTc = sem("group_copied")
        s_h = sem("hidden_projected")
        s_hc = sem("hidden_biased")
        s_hT = sem("hidden_transposed")
        s_hTc = sem("hidden_activated")
        s_yp = sem("expert_output_projected")
        s_yc = sem("expert_output_biased")
        s_yw = [sem("output_written_a"), sem("output_written_b")]
        s_yb = sem("expert_output_biased_b")

        block = ctx.enter_context(nc.Block())
        weights = [(wpack[:], a["wpack"]), (cpack[:], a["cpack"]), (cols[:], a["cols"]),
                   (rpack[:], a["rpack"].partition_broadcast(P)),
                   (ctx_sb[:], a["ctx"].rearrange("(t p) c -> p t c", p=P))]
        NLD = 3

        @block.sync
        def _(sp):
            for c in range(nchunk):
                sp.dma_start(x_sb[:, CT * c:CT * c + CT, :],
                             a["x"][CT * P * c:CT * P * (c + 1)].rearrange("(t p) c -> p t c", p=P)).then_inc(s_x[c], 16)
                if c == 0:
                    for dst, src in weights:
                        sp.dma_start(dst, src).then_inc(s_w, 16)
            for dst, src in ((w1[:], a["w1"].rearrange("e p f -> p e f")),
                             (w2[:], a["w2"].rearrange("e (k p) c -> p e k c", p=P))):
                sp.dma_start(dst, src).then_inc(s_ew, 16)
            sp.wait_ge(s_zero, 1)
            for ty in range(2):
                sp.dma_start(q_scr[:, ty, SHIFT:QROWS, :].rearrange("b r t -> r b t"),
                             zrows[0:R].unsqueeze(1).to_broadcast([R, B, NP * T])).then_inc(s_init, 16)

            def context_keys():
                sp.wait_ge(s_kcp, 4)
                sp.dma_start(kc_scr.rearrange("(i r) (n t) -> (r n) i t", i=3, n=NP), cpiece).then_inc(s_kcw, 16)
                sp.wait_ge(s_kcw, 16)
                for run in KRUNS:
                    sp.dma_start(Kc0[run[0]:run[0] + run[2]], kc_scr[run[1]:run[1] + run[2]]).then_inc(s_kcl, 16)

            def write_pieces(c):
                for j in range(3):
                    sp.wait_ge(s_p3, 3 * c + j + 1)
                    for bb in range(2):
                        b = 2 * c + bb
                        dst = k_scr[b] if j == 1 else q_scr[b, j // 2, 0:SHIFT]
                        sp.dma_start(dst.rearrange("(i r) (n t) -> (r n) i t", i=3, n=NP),
                                     piece[c % 2][:, j, :, bb * T:(bb + 1) * T]).then_inc(s_pw[c], 16)

            def load(b):
                for run in QRUNS:
                    sp.dma_start(QQ[run[0]:run[0] + run[2], bass.ds(b % RING, 1)].rearrange("r o y n t -> r (o y) (n t)"),
                                 q_scr[bass.ds(b, 1), :, run[1]:run[1] + run[2], :]
                                 .rearrange("o y r t -> r (o y) t")).then_inc(s_ldq, 16)
                if not isinstance(b, int) or b >= 1:
                    sp.wait_ge(s_pad, 2 * b)
                    sp.sem_inc(s_stand_sp, 1)
                for run in KRUNS:
                    sp.dma_start(K0[run[0]:run[0] + run[2], :],
                                 k_scr[bass.ds(b, 1), run[1]:run[1] + run[2]].rearrange("o r t -> r (o t)")
                                 ).then_inc(s_ldk, 16)
                sp.wait_ge(s_ldq, 16 * NLD * (b + 1))
                sp.sem_inc(s_stand_sp, 1)
                sp.wait_ge(s_ldk, 16 * NLD * (b + 1))
                sp.sem_inc(s_stand_sp, 1)

            def shifts(hf, b, half):
                sp.wait_ge(s_n2, hf + 1)
                sp.sem_inc(s_stand_sp, 1)
                sp.dma_start(m_scr[bass.ds(hf, 1)].rearrange("o i r q -> r (o i) q"), shift[:]).then_inc(s_mw, 16)
                sp.wait_ge(s_mw, 16 * (hf + 1))
                sp.sem_inc(s_stand_sp, 1)
                sp.dma_start(QQ[SHIFT:SHIFT + 2 * NS, bass.ds(b % RING, 1), :, 4 * half:4 * half + 4, :]
                             .rearrange("i o y n t -> i (o y) (n t)"),
                             m_scr[bass.ds(hf, 1)].rearrange("o i (h y r) q -> (o i h) y (r q)", h=2, y=2)
                             ).then_inc(s_mr, 16)
                sp.wait_ge(s_mr, 16 * (hf + 1))
                sp.sem_inc(s_stand_sp, 1)

            write_pieces(0)
            sp.wait_ge(s_init, 32)
            sp.wait_ge(s_zero, 4)
            sp.wait_ge(s_pw[0], 16 * 6)
            load(0)
            context_keys()
            write_pieces(1)
            load(1)
            write_pieces(2)
            write_pieces(3)
            for c in range(1, nchunk):
                sp.wait_ge(s_pw[c], 16 * 6)
            sp.wait_ge(s_io, 4)
            sp.dma_start(xs_scr.rearrange("(n p) c -> p n c", p=P),
                         zrow[:].unsqueeze(1).to_broadcast([P, NBLK, XW])).then_inc(s_xsz, 16)
            shifts(0, 0, 0)
            shifts(1, 0, 1)

            def body(b, ld, m0, m1):
                if ld:
                    sp.wait_ge(s_stt, 8 * b)
                    sp.sem_inc(s_stand_sp, 1)
                    load(b + 2)
                if m0:
                    shifts(2 * b + 2, b + 1, 0)
                if m1:
                    shifts(2 * b + 3, b + 1, 1)

            body(0, True, True, True)
            with sp.Fori(1, 6) as b:
                body(b, True, True, True)
            body(6, False, True, True)
            sp.wait_ge(s_stt, 8 * B)
            sp.dma_start(kflat[:, 0:E * (F + C)], a["bpack"].partition_broadcast(P)).then_inc(s_eb, 16)

            def load_in(g, u):
                if not isinstance(g, int) or g >= 2:
                    sp.wait_ge(s_gT, g - 1)
                    sp.sem_inc(s_stand_sp, 1)
                sp.dma_start(xg[u], xs_scr[bass.ds(g * GB * P, GB * P), 0:C]
                             .rearrange("(g p) c -> p g c", p=P)).then_inc(s_xg[u], 16)

            def load_rest(g, u):
                if not isinstance(g, int) or g >= 2:
                    sp.wait_ge(s_yw[u], 16 * GB * (g // 2))
                    sp.sem_inc(s_stand_sp, 1)
                sp.dma_start(xr[u], xs_scr[bass.ds(g * GB * P, GB * P), C:XW]
                             .rearrange("(g p) c -> p g c", p=P)).then_inc(s_xr[u], 16)

            sp.wait_ge(s_sc, 16 * NT)
            load_in(0, 0)
            load_in(1, 1)
            load_rest(0, 0)
            load_rest(1, 1)
            load_in(2, 0)
            load_in(3, 1)
            load_rest(2, 0)
            with sp.Fori(1, NG // 2 - 1) as i:
                load_in(2 * i + 2, 0)
                load_rest(2 * i + 1, 1)
                load_in(2 * i + 3, 1)
                load_rest(2 * i + 2, 0)
            load_rest(NG - 1, 1)


        @block.gpsimd
        def _(pool):
            pool.memset(ident[:], 0.0).then_inc(s_cst, 1)
            pool.memset(causal[:], 0.0).then_inc(s_cst, 1)
            pool.memset(before[:], 1.0).then_inc(s_cst, 1)
            pool.memset(half_neg[:], -0.5).then_inc(s_cst, 1)
            pool.memset(ones_bf[:], 1.0).then_inc(s_cst, 1)
            pool.memset(eps2[:], EPS).then_inc(s_cst, 1)
            pool.wait_ge(s_cst, 6)
            pool.affine_select(out=ident[:], in_=ident[:], compare_op=ALU.not_equal, fill=1.0, base=0,
                               pattern=[[-1, P]], channel_multiplier=1).then_inc(s_cst, 1)
            pool.affine_select(out=causal[:], in_=causal[:], compare_op=ALU.is_ge, fill=NEG, base=0,
                               pattern=[[-1, P]], channel_multiplier=1).then_inc(s_cst, 1)
            pool.affine_select(out=before[:], in_=before[:], compare_op=ALU.is_gt, fill=0.0, base=0,
                               pattern=[[1, P]], channel_multiplier=-1).then_inc(s_cst, 1)
            pool.wait_ge(s_cst, 9)
            pool.tensor_copy(ident_bf[:], ident[:]).then_inc(s_cst, 1)
            def rstd_of(c):
                sl = slice(CT * c, CT * c + CT)
                pool.wait_ge(s_st, 3 * (c + 1))
                pool.tensor_tensor(rstd[:, sl], rstd[:, sl], half_neg[:, 0:CT], ALU.pow).then_inc(s_rstd, 1)

            rstd_of(0)
            for c in range(nchunk):
                if c == 0:
                    pool.memset(kflat[:, 0:NP * T // 2], 0.0).then_inc(s_zero, 1)
                    pool.memset(Kc0.bitcast(F32), 0.0).then_inc(s_zero, 1)
                    pool.memset(QQ[:].rearrange("p r y n t -> p (r y n t)").bitcast(F32), 0.0).then_inc(s_zero, 1)
                    pool.memset(K0[:].bitcast(F32), 0.0).then_inc(s_zero, 1)
                    rstd_of(1)
                    rstd_of(2)
                    rstd_of(3)
                for j in range(3):
                    last = 0 if j == 1 else 2
                    pool.wait_ge(s_p2b, 3 * c + j + 1)
                    if j == 0 and c >= 2:
                        pool.wait_ge(s_pw[c - 2], 16 * 6)
                    pool.tensor_tensor(piece[c % 2][:, j, last, :], rest[:, j, :], piece[c % 2][:, j, 1, :],
                                       ALU.subtract).then_inc(s_p3, 1)
                if c == 0:
                    pool.memset(M[:], 0.0).then_inc(s_zero, 1)
                    pool.memset(Vz[:], 0.0).then_inc(s_zero, 1)
                    pool.memset(Vcz[:], 0.0).then_inc(s_zero, 1)
                    pool.wait_ge(s_zero, 7)
                    pool.memset(Vz[:, :, :, :, 24:25], 1.0).then_inc(s_zero, 1)
                    pool.memset(Vcz[0:64, :, :, 8:9], 1.0).then_inc(s_zero, 1)
                    pool.wait_ge(s_zero, 9)
                    pool.memset(Vcz[64:128, :, :, 24:25], 1.0).then_inc(s_zero, 1)
                    pool.wait_ge(s_zero, 10)
                if c == 1:
                    pool.iota(iota_i[:], pattern=[[1, 32]], base=0, channel_multiplier=0).then_inc(s_io, 1)
                    pool.iota(xp[:, :, 2 * C + 1].bitcast(I32), pattern=[[P, NT]], base=0,
                              channel_multiplier=1).then_inc(s_io, 1)
                    pool.memset(zrow[:], 0.0).then_inc(s_io, 1)
                    pool.wait_ge(s_io, 3)
                    pool.memset(zrow[:, XW - 1:XW].bitcast(I32), DEAD).then_inc(s_io, 1)
                    pool.tensor_copy(iota[:], iota_i[:]).then_inc(s_io, 1)

            def v_blocks(hf, b, half):
                if not isinstance(hf, int) or hf >= 2:
                    pool.wait_ge(s_pv, hf - 1)
                    pool.sem_inc(s_stand_pool, 1)
                pool.tensor_copy(Vz[:, half, :, :, 16:24],
                                 v_all[:, bass.ds(2 * b, 2), 64 * half:64 * half + 64]
                                 .rearrange("p k (h d) -> p k h d", d=D)).then_inc(s_vz, 1)

            def select(b, k):
                pool.wait_ge(s_exp, 8 * b + k + 1)
                pool.sem_inc(s_stand_pool, 1)
                v = probs[:, k, :].rearrange("p (g q) -> p g q", q=256)[:, :, 0:128]
                pool.affine_select(out=v, in_=v, compare_op=ALU.is_ge, fill=0.0, base=0,
                                   pattern=[[0, 4], [1, P]], channel_multiplier=-1).then_inc(s_sel, 1)

            def y_sum(hf, half):
                pool.wait_ge(s_yn, hf + 1)
                if half == 0 and (not isinstance(hf, int) or hf >= 2):
                    pool.wait_ge(s_yt, bass_half(hf))
                pool.tensor_tensor(y_sb[:, :, 64 * half:64 * half + 64], yn[:, 0], yn[:, 1], ALU.add).then_inc(s_y, 1)

            def bass_half(hf):
                return hf // 2

            def ffn_norm(b):
                n0 = 5 * b
                pool.wait_ge(s_zst, 3 * b + 3)
                pool.tensor_tensor(rs[:, 0, :], rs[:, 0, :], half_neg[:, 0:2], ALU.pow).then_inc(s_zr, 1)
                pool.wait_ge(s_zr, n0 + 1)
                pool.tensor_tensor(rs[:, 1, :], mvz[:, :, 1], rs[:, 0, :], ALU.mult).then_inc(s_zr, 1)
                pool.wait_ge(s_zr, n0 + 2)
                pool.tensor_tensor(rs[:, 1, :], rs[:, 1, :], rs[:, 0, :], ALU.mult).then_inc(s_zr, 1)
                pool.wait_ge(s_zr, n0 + 3)
                pool.tensor_tensor(rs[:, 1, :], rs[:, 1, :], eps2[:], ALU.add).then_inc(s_zr, 1)
                pool.wait_ge(s_zr, n0 + 4)
                pool.tensor_tensor(rs[:, 1, :], rs[:, 1, :], half_neg[:, 0:2], ALU.pow).then_inc(s_zr, 1)

            def body(b, prev2, prev, cur):
                for k in range(NP):
                    if cur:
                        if k == 0:
                            v_blocks(2 * b, b, 0)
                        if k == 4:
                            v_blocks(2 * b + 1, b, 1)
                        select(b, k)
                    if prev and k == 0:
                        y_sum(2 * b - 2, 0)
                    if prev2 and k == 1:
                        ffn_norm(b - 2)
                    if prev:
                        if k == 3:
                            y_sum(2 * b - 1, 1)
                        if k == 4:
                            if not isinstance(b, int) or b >= 2:
                                pool.wait_ge(s_x1, b - 1)
                            pool.sem_inc(s_stand_pool, 1)
                            pool.tensor_tensor(
                                xb[:], x_sb[:, bass.ds(2 * b - 2, 2), :],
                                att_bias[:].unsqueeze(1).to_broadcast([P, 2, C]), ALU.add).then_inc(s_xb, 1)

            pool.wait_ge(s_zero, 10)
            pool.wait_ge(s_v, nchunk)
            pool.wait_ge(s_vc, 2)
            body(0, False, False, True)
            pool.wait_ge(s_abias, 1)
            body(1, False, True, True)
            with pool.Fori(2, B) as b:
                body(b, True, True, True)
            body(B, True, True, False)
            body(B + 1, True, False, False)

            pool.wait_ge(s_slot, 2)
            pool.wait_ge(s_xsz, 16)
            pool.wait_ge(s_xn, 2 * B)
            pool.wait_ge(s_io, 5)
            for t in range(NT):
                pool.indirect_dma_start(out=xs_scr, out_offset=bass.IndirectOffsetOnAxis(
                    ap=slot[:, t:t + 1].bitcast(U32), axis=0), in_=xp[:, t, :], in_offset=None).then_inc(s_sc, 16)

            def write_out(j, g, u, n):
                pool.wait_ge(s_yc, j + 1)
                pool.sem_inc(s_stand_pool, 1)
                pool.indirect_dma_start(out=out, out_offset=bass.IndirectOffsetOnAxis(
                    ap=xr[u][:, n, C + 1:C + 2].bitcast(U32), axis=0), in_=yg[u][:, n, :], in_offset=None,
                    bounds_check=B * T - 1, oob_is_err=False).then_inc(s_yw[u], 16)

            with pool.Fori(0, NG // 2) as i:
                for n in range(2 * GB):
                    write_out(2 * GB * i + n, 2 * i + n // GB, n // GB, n % GB)
            pool.wait_ge(s_yw[0], 16 * GB * NG // 2)
            pool.wait_ge(s_yw[1], 16 * GB * NG // 2)

        @block.scalar
        def _(act):
            act.wait_ge(s_w, 16 * len(weights))
            act.activation(tanh_g[:], gate_x, ACT.Tanh).then_inc(s_tanh, 1)
            act.wait_ge(s_ctxT, 1)
            for i in range(2):
                act.copy(ctxT2[:, :, i, :], pb(7)[0:TC, :].rearrange("p (b t) -> p b t", b=B)).then_inc(s_ctxs, 1)
            act.copy(ctxT[:], pb(7)[0:TC, :]).then_inc(s_ctxs, 1)

            def xT_copy(c):
                act.wait_ge(s_xTp, c + 1)
                if c >= 2:
                    act.wait_ge(s_pr, 4 * (c - 1))
                act.copy(xT[:, c % 2], pb(5 * (c % 2))).then_inc(s_xT, 1)

            xT_copy(0)
            act.wait_ge(s_wp, 2)
            for c in range(nchunk):
                if c >= 2:
                    act.wait_ge(s_pw[c - 2], 16 * 6)
                for j in range(3):
                    first, scale = (2, 1.0) if j == 1 else (0, SCALE)
                    act.wait_ge(s_pr, 4 * c + j + 1)
                    act.activation(piece[c % 2][:, j, first, :], pb(1 + j), ACT.Identity, bias=b_col[:, j:j + 1],
                                   scale=scale).then_inc(s_p1, 1)
                    if c:
                        act.wait_ge(s_p2, 3 * (c - 1) + j + 1)
                    act.activation(full[:, j, :], pb(1 + j), ACT.Identity, bias=b_col[:, j:j + 1],
                                   scale=scale).then_inc(s_full, 1)
                    if j == 1 and c < nchunk - 1:
                        xT_copy(c + 1)
                if c == 0:
                    act.wait_ge(s_kcps, 1)
                    act.activation(cfull, pb(6), ACT.Identity, bias=b_col[:, 3:4]).then_inc(s_kcf, 1)

            def exp(b, k):
                act.wait_ge(s_stt, 8 * b + k + 1)
                if not isinstance(b, int) or b >= 1:
                    act.wait_ge(s_pv, 2 * b - 1 + k // 4)
                act.activation(probs[:, k, :], pb(2 + 2 * (k % 2), 2), ACT.Exp).then_inc(s_exp, 1)

            def vc_blocks(hf, b, half):
                if not isinstance(hf, int) or hf >= 2:
                    act.wait_ge(s_pv, hf - 1)
                for hh in range(2):
                    pr = slice(64 * hh, 64 * hh + 64)
                    act.copy(
                        Vcz[pr, half, :, 16 * hh:16 * hh + 8],
                        vc_all[pr, bass.ds(b, 1), 64 * half:64 * half + 64]
                        .rearrange("p o (n s d) -> p (o n) s d", s=2, d=D)[:, :, hh, :]).then_inc(s_vcz, 1)

            def shift1(hf):
                act.wait_ge(s_mt, hf + 1)
                if not isinstance(hf, int) or hf >= 1:
                    act.wait_ge(s_mw, 16 * hf)
                act.activation(shift[:, 0, :], pb(7)[0:32, 0:P], ACT.Copy, scale=-1.0).then_inc(s_n1, 1)

            def o_copy(hf):
                act.wait_ge(s_pv, hf + 1)
                if not isinstance(hf, int) or hf >= 1:
                    act.wait_ge(s_ot, hf)
                act.copy(o_sb[:], pb(6)).then_inc(s_osb, 1)

            def yT_copy(b):
                act.wait_ge(s_yt, b + 1)
                act.copy(yT[:], pb(7)[:, 0:T]).then_inc(s_yts, 1)

            def zT_copy(b):
                act.wait_ge(s_zTp, b + 1)
                act.copy(zT[:], pb(7)[:, 0:T]).then_inc(s_zT, 1)

            def body(b, prev2, prev, cur, m):
                for k in range(NP):
                    if cur:
                        if k == 2:
                            vc_blocks(2 * b, b, 0)
                        if k == 6:
                            vc_blocks(2 * b + 1, b, 1)
                        exp(b, k)
                    if prev and k == 1:
                        o_copy(2 * b - 1)
                    if m and k == 1:
                        shift1(2 * b + 2)
                    if prev2 and k == 2:
                        zT_copy(b - 2)
                    if prev2 and k == 4:
                        xn_norm(b - 2)
                    if cur and k == 5:
                        o_copy(2 * b)
                    if m and k == 5:
                        shift1(2 * b + 3)
                    if prev and k == 6:
                        yT_copy(b - 1)

            def xn_norm(b):
                act.wait_ge(s_zr, 5 * b + 5)
                act.sem_inc(s_stand_act, 1)
                for i in range(2):
                    act.activation(xp[:, bass.ds(2 * b + i, 1), 0:C].rearrange("p o c -> p (o c)"), z[:, i, :],
                                   ACT.Copy, scale=rs[:, 1, i:i + 1]).then_inc(s_xn, 1)

            act.wait_ge(s_zero, 10)
            act.wait_ge(s_vc, 2)
            shift1(0)
            shift1(1)
            body(0, False, False, True, True)
            body(1, False, True, True, True)
            with act.Fori(2, 7) as b:
                body(b, True, True, True, True)
            body(7, True, True, True, False)
            body(8, True, True, False, False)
            body(9, True, False, False, False)

            act.wait_ge(s_rt, 2)
            act.activation(work[:], work[:], ACT.Exp).then_inc(s_ge, 1)

            def group_T(g, u):
                act.wait_ge(s_gT, g + 1)
                if not isinstance(g, int) or g >= 2:
                    act.wait_ge(s_h, GB * (g - 1))
                act.activation(xnT[u], pb(6), ACT.Identity, bias=ln_b, scale=ln_g).then_inc(s_gTc, 1)

            def hidden_T(j, v):
                act.wait_ge(s_hT, j + 1)
                if not isinstance(j, int) or j >= 2:
                    act.wait_ge(s_yp, j - 1)
                act.activation(hidT[v], pb(2 + v), ACT.Relu).then_inc(s_hTc, 1)

            group_T(0, 0)

            def blocks(i, last):
                for u in range(2):
                    for n in range(GB):
                        if n == 2 and not (last and u == 1):
                            group_T(2 * i + u + 1, 1 - u)
                        hidden_T(GB * (2 * i + u) + n, n % 2)

            blocks(0, False)
            with act.Fori(1, NG // 2 - 1) as i:
                blocks(i, False)
            blocks(NG // 2 - 1, True)

        @block.vector
        def _(dve):
            def pad_keys(b):
                dve.wait_ge(s_ldk, 16 * NLD * (b + 1))
                if not isinstance(b, int) or b >= RING:
                    dve.wait_ge(s_stt, 8 * (b - RING) + 8)
                for h in range(2):
                    dve.tensor_scalar(K[:, bass.ds(b % RING, 1), :, h, :].rearrange("p o n t -> p (o n) t"),
                                       K0[:].rearrange("p (n t) -> p n t", n=NP), own_rows[:, h:h + 1],
                                       one_rows[:, h:h + 1], ALU.mult, ALU.add).then_inc(s_pad, 1)

            def stats(c):
                sl = slice(CT * c, CT * c + CT)
                dve.wait_ge(s_x[c], 16)
                for t in range(CT * c, CT * c + CT):
                    ins = dve.bn_stats(st6[:, t, :], x_sb[:, t, :])
                ins.then_inc(s_st, 1)
                dve.wait_ge(s_st, 3 * c + 1)
                for t in range(CT * c, CT * c + CT):
                    ins = dve.bn_aggr(mv[:, t, :], st6[:, t, :])
                ins.then_inc(s_st, 1)
                dve.wait_ge(s_st, 3 * c + 2)
                dve.tensor_scalar(rstd[:, sl], mv[:, sl, 1], EPS, None, ALU.add).then_inc(s_st, 1)

            def xhat(c):
                dve.wait_ge(s_rstd, c + 1)
                if c >= 2:
                    dve.wait_ge(s_xTp, c - 1)
                for i in range(CT):
                    t = CT * c + i
                    ins = dve.tensor_scalar(xh[:, c % 2, i, :], x_sb[:, t, :], mv[:, t, 0:1], rstd[:, t:t + 1],
                                            ALU.subtract, ALU.mult)
                ins.then_inc(s_xh, 1)

            stats(0)
            dve.wait_ge(s_w, 16 * len(weights))
            dve.tensor_scalar(b_col[:, 0:1], b_col[:, 0:1], SCALE, None, ALU.mult).then_inc(s_wp, 1)
            dve.tensor_scalar(b_col[:, 2:3], b_col[:, 2:3], SCALE, None, ALU.mult).then_inc(s_wp, 1)
            xhat(0)
            stats(1)
            xhat(1)
            dve.wait_ge(s_tanh, 1)
            dve.tensor_tensor(bvs[:], bv_col[:, 0:1], bv_col[:, 1:2], ALU.add).then_inc(s_bvs, 1)
            dve.tensor_scalar(w_p, w_p, tanh_g[:, 0:1], None, ALU.mult).then_inc(s_wp, 1)
            dve.tensor_scalar(bp_bc, bp_bc, tanh_g[:, 0:1], None, ALU.mult).then_inc(s_wp, 1)
            dve.wait_ge(s_bvs, 1)
            dve.tensor_copy(bvs_w[:], bvs[:, 0:1].to_broadcast([P, P])).then_inc(s_bvs, 1)
            stats(2)
            stats(3)
            for c in range(nchunk):
                if 0 < c < nchunk - 1:
                    xhat(c + 1)
                for j in range(3):
                    at = 3 * c + j
                    first = 2 if j == 1 else 0
                    dve.wait_ge(s_full, at + 1)
                    if c:
                        dve.wait_ge(s_p3, at - 2)
                    dve.tensor_tensor(rest[:, j, :], full[:, j, :], piece[c % 2][:, j, first, :],
                                      ALU.subtract).then_inc(s_p2, 1)
                    dve.wait_ge(s_p2, at + 1)
                    if j == 0 and c >= 2:
                        dve.wait_ge(s_pw[c - 2], 16 * 6)
                    dve.tensor_copy(piece[c % 2][:, j, 1, :], rest[:, j, :]).then_inc(s_p2b, 1)
                dve.wait_ge(s_pr, 4 * c + 4)
                dve.tensor_copy(v_all[:, CT * c:CT * c + CT, :],
                                pb(4).rearrange("p (t c) -> p t c", t=CT)).then_inc(s_v, 1)
                if c == 0:
                    dve.wait_ge(s_vcps, 1)
                    dve.tensor_copy(vc_all[:, 0:4, :], pb(7).rearrange("p (b c) -> p b c", b=4)).then_inc(s_vc, 1)
                    dve.wait_ge(s_kcf, 1)
                    dve.tensor_copy(cpiece[:, 2, :], cfull).then_inc(s_kcp, 1)
                    dve.wait_ge(s_kcp, 1)
                    dve.tensor_tensor(cfull, cfull, cpiece[:, 2, :], ALU.subtract).then_inc(s_kcp, 1)
                    dve.wait_ge(s_kcp, 2)
                    dve.tensor_copy(cpiece[:, 1, :], cfull).then_inc(s_kcp, 1)
                    dve.wait_ge(s_kcp, 3)
                    dve.tensor_tensor(cpiece[:, 0, :], cfull, cpiece[:, 1, :], ALU.subtract).then_inc(s_kcp, 1)
                if c == 1:
                    dve.wait_ge(s_vcps, 2)
                    dve.tensor_copy(vc_all[:, 4:8, :], pb(6).rearrange("p (b c) -> p b c", b=4)).then_inc(s_vc, 1)
                    dve.wait_ge(s_bmm, 1)
                    dve.tensor_tensor(att_bias[:], pb(7)[:, 0:C], bp_bc, ALU.add).then_inc(s_abias, 1)
                    pad_keys(0)
                if c == 2:
                    pad_keys(1)
                    dve.wait_ge(s_kcl, 16 * 3)
                    for h in range(2):
                        dve.tensor_scalar(Kc[:, :, h, :], Kc0.rearrange("p (n t) -> p n t", t=TC),
                                          own_rows[:, h:h + 1], one_rows[:, h:h + 1], ALU.mult,
                                          ALU.add).then_inc(s_kcpad, 1)

            def reduce(hf, j):
                g = 4 * hf + j
                at = 2 * (g % 3) if isinstance(hf, int) and hf < 3 else 0
                for i in range(2):
                    dve.wait_ge(s_s, 2 * g + i + 1)
                    dve.tensor_reduce(top[:, j, 8 * i:8 * i + 8], pb(at + i).rearrange("p (g k) -> p g k", k=64), AX_X,
                                      ALU.max).then_inc(s_red, 1)

            def maxima(hf):
                Mv = M[:, 0:32].rearrange("p (h y n u) -> p y h n u", y=2, h=2, n=4)
                dve.wait_ge(s_red, 8 * hf + 8)
                if not isinstance(hf, int) or hf >= 1:
                    dve.wait_ge(s_mt, hf)
                dve.tensor_reduce(Mv[:, 0, :, :, 1].rearrange("p h n -> p n h"),
                                  top[:, :, 0:8].rearrange("p n (h g) -> p n h g", h=2), AX_X, ALU.max).then_inc(s_m, 1)
                dve.tensor_reduce(Mv[:, 0, :, :, 0].rearrange("p h n -> p n h"),
                                  top[:, :, 8:12].rearrange("p n (h g) -> p n h g", h=2), AX_X, ALU.max).then_inc(s_m, 1)
                for u in range(2):
                    dve.tensor_copy(Mv[:, 1, :, :, u].rearrange("p h n -> p n h"),
                                    top[:, :, 12 + 2 * u:14 + 2 * u]).then_inc(s_m, 1)
                dve.wait_ge(s_m, 4 * hf + 4)

            def shift2(hf):
                dve.wait_ge(s_n1, hf + 1)
                dve.scalar_tensor_tensor(out=shift[:, 1, :], in0=pb(7)[0:32, 0:P], scalar=-1.0,
                                         in1=shift[:, 0, :], op0=ALU.mult, op1=ALU.subtract).then_inc(s_n2, 1)

            def normalise(hf):
                O = pb(7).rearrange("p (g r) -> p g r", r=16)
                dve.wait_ge(s_ot, hf + 1)
                dve.reciprocal(rec[:], O[:, :, 8]).then_inc(s_rec, 1)
                dve.wait_ge(s_rec, hf + 1)
                if not isinstance(hf, int) or hf >= 1:
                    dve.wait_ge(s_y, hf)
                dve.tensor_tensor(yn[:].rearrange("p y u (g d) -> p (y u g) d", d=D), O[:, :, 0:8],
                                  rec[:].unsqueeze(2).to_broadcast([P, 32, D]), ALU.mult).then_inc(s_yn, 1)

            def x1(b):
                dve.wait_ge(s_att, b + 1)
                dve.wait_ge(s_xb, b + 1)
                dve.tensor_tensor(x_sb[:, bass.ds(2 * b, 2), :], pb(7)[:, 0:2 * C]
                                  .rearrange("p (u c) -> p u c", u=2), xb[:], ALU.add).then_inc(s_x1, 1)

            def ffn_stats(b):
                at = 3 * b
                dve.wait_ge(s_x1, b + 1)
                for i in range(2):
                    ins = dve.bn_stats(st6z[:, i, :], x_sb[:, bass.ds(2 * b + i, 1), :].rearrange("p o c -> p (o c)"))
                ins.then_inc(s_zst, 1)
                dve.wait_ge(s_zst, at + 1)
                dve.sem_inc(s_stand_dve, 1)
                for i in range(2):
                    ins = dve.bn_aggr(mvz[:, i, :], st6z[:, i, :])
                ins.then_inc(s_zst, 1)
                dve.wait_ge(s_zst, at + 2)
                dve.tensor_scalar(rs[:, 0, :], mvz[:, :, 1], EPS, None, ALU.add).then_inc(s_zst, 1)

            def z_norm(b):
                dve.wait_ge(s_zr, 5 * b + 1)
                for i in range(2):
                    dve.tensor_scalar(z[:, i, :], x_sb[:, bass.ds(2 * b + i, 1), :].rearrange("p o c -> p (o c)"),
                                      mvz[:, i, 0:1], rs[:, 0, i:i + 1], ALU.subtract, ALU.mult).then_inc(s_z, 1)

            def logits(b):
                dve.wait_ge(s_lgp, b + 1)
                dve.tensor_tensor(logit[:, bass.ds(2 * b, 2), :],
                                  pb(7)[:, 0:2 * E].rearrange("p (t e) -> p t e", t=2),
                                  br_bc.unsqueeze(1).to_broadcast([P, 2, E]), ALU.add).then_inc(s_lg, 1)

            def body(b, prev2, prev, p1a, p1b):
                for k in range(NP):
                    if (p1a and k < 4) or (p1b and k >= 4):
                        reduce(2 * b + 3 + k // 4, k % 4)
                        if k % 4 == 3:
                            maxima(2 * b + 3 + k // 4)
                    if prev and k == 0:
                        normalise(2 * b - 2)
                    if prev2 and k == 0:
                        ffn_stats(b - 2)
                    if p1a and k == 1:
                        shift2(2 * b + 2)
                    if prev2 and k == 1:
                        z_norm(b - 2)
                    if p1b and k == 2:
                        pad_keys(b + 2)
                    if prev and k == 3:
                        normalise(2 * b - 1)
                    if prev2 and k == 4:
                        logits(b - 2)
                    if p1a and k == 5:
                        shift2(2 * b + 3)
                    if prev and k == 7:
                        x1(b - 1)

            for hf in range(3):
                for j in range(4):
                    reduce(hf, j)
                    if hf and j == 2:
                        shift2(hf - 1)
                maxima(hf)
            body(0, False, False, True, True)
            body(1, False, True, True, True)
            with dve.Fori(2, 6) as b:
                body(b, True, True, True, True)
            body(6, True, True, True, False)
            body(7, True, True, False, False)
            body(8, True, True, False, False)
            body(9, True, False, False, False)

            step = [0]

            def did(ins):
                step[0] += 1
                ins.then_inc(s_rt, 1)
                dve.wait_ge(s_rt, step[0])

            all_e = [P, NT, E]
            over_e = lambda v: v.unsqueeze(2).to_broadcast(all_e)
            over_t = lambda v: v.unsqueeze(1).to_broadcast(all_e)
            dve.wait_ge(s_lg, B)
            dve.wait_ge(s_io, 5)
            did(dve.tensor_reduce(top1[:], logit[:], AX_X, ALU.max))
            did(dve.tensor_tensor(work[:], logit[:], over_e(top1[:]), ALU.subtract))
            did(dve.tensor_tensor(onehot[:], logit[:], over_e(top1[:]), ALU.is_equal))
            did(dve.tensor_scalar(nb[0][:], iota[:, 0:E], -1.0, float(E), ALU.mult, ALU.add))
            did(dve.tensor_tensor(onehot[:], onehot[:], over_t(nb[0][:]), ALU.mult))
            did(dve.tensor_reduce(top1[:], onehot[:], AX_X, ALU.max))
            did(dve.tensor_tensor(onehot[:], over_t(nb[0][:]), over_e(top1[:]), ALU.is_equal))
            dve.wait_ge(s_ge, 1)
            did(dve.tensor_reduce(gate[:], work[:], AX_X, ALU.add))
            did(dve.reciprocal(gate[:], gate[:]))
            dve.tensor_scalar(xp[:, :, 2 * C], gate[:], tanh_g[:, 1:2], None, ALU.mult).then_inc(s_slot, 1)
            src, dst = onehot, cum[0]
            for sh in (1, 2, 4, 8):
                did(dve.tensor_copy(dst[:, 0:sh, :], src[:, 0:sh, :]))
                did(dve.tensor_tensor(dst[:, sh:NT, :], src[:, sh:NT, :], src[:, 0:NT - sh, :], ALU.add))
                src, dst = dst, cum[1] if dst is cum[0] else cum[0]
            did(dve.tensor_copy(rows_bf[:], src[:, NT - 1, :]))
            dve.wait_ge(s_rkp, 1)
            did(dve.tensor_copy(base[:], pb(1)[:, 0:2 * E]))
            did(dve.tensor_scalar(own_f[:, 0:NT], iota[:, 0:NT], float(P), None, ALU.mult))
            did(dve.tensor_tensor(over[:], base[:, E:2 * E].unsqueeze(2).to_broadcast([P, E, NT]),
                                  own_f[:, 0:NT].unsqueeze(1).to_broadcast([P, E, NT]), ALU.is_gt))
            did(dve.tensor_reduce(nb[0][:], over[:], AX_X, ALU.add))
            did(dve.tensor_copy(start[:], nb[0][:]))
            a_, b_ = nb
            for sh in (1, 2, 4):
                did(dve.tensor_copy(b_[:, 0:sh], a_[:, 0:sh]))
                did(dve.tensor_tensor(b_[:, sh:E], a_[:, sh:E], a_[:, 0:E - sh], ALU.add))
                a_, b_ = b_, a_
            did(dve.tensor_tensor(start[:], a_[:], start[:], ALU.subtract))
            did(dve.tensor_scalar(start[:], start[:], float(P), -1.0, ALU.mult, ALU.add))
            did(dve.tensor_tensor(start[:], start[:], base[:, 0:E], ALU.add))
            did(dve.tensor_tensor(src[:], src[:], over_t(start[:]), ALU.add))
            did(dve.tensor_tensor(src[:], src[:], onehot[:], ALU.mult))
            did(dve.tensor_reduce(slot_f[:], src[:], AX_X, ALU.add))
            did(dve.tensor_tensor(passed[:], iota[:, 0:NBLK].unsqueeze(2).to_broadcast([P, NBLK, E]),
                                  a_[:].unsqueeze(1).to_broadcast([P, NBLK, E]), ALU.is_ge))
            did(dve.tensor_reduce(own_f[:], passed[:], AX_X, ALU.add))
            did(dve.tensor_scalar(own_f[:], own_f[:], float(E - 1), None, ALU.min))
            did(dve.tensor_copy(owner[:], own_f[:]))
            dve.tensor_copy(slot[:], slot_f[:]).then_inc(s_slot, 1)

            def bias1(j, v):
                e = dve.value_load(owner[0:1, bass.ds(j, 1)], min_val=0, max_val=E - 1)
                dve.wait_ge(s_h, j + 1)
                if not isinstance(j, int) or j >= 2:
                    dve.wait_ge(s_hT, j - 1)
                dve.tensor_tensor(hid[v], pb(v), b1_bc[:, bass.ds(e, 1), :].rearrange("p o f -> p (o f)"),
                                  ALU.add).then_inc(s_hc, 1)
                return e

            def bias2(j, g, u, n, v):
                e = dve.value_load(owner[0:1, bass.ds(j, 1)], min_val=0, max_val=E - 1)
                dve.wait_ge(s_yp, j + 1)
                dve.tensor_tensor(yb[v], pb(4 + v)[:, 0:C], b2_bc[:, bass.ds(e, 1), :]
                                  .rearrange("p o f -> p (o f)"), ALU.add).then_inc(s_yb, 1)
                if n == 0:
                    dve.wait_ge(s_xr[u], 16 * (g // 2 + 1))
                    if not isinstance(g, int) or g >= 2:
                        dve.wait_ge(s_yw[u], 16 * GB * (g // 2))
                dve.wait_ge(s_yb, j + 1)
                dve.scalar_tensor_tensor(out=yg[u][:, n, :], in0=yb[v], scalar=xr[u][:, n, C:C + 1],
                                         in1=xr[u][:, n, 0:C], op0=ALU.mult, op1=ALU.add).then_inc(s_yc, 1)

            dve.wait_ge(s_eb, 16)
            bias1(0, 0)
            bias1(1, 1)
            bias2(0, 0, 0, 0, 0)
            for j in range(2, 8):
                bias1(j, j % 2)
                bias2(j - 1, (j - 1) // 4, (j - 1) // 4, (j - 1) % 4, (j - 1) % 2)
            with dve.Fori(1, NG // 2) as i:
                for n in range(8):
                    bias1(8 * i + n, n % 2)
                    if n == 0:
                        bias2(8 * i - 1, 2 * i - 1, 1, 3, 1)
                    else:
                        bias2(8 * i + n - 1, 2 * i + (n - 1) // 4, (n - 1) // 4, (n - 1) % 4, (n - 1) % 2)
            bias2(NBLK - 1, NG - 1, 1, 3, 1)

        @block.tensor
        def _(pe):
            pe.wait_ge(s_cst, 10)
            pe.wait_ge(s_w, 16 * len(weights))
            for i in range(4):
                ins = pe.transpose(pb(7)[0:TC, P * i:P * i + P], ctx_sb[:, i, :], ident[:])
            ins.then_inc(s_ctxT, 1)

            def transposes(c):
                pe.wait_ge(s_xh, c + 1)
                if c >= 2:
                    pe.wait_ge(s_xT, c - 1)
                for i in range(CT):
                    ins = pe.transpose(pb(5 * (c % 2))[:, P * i:P * i + P], xh[:, c % 2, i, :], ident[:])
                ins.then_inc(s_xTp, 1)

            def context_values(i, bank):
                for j in range(4):
                    ins = pe.matmul(pb(bank)[:, C * j:C * j + C],
                                    ctxT2[:, 4 * i + j].rearrange("p u t -> p (u t)"), w_cv, start=True, stop=True)
                ins.then_inc(s_vcps, 1)

            transposes(0)
            for c in range(nchunk):
                pe.wait_ge(s_xT, c + 1)
                for j in range(3):
                    if c:
                        pe.wait_ge(s_full, 3 * (c - 1) + j + 1)
                    pe.matmul(pb(1 + j), w_q[:, j, :], xT[:, c % 2], start=True, stop=True).then_inc(s_pr, 1)
                    if j == 1 and c < nchunk - 1:
                        transposes(c + 1)
                if c:
                    pe.wait_ge(s_v, c)
                for i in range(CT):
                    ins = pe.matmul(pb(4)[:, C * i:C * i + C], xT[:, c % 2, P * i:P * i + P], w_v, start=True, stop=True)
                ins.then_inc(s_pr, 1)
                if c == 0:
                    pe.wait_ge(s_ctxs, 3)
                    pe.matmul(pb(6), w_ck, ctxT[:], start=True, stop=True).then_inc(s_kcps, 1)
                    context_values(0, 7)
                if c == 1:
                    pe.wait_ge(s_kcf, 1)
                    context_values(1, 6)
                    pe.wait_ge(s_bvs, 2)
                    pe.wait_ge(s_wp, 4)
                    pe.wait_ge(s_vc, 1)
                    pe.matmul(pb(7)[:, 0:C], bvs_w[:], w_p, start=True, stop=True).then_inc(s_bmm, 1)

            def pass1(hf, b, half, j):
                hp = 4 * half + j
                g = 4 * hf + j
                ahead = 3 if isinstance(hf, int) and hf < 3 else 1
                at = 2 * (g % 3) if ahead == 3 else 0
                slot = bass.ds(b % RING, 1)
                k2 = K[:, slot, hp].rearrange("p o h t -> p (o h) t")
                q2 = QQ[:, slot, 0, hp].rearrange("p o t -> p (o t)")
                qc2 = QQ[:, slot, 1, hp].rearrange("p o t -> p (o t)")
                kc2 = Kc[:, bass.ds(hp * B + b, 1)].rearrange("p o h t -> p (o h t)")
                mask = causal[:].unsqueeze(1).to_broadcast([P, 2, P])
                b0, b1 = pb(at), pb(at + 1)
                if ahead == 1 or g >= ahead:
                    pe.wait_ge(s_red, 2 * (g - ahead) + 1)
                pe.matmul(b0, q2[:, P:T], k2, start=True, stop=True)
                pe.matmul(b0.rearrange("p (h t) -> p h t", h=2)[:, :, P:T], ident_bf[:], mask, start=False, stop=True,
                          skip_group_check=True).then_inc(s_s, 1)
                if ahead == 1 or g >= ahead:
                    pe.wait_ge(s_red, 2 * (g - ahead) + 2)
                pe.matmul(b1[:, 0:256], q2[:, 0:P], k2[:, :, 0:P], start=True, stop=False)
                pe.matmul(b1[:, 0:256].rearrange("p (h t) -> p h t", h=2), ident_bf[:], mask, start=False, stop=True)
                pe.matmul(b1[:, 256:384], qc2[:, 0:P], kc2, start=True, stop=True)
                pe.matmul(b1[:, 384:512], qc2[:, P:T], kc2, start=True, stop=True).then_inc(s_s, 1)

            def pass2(b, k):
                g = 8 * b + k
                if not isinstance(b, int) or g >= 2:
                    pe.wait_ge(s_exp, g - 1)
                else:
                    pe.wait_ge(s_red, 2 * (10 + g) + 2)
                if k % 4 == 0:
                    pe.wait_ge(s_mr, 16 * (2 * b + k // 4 + 1))
                slot = bass.ds(b % RING, 1)
                k2 = K[:, slot, k].rearrange("p o h t -> p (o h) t")
                q2 = QQ[:, slot, 0, k].rearrange("p o t -> p (o t)")
                qc2 = QQ[:, slot, 1, k].rearrange("p o t -> p (o t)")
                b0, b1 = pb(2 + 2 * (k % 2)), pb(3 + 2 * (k % 2))
                for hh in range(2):
                    pe.matmul(b0[:, T * hh:T * hh + T], k2[:, hh, 0:P], q2, start=True, stop=True)
                    pe.matmul(b1[:, T * hh:T * hh + P], k2[:, hh, P:T], q2[:, P:T], start=True, stop=True)
                pe.matmul(b1.rearrange("p (g q) -> p g q", q=256)[:, :, P:256], Kc[:, bass.ds(k * B + b, 1)].rearrange("p o h t -> p (o h t)"),
                          qc2.rearrange("p (g q) -> p g q", q=P), start=True, stop=True).then_inc(s_stt, 1)

            def pv(hf, half):
                pe.wait_ge(s_sel, 4 * hf + 4)
                pe.wait_ge(s_vz, hf + 1)
                pe.wait_ge(s_vcz, 2 * hf + 2)
                if not isinstance(hf, int) or hf >= 1:
                    pe.wait_ge(s_osb, hf)
                O = pb(6)
                for step in range(5):
                    for q in range(4):
                        rows = slice(32 * q, 32 * q + 32)
                        pr = probs[:, 4 * half + q, :]
                        hh, kb = ((0, 0), (0, 1), (1, 1), (1, 0), (0, 0))[step]
                        if step == 4:
                            ins = pe.matmul(O[rows, 256:512].rearrange("p (g q) -> p g q", q=P), Vcz[:, half, q, :],
                                            pr[:, 512:1024].rearrange("p (g q) -> p g q", q=256)[:, :, P:256],
                                            start=True, stop=True)
                            continue
                        win = slice(16, 48) if hh == 0 else slice(0, 32)
                        lhs = Vz[:, half, kb, 2 * q + hh, win]
                        if kb == 0:
                            pe.matmul(O[rows, 0:T], lhs, pr[:, T * hh:T * hh + T], start=(hh == 0),
                                      stop=(hh == 1))
                        else:
                            pe.matmul(O[rows, P:T], lhs, pr[:, 512 + T * hh:512 + T * hh + P], start=False,
                                      stop=False)
                ins.then_inc(s_pv, 1)

            def max_T(hf):
                pe.wait_ge(s_m, 4 * hf + 4)
                pe.transpose(pb(7)[:, 0:P], M[:], ident[:]).then_inc(s_mt, 1)

            def o_T(hf):
                pe.wait_ge(s_osb, hf + 1)
                for i in range(4):
                    ins = pe.transpose(pb(7)[:, P * i:P * i + P], o_sb[:, P * i:P * i + P], ident[:])
                ins.then_inc(s_ot, 1)

            def y_T(b):
                pe.wait_ge(s_y, 2 * b + 2)
                for i in range(2):
                    ins = pe.transpose(pb(7)[:, P * i:P * i + P], y_sb[:, i, :], ident[:])
                ins.then_inc(s_yt, 1)

            def project(b):
                pe.wait_ge(s_yts, b + 1)
                for i in range(2):
                    ins = pe.matmul(pb(7)[:, C * i:C * i + C], yT[:, P * i:P * i + P], w_p, start=True, stop=True)
                ins.then_inc(s_att, 1)

            def z_T(b):
                pe.wait_ge(s_z, 2 * b + 2)
                for i in range(2):
                    ins = pe.transpose(pb(7)[:, P * i:P * i + P], z[:, i, :], ident[:])
                ins.then_inc(s_zTp, 1)

            def route(b):
                pe.wait_ge(s_zT, b + 1)
                for i in range(2):
                    ins = pe.matmul(pb(7)[:, E * i:E * i + E], zT[:, P * i:P * i + P], w_r, start=True, stop=True)
                ins.then_inc(s_lgp, 1)

            def body(b, prev2, prev, cur, p1a, p1b):
                for k in range(NP):
                    if cur:
                        pass2(b, k)
                    if p1a and k < 4:
                        pass1(2 * b + 3, b + 1, 1, k)
                    if p1b and k >= 4:
                        if k == 4:
                            pe.wait_ge(s_ldq, 16 * NLD * (b + 3))
                            pe.wait_ge(s_pad, 2 * (b + 3))
                        pass1(2 * b + 4, b + 2, 0, k - 4)
                    if prev and k == 0:
                        if prev2:
                            pe.wait_ge(s_x1, b - 1)
                        o_T(2 * b - 2)
                    if prev and k == 1:
                        pv(2 * b - 1, 1)
                    if p1a and k == 1:
                        if prev:
                            pe.wait_ge(s_yn, 2 * b - 1)
                        max_T(2 * b + 2)
                    if prev2 and k == 2:
                        if p1a:
                            pe.wait_ge(s_n2, 2 * b + 3)
                        elif prev:
                            pe.wait_ge(s_yn, 2 * b - 1)
                        else:
                            pe.wait_ge(s_x1, b - 1)
                        z_T(b - 2)
                    if prev and k == 3:
                        if prev2:
                            pe.wait_ge(s_zT, b - 1)
                        elif p1a:
                            pe.wait_ge(s_n2, 2 * b + 3)
                        o_T(2 * b - 1)
                    if prev2 and k == 4:
                        if prev:
                            pe.wait_ge(s_yn, 2 * b)
                        route(b - 2)
                    if cur and k == 5:
                        pv(2 * b, 0)
                    if p1a and k == 5:
                        if prev2:
                            pe.wait_ge(s_lg, b - 1)
                        elif prev:
                            pe.wait_ge(s_yn, 2 * b)
                        else:
                            pe.wait_ge(s_n2, 3)
                        max_T(2 * b + 3)
                    if prev and k == 6:
                        if p1a:
                            pe.wait_ge(s_n2, 2 * b + 4)
                        else:
                            pe.wait_ge(s_lg, b - 1)
                        y_T(b - 1)
                    if prev and k == 7:
                        project(b - 1)

            pe.wait_ge(s_full, 3 * nchunk)
            pe.wait_ge(s_v, nchunk)
            pe.wait_ge(s_vc, 2)
            pe.wait_ge(s_abias, 1)
            pe.wait_ge(s_kcpad, 2)
            for hf in range(3):
                if hf % 2 == 0:
                    pe.wait_ge(s_ldq, 16 * NLD * (hf // 2 + 1))
                    pe.wait_ge(s_pad, 2 * (hf // 2 + 1))
                for j in range(4):
                    pass1(hf, hf // 2, hf % 2, j)
                    if hf and j == 1:
                        if hf == 2:
                            pe.wait_ge(s_n2, 1)
                        max_T(hf - 1)
            pe.wait_ge(s_n2, 2)
            body(0, False, False, True, True, True)
            body(1, False, True, True, True, True)
            with pe.Fori(2, 6) as b:
                body(b, True, True, True, True, True)
            body(6, True, True, True, True, False)
            body(7, True, True, True, False, False)
            body(8, True, True, False, False, False)
            body(9, True, False, False, False, False)

            pe.wait_ge(s_ew, 32)
            pe.wait_ge(s_rt, 18)
            pe.matmul(pb(1)[:, 0:E], before[:], rows_bf[:], start=True, stop=True)
            pe.matmul(pb(1)[:, E:2 * E], ones_bf[:], rows_bf[:], start=True, stop=True).then_inc(s_rkp, 1)

            def group_T(g, u):
                pe.wait_ge(s_xg[u], 16 * (g // 2 + 1))
                if not isinstance(g, int) or g >= 1:
                    pe.wait_ge(s_gTc, g)
                for i in range(GB):
                    ins = pe.transpose(pb(6)[:, P * i:P * i + P], xg[u][:, i, :], ident[:])
                ins.then_inc(s_gT, 1)

            def hidden(j, g, u, n):
                e = pe.value_load(owner[0:1, bass.ds(j, 1)], min_val=0, max_val=E - 1)
                if n == 0:
                    pe.wait_ge(s_gTc, g + 1)
                if not isinstance(j, int) or j >= 2:
                    pe.wait_ge(s_hc, j - 1)
                pe.matmul(pb(n % 2), xnT[u][:, P * n:P * n + P], w1[:, bass.ds(e, 1), :].rearrange("p o f -> p (o f)"),
                          start=True, stop=True).then_inc(s_h, 1)

            def hidden_T(j, v):
                pe.wait_ge(s_hc, j + 1)
                if not isinstance(j, int) or j >= 2:
                    pe.wait_ge(s_hTc, j - 1)
                for k in range(FC):
                    ins = pe.transpose(pb(2 + v)[:, P * k:P * k + P], hid[v][:, P * k:P * k + P], ident[:])
                ins.then_inc(s_hT, 1)

            def outp(j, v):
                e = pe.value_load(owner[0:1, bass.ds(j, 1)], min_val=0, max_val=E - 1)
                pe.wait_ge(s_hTc, j + 1)
                if not isinstance(j, int) or j >= 2:
                    pe.wait_ge(s_yc, j - 1)
                for k in range(FC):
                    ins = pe.matmul(pb(4 + v)[:, 0:C], hidT[v][:, P * k:P * k + P],
                                    w2[:, bass.ds(e, 1), k, :].rearrange("p o c -> p (o c)"),
                                    start=(k == 0), stop=(k == FC - 1))
                ins.then_inc(s_yp, 1)

            def blocks(i, first, last):
                for u in range(2):
                    for n in range(GB):
                        j = 8 * i + GB * u + n
                        hidden(j, 2 * i + u, u, n)
                        if n == 1 and not (last and u == 1):
                            group_T(2 * i + u + 1, 1 - u)
                        if not (first and u == 0 and n < 1):
                            hidden_T(j - 1, (n + 1) % 2)
                        if not (first and u == 0 and n < 2):
                            outp(j - 2, n % 2)

            pe.wait_ge(s_slot, 1)
            group_T(0, 0)
            blocks(0, True, False)
            with pe.Fori(1, NG // 2 - 1) as i:
                blocks(i, False, False)
            blocks(NG // 2 - 1, False, True)
            hidden_T(NBLK - 1, 1)
            outp(NBLK - 2, 0)
            outp(NBLK - 1, 1)


def _by_row(w):
    return w.reshape(-1, NP, 2, D).transpose(0, 3, 2, 1).reshape(-1, C)


def kernel(**inputs):
    import numpy as np
    import concourse.bacc as bacc
    from concourse.bass_utils import run_bass_kernel_spmd as run

    inp = {k: np.ascontiguousarray(v) for k, v in inputs.items()}
    att = lambda n: inp["L0_xattn_" + n]
    ffn = lambda n: inp["L0_ffn_" + n]
    col = lambda v: v.reshape(C, 1)
    rows = np.arange(P)
    own = np.stack([rows % 2 == h for h in range(2)], 1).astype(np.float32)
    ones = np.stack([(rows % 2 == h) & (rows >= SHIFT) & (rows < SHIFT + 2 * NS) for h in range(2)], 1).astype(np.float32)
    arrays = {
        "x": inp["x"].reshape(B * T, C), "ctx": inp["ctx_512"].reshape(B * TC, TC),
        "wpack": np.concatenate([_by_row(att("Wq")), _by_row(att("Wk")), _by_row(att("Wcq")), att("Wv"), att("Wp"),
                                 ffn("Wr")], 1),
        "cpack": np.concatenate([_by_row(att("Wck")), att("Wcv")], 1),
        "cols": np.concatenate([col(_by_row(att("bq"))), col(_by_row(att("bk"))), col(_by_row(att("bcq"))),
                                col(_by_row(att("bck"))), col(att("bv")), col(att("bcv")), col(ffn("ln_g")),
                                col(ffn("ln_b")), own, ones], 1),
        "rpack": np.concatenate([att("bp"), ffn("br"), inp["g_xattn"].reshape(1), inp["g_ffn"].reshape(1)]),
        "bpack": np.concatenate([ffn("b1").reshape(-1), ffn("b2").reshape(-1)]),
        "w1": ffn("W1"), "w2": ffn("W2"),
    }
    arrays = {k: np.ascontiguousarray(v) for k, v in arrays.items()}
    nc = bacc.Bacc("TRN2", target_bir_lowering=False, num_devices=1)
    aps = {k: nc.dram_tensor("in_" + k, v.shape, mybir.dt.from_np(v.dtype), kind="ExternalInput").ap()
           for k, v in arrays.items()}
    out = nc.dram_tensor("out", [B * T, C], F32, kind="ExternalOutput").ap()
    build(nc, aps, out)
    r = run(nc, [{"in_" + k: v for k, v in arrays.items()}], core_ids=[0])
    return r.results[0]["out"].reshape(B, T, C)
```

```python
from contextlib import ExitStack

import concourse.bass as bass
from concourse import mybir

ALU = mybir.AluOpType
ACT = mybir.ActivationFunctionType
AX_X = mybir.AxisListType.X
F32 = mybir.dt.float32
BF16 = mybir.dt.bfloat16
I32 = mybir.dt.int32
U32 = mybir.dt.uint32

P = 128
B = 8
T = 256
TC = 64
C = 128
H = 16
D = C // H
NP = H // 2
NT = B * T // P
E = 8
F = 512
FC = F // P
SCALE = float(D) ** -0.5
EPS = 1e-5
NEG = -1e30

R = 2 * D
NS = 2
SHIFT = 3 * R
QROWS, KROWS = 4 * R, 3 * R
QRUNS = [(0, 0, 4 * R), (4 * R, 0, 2 * R), (6 * R, 0, R)]
KRUNS = [(0, 0, 3 * R), (4 * R, R, 2 * R), (6 * R, 2 * R, R)]
XW = 2 * C + 2
DEAD = 1 << 20
RING = 3
VW = 48
NBLK = NT + E - 1
STRIDE = B * T + P
NSLOT = E * STRIDE + P
U = 6
PARTS = ((0, 1), (2, 3, 4))
NRT = 16


def build(nc, a, out):
    nchunk = 4
    CT = 4
    with ExitStack() as ctx:
        def sb(name, shape, dt=F32):
            return ctx.enter_context(nc.sbuf_tensor(name, shape, dt))

        def sem(name):
            return ctx.enter_context(nc.semaphore(name))

        def buf(b):
            return int(isinstance(b, int) and b == B - 2)

        def dram(name, shape, dt):
            return nc.dram_tensor(name, shape, dt, kind="Internal").ap()

        ps_all = ctx.enter_context(nc.psum_tensor("ps_all", [P, 8 * 512], F32))

        def pb(i, n=1):
            return ps_all[:, 512 * i:512 * (i + n)]

        q_scr = dram("q_scr", [B, 2, QROWS, NP * T], BF16)
        k_scr = dram("k_scr", [B, KROWS, NP * T], BF16)
        kc_scr = dram("kc_scr", [KROWS, NP * B * TC], BF16)
        m_scr = dram("m_scr", [2 * B, NS, 32, P], BF16)
        xs_scr = dram("xs_scr", [NSLOT, XW], F32)

        x_sb = sb("x_sb", [P, NT, C])
        rcd = sb("rcd", [P, 2, 2, XW])
        v_all = sb("v_all", [P, NT, C])
        vc_all = sb("vc_all", [P, B, C])
        K = sb("K", [P, RING, NP, 2, T], BF16)
        K0 = sb("K0", [P, NP * T], BF16)
        QQ = sb("QQ", [P, RING, 2, NP, T], BF16)
        Kc = sb("Kc", [P, NP * B, 2, TC], BF16)
        probs = sb("probs", [P, NP, 1024])
        Vz = sb("Vz", [P, 2, 2, H // 2, VW])
        Vcz = sb("Vcz", [P, 2, NP // 2, 32])
        ident = sb("ident", [P, P])
        ident_bf = sb("ident_bf", [P, P], BF16)
        causal = sb("causal", [P, P], BF16)
        before = sb("before", [P, P], BF16)
        ones_bf = sb("ones_bf", [P, P], BF16)
        half_neg = sb("half_neg", [P, 2 * NT])
        eps2 = sb("eps2", [P, 2])
        wpack = sb("wpack", [P, 5 * C + E])
        w_q = wpack[:, 0:3 * C].rearrange("p (j c) -> p j c", j=3)
        w_v = wpack[:, 3 * C:4 * C]
        w_p = wpack[:, 4 * C:5 * C]
        w_r = wpack[:, 5 * C:5 * C + E]
        cpack = sb("cpack", [TC, 2 * C])
        w_ck, w_cv = cpack[:, 0:C], cpack[:, C:2 * C]
        cols = sb("cols", [P, 12 + E * FC])
        b_col = cols[:, 0:4]
        bv_col = cols[:, 4:6]
        ln_g, ln_b = cols[:, 6:7], cols[:, 7:8]
        own_rows = cols[:, 8:10]
        one_rows = cols[:, 10:12]
        b1_col = cols[:, 12:12 + E * FC].rearrange("p (e k) -> p e k", e=E)
        rpack = sb("rpack", [P, C + E + 2])
        bp_bc = rpack[:, 0:C]
        br_bc = rpack[:, C:C + E]
        gate_x = rpack[:, C + E:C + E + 2]
        bvs = sb("bvs", [P, 1])
        bvs_w = sb("bvs_w", [P, P])
        att_bias = sb("att_bias", [P, C])
        tanh_g = sb("tanh_g", [P, 2])
        ctx_sb = sb("ctx_sb", [P, 4, TC])
        ctxT = sb("ctxT", [TC, B * TC])
        ctxT2 = sb("ctxT2", [TC, B, 2, TC])
        st6 = sb("st6", [P, NT, 6])
        mv = sb("mv", [P, NT, 2])
        rstd = sb("rstd", [P, NT])
        xh = sb("xh", [P, 2, CT, C])
        xT = sb("xT", [P, 2, CT * P])
        flat = probs[:].rearrange("p n q -> p (n q)")
        w12 = sb("w12", [P, E * F + E * FC * C])
        full = w12[:, 0:1536].rearrange("p (j t) -> p j t", j=3)
        rest = w12[:, 1536:3072].rearrange("p (j t) -> p j t", j=3)
        piece = [w12[:, 3072 + 2304 * i:5376 + 2304 * i].bitcast(BF16).rearrange("p (j i t) -> p j i t", j=3, i=3)
                 for i in range(2)]
        kflat = K[:].rearrange("p r n h t -> p (r n h t)").bitcast(F32)
        cfull = kflat[:, 2048:2560]
        cpiece = kflat[:, 2560:3328].bitcast(BF16).rearrange("p (i t) -> p i t", i=3)
        zrows = kflat[:, 0:NP * T // 2].bitcast(BF16)
        Kc0 = kflat[:, 4096:6144].bitcast(BF16)
        top = sb("top", [P, NP // 2, 16])
        M = sb("M", [P, P])
        shift = sb("shift", [32, NS, P], BF16)
        o_sb = sb("o_sb", [P, 512])
        rec = sb("rec", [P, 32])
        yn = sb("yn", [P, 2, 2, 64])
        y_sb = sb("y_sb", [P, 2, C])
        yT = sb("yT", [P, T])
        xb = sb("xb", [P, 2, C])

        w1 = w12[:, 0:E * F].rearrange("p (e f) -> p e f", e=E)
        w2 = w12[:, E * F:].rearrange("p (e k c) -> p e k c", e=E, k=FC)
        b2_bc = kflat[:, 0:E * C].rearrange("p (e c) -> p e c", e=E)
        zrow = sb("zrow", [P, XW])
        iota_i = sb("iota_i", [P, 32], I32)
        iota = sb("iota", [P, 32])
        st6z = sb("st6z", [P, 2, 6])
        mvz = sb("mvz", [P, 2, 2])
        rs = sb("rs", [P, 4, 2])
        z = sb("z", [P, 2, C])
        zT = sb("zT", [P, T])
        logit = sb("logit", [P, 2, E])
        top1 = sb("top1", [P, 2])
        last = sb("last", [P, 2])
        work = sb("work", [P, 2, E])
        ties = sb("ties", [P, 2, E])
        onehot = sb("onehot", [P, 2, E], BF16)
        gate = sb("gate", [P, 2])
        desc = sb("desc", [P, E])
        tok_i = sb("tok_i", [P, 2], I32)
        tok = sb("tok", [P, 2])
        region_i = sb("region_i", [P, E], I32)
        region = sb("region", [P, E])
        fill = sb("fill", [P, E])
        fill_i = sb("fill_i", [P, E], I32)
        pos = sb("pos", [P, 2, E])
        slot_f = sb("slot_f", [P, 2])
        slot = sb("slot", [P, 2, 2], I32)
        count = sb("count", [P, E])
        iota_p = sb("iota_p", [P, 32])
        over = sb("over", [P, E, NT])
        nblk = sb("nblk", [P, E])
        nb = [sb("nb_a", [P, E]), sb("nb_b", [P, E])]
        jump = sb("jump", [P, E])
        passed = sb("passed", [P, NBLK, E])
        own_f = sb("own_f", [P, NBLK])
        owner = sb("owner", [P, NBLK], I32)
        row_f = sb("row_f", [P, NBLK])
        row_i = sb("row_i", [P, NBLK], I32)
        at = [0]

        def part(width, n):
            found = [flat[:, at[0] + width * i:at[0] + width * i + width] for i in range(n)]
            at[0] += width * n
            return found

        w1s = [K0[:, 2 * F * i:2 * F * i + 2 * F].bitcast(F32) for i in range(2)]
        xnT = part(P, 2)
        hid = part(F, 2)
        hidT = part(F, 2)
        yb = part(C, 2)
        yg = part(C + 1, U)
        rx = part(XW, U)

        s_stand_sp = sem("sp_wait_stands_alone")
        s_stand_pool = sem("pool_wait_stands_alone")
        s_stand_act = sem("act_wait_stands_alone")
        s_stand_dve = sem("dve_wait_stands_alone")
        s_w = sem("weights_loaded")
        s_x = [sem(f"x_loaded_{c}") for c in range(4)]
        s_cst = sem("constants_made")
        s_zero = sem("operands_zeroed")
        s_init = sem("scratch_rows_written")
        s_tanh = sem("tanh_done")
        s_wp = sem("wp_scaled")
        s_bvs = sem("value_bias_summed")
        s_bmm = sem("bias_product_done")
        s_abias = sem("attention_bias_done")
        s_ctxT = sem("context_transposed")
        s_ctxs = sem("context_copied")
        s_kcps = sem("context_keys_projected")
        s_kcf = sem("context_keys_full")
        s_kcp = sem("context_pieces_step")
        s_kcw = sem("context_pieces_written")
        s_kcl = sem("context_keys_loaded")
        s_vcps = sem("context_values_projected")
        s_vc = sem("context_values_copied")
        s_st = sem("stats_step")
        s_rstd = sem("rstd_done")
        s_xh = sem("xhat_done")
        s_xTp = sem("xhat_transposed")
        s_xT = sem("xT_copied")
        s_pr = sem("projections_done")
        s_full = sem("projections_copied")
        s_v = sem("values_copied")
        s_pw = [sem(f"pieces_written_{c}") for c in range(4)]
        s_p2 = sem("rest_done")
        s_p2b = sem("second_piece_done")
        s_p3 = sem("third_piece_done")
        s_kcpad = sem("context_keys_padded")

        s_ldq = sem("queries_loaded")
        s_ldk = sem("keys_loaded")
        s_pad = sem("keys_padded")
        s_s = sem("scores_ready")
        s_red = sem("scores_reduced")
        s_m = sem("maxima_step")
        s_mt = sem("maxima_transposed")
        s_n1 = sem("shift1_done")
        s_n2 = sem("shift2_done")
        s_mw = sem("shift_written")
        s_mr = sem("shift_rows_loaded")
        s_stt = sem("scoresT_ready")
        s_exp = sem("exp_done")
        s_sel = sem("probs_masked")
        s_pv = sem("pv_done")
        s_osb = sem("o_copied")
        s_ot = sem("o_transposed")
        s_rec = sem("reciprocal_done")
        s_yn = sem("heads_normalised")
        s_y = sem("y_summed")
        s_yt = sem("y_transposed")
        s_yts = sem("yT_copied")
        s_xb = sem("x_plus_bias")
        s_att = sem("attention_projected")
        s_x1 = sem("x1_done")
        s_ew = sem("expert_weights_loaded")
        s_eb = sem("expert_biases_loaded")
        s_xsz = sem("slots_zeroed")
        s_io = sem("iota_made")
        s_zst = sem("ffn_stats_step")
        s_zr = sem("ffn_rstd_step")
        s_z = sem("z_done")
        s_zTp = sem("z_transposed")
        s_zT = sem("zT_copied")
        s_lgp = sem("logits_projected")
        s_lg = sem("logits_done")
        s_xn = sem("expert_input_done")
        s_rt = sem("routing_step")
        s_ge = sem("gate_exp_done")
        s_rkp = sem("ranks_counted")
        s_slot = sem("slots_done")
        s_sc = [sem("tokens_scattered"), sem("tokens_scattered_b")]
        s_xc = sem("x1_copied_to_records")
        s_pre = sem("routing_constants_made")
        s_dead = sem("dead_slots_written")
        s_rx = [sem(f"block_loaded_{i}") for i in range(U)]
        s_gT = sem("block_transposed")
        s_gTc = sem("block_copied")
        s_h = sem("hidden_projected")
        s_hc = sem("hidden_biased")
        s_wc = sem("expert_weights_copied")
        s_hTc = sem("hidden_activated")
        s_yp = sem("expert_output_projected")
        s_yc = sem("expert_output_biased")
        s_yw = [sem(f"output_written_{i}") for i in range(U)]
        s_yb = sem("expert_output_biased_b")

        def score_banks(hf, j):
            if isinstance(hf, int) and hf < 3:
                g = 4 * hf + j
                if g < 4:
                    return ((6, 7), (0, 5))[g % 2], g - 2 if g >= 2 else None
                return ((2, 3), (4, 5), (0, 1))[g % 3], 3 if g < 7 else g - 3
            return (0, 1), 4 * hf + j - 1

        block = ctx.enter_context(nc.Block())
        weights = [(wpack[:], a["wpack"]), (cpack[:], a["cpack"]), (cols[:], a["cols"]),
                   (rpack[:], a["rpack"].partition_broadcast(P)),
                   (ctx_sb[:], a["ctx"].rearrange("(t p) c -> p t c", p=P))]
        NLD = 3

        def dead_slots(eng, experts):
            eng.wait_ge(s_slot, 1)
            for e in experts:
                row = eng.value_load(fill_i[0:1, e:e + 1], min_val=0, max_val=E * STRIDE)
                eng.dma_start(xs_scr[bass.ds(row, P)], zrow[:]).then_inc(s_dead, 16)

        @block.sync
        def _(sp):
            for c in range(nchunk):
                sp.dma_start(x_sb[:, CT * c:CT * c + CT, :],
                             a["x"][CT * P * c:CT * P * (c + 1)].rearrange("(t p) c -> p t c", p=P)).then_inc(s_x[c], 16)
                if c == 0:
                    for dst, src in weights:
                        sp.dma_start(dst, src).then_inc(s_w, 16)
            sp.wait_ge(s_zero, 1)
            for ty in range(2):
                sp.dma_start(q_scr[:, ty, SHIFT:QROWS, :].rearrange("b r t -> r b t"),
                             zrows[0:R].unsqueeze(1).to_broadcast([R, B, NP * T])).then_inc(s_init, 16)

            def write_context_keys():
                sp.wait_ge(s_kcp, 4)
                sp.dma_start(kc_scr.rearrange("(i r) (n t) -> (r n) i t", i=3, n=NP), cpiece).then_inc(s_kcw, 16)

            def load_context_keys():
                sp.wait_ge(s_kcw, 16)
                for run in KRUNS:
                    sp.dma_start(Kc0[run[0]:run[0] + run[2]], kc_scr[run[1]:run[1] + run[2]]).then_inc(s_kcl, 16)

            def write_pieces(c):
                for j in range(3):
                    sp.wait_ge(s_p3, 3 * c + j + 1)
                    for bb in range(2):
                        b = 2 * c + bb
                        dst = k_scr[b] if j == 1 else q_scr[b, j // 2, 0:SHIFT]
                        sp.dma_start(dst.rearrange("(i r) (n t) -> (r n) i t", i=3, n=NP),
                                     piece[c % 2][:, j, :, bb * T:(bb + 1) * T]).then_inc(s_pw[c], 16)

            def load(b):
                if not isinstance(b, int) or b >= 1:
                    sp.wait_ge(s_ldq, 16 * NLD * b)
                    sp.sem_inc(s_stand_sp, 1)
                    sp.wait_ge(s_ldk, 16 * NLD * b)
                    sp.sem_inc(s_stand_sp, 1)
                if not isinstance(b, int) or b >= 1:
                    sp.wait_ge(s_pad, 2 * b)
                    sp.sem_inc(s_stand_sp, 1)
                for run in KRUNS:
                    sp.dma_start(K0[run[0]:run[0] + run[2], :],
                                 k_scr[bass.ds(b, 1), run[1]:run[1] + run[2]].rearrange("o r t -> r (o t)")
                                 ).then_inc(s_ldk, 16)
                for run in QRUNS:
                    sp.dma_start(QQ[run[0]:run[0] + run[2], bass.ds(b % RING, 1)].rearrange("r o y n t -> r (o y) (n t)"),
                                 q_scr[bass.ds(b, 1), :, run[1]:run[1] + run[2], :]
                                 .rearrange("o y r t -> r (o y) t")).then_inc(s_ldq, 16)

            def shifts(hf, b, half):
                sp.wait_ge(s_n2, hf + 1)
                sp.sem_inc(s_stand_sp, 1)
                sp.dma_start(m_scr[bass.ds(hf, 1)].rearrange("o i r q -> r (o i) q"), shift[:]).then_inc(s_mw, 16)
                sp.wait_ge(s_mw, 16 * (hf + 1))
                sp.sem_inc(s_stand_sp, 1)
                sp.dma_start(QQ[SHIFT:SHIFT + 2 * NS, bass.ds(b % RING, 1), :, 4 * half:4 * half + 4, :]
                             .rearrange("i o y n t -> i (o y) (n t)"),
                             m_scr[bass.ds(hf, 1)].rearrange("o i (h y r) q -> (o i h) y (r q)", h=2, y=2)
                             ).then_inc(s_mr, 16)
                sp.wait_ge(s_mr, 16 * (hf + 1))
                sp.sem_inc(s_stand_sp, 1)

            write_pieces(0)
            write_context_keys()
            sp.wait_ge(s_init, 32)
            sp.wait_ge(s_zero, 4)
            sp.wait_ge(s_pw[0], 16 * 6)
            load(0)
            load_context_keys()
            write_pieces(1)
            write_pieces(2)
            sp.wait_ge(s_zero, 12)
            load(1)
            for c in range(1, nchunk - 1):
                sp.wait_ge(s_pw[c], 16 * 6)
            load(2)
            shifts(0, 0, 0)
            write_pieces(3)
            shifts(1, 0, 1)
            sp.wait_ge(s_pw[3], 16 * 6)
            sp.wait_ge(s_io, 4)
            sp.dma_start(xs_scr[E * STRIDE:NSLOT], zrow[:]).then_inc(s_xsz, 16)

            def body(b, ld, m0, m1):
                if ld:
                    sp.wait_ge(s_stt, 8 * b)
                    sp.sem_inc(s_stand_sp, 1)
                    load(b + 2)
                if m0:
                    shifts(2 * b + 2, b + 1, 0)
                if m1:
                    shifts(2 * b + 3, b + 1, 1)

            body(0, False, True, True)
            with sp.Fori(1, 6) as b:
                body(b, True, True, True)
            body(6, False, True, True)
            for dst, src in ((w1, a["w1"].rearrange("e p f -> p e f")),
                             (w2, a["w2"].rearrange("e (k p) c -> p e k c", p=P))):
                sp.dma_start(dst, src).then_inc(s_ew, 16)
            sp.wait_ge(s_stt, 8 * B)
            sp.dma_start(kflat[:, 0:E * C], a["b2"].partition_broadcast(P)).then_inc(s_eb, 16)

            dead_slots(sp, range(E // 2))

            def load_block(j, v):
                if not isinstance(j, int) or j >= U:
                    sp.wait_ge(s_yc, 2 * (j - U) + 2)
                    sp.sem_inc(s_stand_sp, 1)
                row = sp.value_load(row_i[0:1, bass.ds(j, 1)], min_val=0, max_val=E * STRIDE)
                sp.dma_start(rx[v], xs_scr[bass.ds(row, P)]).then_inc(s_rx[v], 16)

            sp.wait_ge(s_slot, 2)
            sp.wait_ge(s_sc[0], 32 * (B - 1))
            sp.wait_ge(s_sc[1], 32)
            sp.wait_ge(s_dead, 16 * E)
            sp.wait_ge(s_xsz, 16)
            for n in range(U):
                load_block(n, n)
            with sp.Fori(1, NBLK // U) as i:
                for n in range(U):
                    load_block(U * i + n, n)
            for j in range(NBLK - NBLK % U, NBLK):
                load_block(j, j % U)

        @block.gpsimd
        def _(pool):
            pool.memset(ident[:], 0.0).then_inc(s_cst, 1)
            pool.memset(causal[:], 0.0).then_inc(s_cst, 1)
            pool.memset(before[:], 1.0).then_inc(s_cst, 1)
            pool.memset(half_neg[:], -0.5).then_inc(s_cst, 1)
            pool.memset(ones_bf[:], 1.0).then_inc(s_cst, 1)
            pool.memset(eps2[:], EPS).then_inc(s_cst, 1)
            pool.wait_ge(s_cst, 6)
            pool.affine_select(out=ident[:], in_=ident[:], compare_op=ALU.not_equal, fill=1.0, base=0,
                               pattern=[[-1, P]], channel_multiplier=1).then_inc(s_cst, 1)
            pool.affine_select(out=causal[:], in_=causal[:], compare_op=ALU.is_ge, fill=NEG, base=0,
                               pattern=[[-1, P]], channel_multiplier=1).then_inc(s_cst, 1)
            pool.affine_select(out=before[:], in_=before[:], compare_op=ALU.is_gt, fill=0.0, base=0,
                               pattern=[[1, P]], channel_multiplier=-1).then_inc(s_cst, 1)
            pool.wait_ge(s_cst, 9)
            pool.tensor_copy(ident_bf[:], ident[:]).then_inc(s_cst, 1)
            def qq0(i):
                return QQ[:, i].rearrange("p y n t -> p (y n t)").bitcast(F32)

            def rstd_of(c):
                sl = slice(CT * c, CT * c + CT)
                pool.wait_ge(s_st, 3 * (c + 1))
                pool.tensor_tensor(rstd[:, sl], rstd[:, sl], half_neg[:, 0:CT], ALU.pow).then_inc(s_rstd, 1)

            rstd_of(0)
            for c in range(nchunk):
                if c == 0:
                    pool.memset(kflat[:, 0:NP * T // 2], 0.0).then_inc(s_zero, 1)
                    rstd_of(1)
                    pool.memset(Kc0.bitcast(F32), 0.0).then_inc(s_zero, 1)
                    rstd_of(2)
                    rstd_of(3)
                    pool.memset(qq0(0), 0.0).then_inc(s_zero, 1)
                    pool.memset(K0[:].bitcast(F32), 0.0).then_inc(s_zero, 1)
                for j in range(3):
                    last = 0 if j == 1 else 2
                    pool.wait_ge(s_p2b, 3 * c + j + 1)
                    if j == 0 and c >= 2:
                        pool.wait_ge(s_pw[c - 2], 16 * 6)
                    pool.tensor_tensor(piece[c % 2][:, j, last, :], rest[:, j, :], piece[c % 2][:, j, 1, :],
                                       ALU.subtract).then_inc(s_p3, 1)
                if c == 0:
                    pool.memset(M[:], 0.0).then_inc(s_zero, 1)
                    pool.memset(Vz[:], 0.0).then_inc(s_zero, 1)
                    pool.memset(Vcz[:], 0.0).then_inc(s_zero, 1)
                    pool.wait_ge(s_zero, 7)
                    pool.memset(Vz[:, :, :, :, 24:25], 1.0).then_inc(s_zero, 1)
                    pool.memset(Vcz[0:64, :, :, 8:9], 1.0).then_inc(s_zero, 1)
                    pool.wait_ge(s_zero, 9)
                    pool.memset(Vcz[64:128, :, :, 24:25], 1.0).then_inc(s_zero, 1)
                    pool.wait_ge(s_zero, 10)
                    pool.memset(qq0(1), 0.0).then_inc(s_zero, 1)
                    pool.memset(qq0(2), 0.0).then_inc(s_zero, 1)
                if c == 1:
                    pool.iota(iota_i[:], pattern=[[1, 32]], base=0, channel_multiplier=0).then_inc(s_io, 1)
                    pool.iota(tok_i[:], pattern=[[P, 2]], base=0, channel_multiplier=1).then_inc(s_io, 1)
                    pool.memset(zrow[:], 0.0).then_inc(s_io, 1)
                    pool.wait_ge(s_io, 3)
                    pool.memset(zrow[:, XW - 1:XW].bitcast(I32), DEAD).then_inc(s_io, 1)
                    pool.iota(region_i[:], pattern=[[STRIDE, E]], base=0, channel_multiplier=0).then_inc(s_io, 1)
                    pool.tensor_copy(iota[:], iota_i[:]).then_inc(s_io, 1)

            def v_blocks(hf, b, half):
                if not isinstance(hf, int) or hf >= 2:
                    pool.wait_ge(s_pv, hf - 1)
                    pool.sem_inc(s_stand_pool, 1)
                pool.tensor_copy(Vz[:, half, :, :, 16:24],
                                 v_all[:, bass.ds(2 * b, 2), 64 * half:64 * half + 64]
                                 .rearrange("p k (h d) -> p k h d", d=D))

            def select(b, k):
                pool.wait_ge(s_exp, 8 * b + k + 1)
                pool.sem_inc(s_stand_pool, 1)
                v = probs[:, k, :].rearrange("p (g q) -> p g q", q=256)[:, :, 0:128]
                pool.affine_select(out=v, in_=v, compare_op=ALU.is_ge, fill=0.0, base=0,
                                   pattern=[[0, 4], [1, P]], channel_multiplier=-1).then_inc(s_sel, 1)

            def y_sum(hf, half):
                pool.wait_ge(s_yn, hf + 1)
                if half == 0 and (not isinstance(hf, int) or hf >= 2):
                    pool.wait_ge(s_yt, hf // 2)
                pool.tensor_tensor(y_sb[:, :, 64 * half:64 * half + 64], yn[:, 0], yn[:, 1], ALU.add).then_inc(s_y, 1)

            def ffn_norm(b):
                n0 = 5 * b
                pool.wait_ge(s_zst, 3 * b + 3)
                pool.tensor_tensor(rs[:, 0, :], rs[:, 0, :], half_neg[:, 0:2], ALU.pow).then_inc(s_zr, 1)
                pool.wait_ge(s_zr, n0 + 1)
                if not isinstance(b, int) or b >= 1:
                    pool.wait_ge(s_xn, 2 * b)
                pool.tensor_tensor(rs[:, 1, :], mvz[:, :, 1], rs[:, 0, :], ALU.mult).then_inc(s_zr, 1)
                pool.wait_ge(s_zr, n0 + 2)
                pool.tensor_tensor(rs[:, 1, :], rs[:, 1, :], rs[:, 0, :], ALU.mult).then_inc(s_zr, 1)
                pool.wait_ge(s_zr, n0 + 3)
                pool.tensor_tensor(rs[:, 1, :], rs[:, 1, :], eps2[:], ALU.add).then_inc(s_zr, 1)
                pool.wait_ge(s_zr, n0 + 4)
                pool.tensor_tensor(rs[:, 1, :], rs[:, 1, :], half_neg[:, 0:2], ALU.pow).then_inc(s_zr, 1)

            def record(b):
                pool.wait_ge(s_xn, 2 * b + 2)
                pool.sem_inc(s_stand_pool, 1)
                pool.tensor_copy(rcd[:, buf(b), :, C:2 * C], x_sb[:, bass.ds(2 * b, 2), :]).then_inc(s_xc, 1)

            def scatter(b):
                pool.wait_ge(s_xc, b + 1)
                pool.sem_inc(s_stand_pool, 1)
                pool.wait_ge(s_rt, NRT * b + NRT)
                pool.sem_inc(s_stand_pool, 1)
                for t in range(2):
                    pool.indirect_dma_start(out=xs_scr, out_offset=bass.IndirectOffsetOnAxis(
                        ap=slot[:, buf(b), t:t + 1].bitcast(U32), axis=0), in_=rcd[:, buf(b), t, :], in_offset=None
                        ).then_inc(s_sc[buf(b)], 16)

            def body(b, prev3, prev2, prev, cur):
                for k in range(NP):
                    if prev3 and k == 2:
                        record(b - 3)
                    if prev3 and k == 4:
                        scatter(b - 3)
                    if cur:
                        if k == 0:
                            v_blocks(2 * b, b, 0)
                        if k == 4:
                            v_blocks(2 * b + 1, b, 1)
                        select(b, k)
                    if prev and k == 0:
                        y_sum(2 * b - 2, 0)
                    if prev2 and k == 1:
                        ffn_norm(b - 2)
                    if prev:
                        if k == 3:
                            y_sum(2 * b - 1, 1)
                        if k == 4:
                            if not isinstance(b, int) or b >= 2:
                                pool.wait_ge(s_x1, b - 1)
                            pool.sem_inc(s_stand_pool, 1)
                            pool.tensor_tensor(
                                xb[:], x_sb[:, bass.ds(2 * b - 2, 2), :],
                                att_bias[:].unsqueeze(1).to_broadcast([P, 2, C]), ALU.add).then_inc(s_xb, 1)

            pool.wait_ge(s_zero, 10)
            pool.wait_ge(s_v, nchunk)
            pool.wait_ge(s_vc, 2)
            body(0, False, False, False, True)
            pool.wait_ge(s_abias, 1)
            body(1, False, False, True, True)
            body(2, False, True, True, True)
            with pool.Fori(3, B) as b:
                body(b, True, True, True, True)
            body(B, True, True, True, False)
            body(B + 1, True, True, False, False)
            body(B + 2, True, False, False, False)

            def write_out(j, v):
                pool.wait_ge(s_yc, 2 * j + 2)
                pool.sem_inc(s_stand_pool, 1)
                pool.indirect_dma_start(out=out, out_offset=bass.IndirectOffsetOnAxis(
                    ap=yg[v][:, C:C + 1].bitcast(U32), axis=0), in_=yg[v][:, 0:C], in_offset=None,
                    bounds_check=B * T - 1, oob_is_err=False).then_inc(s_yw[v], 16)

            with pool.Fori(0, NBLK // U) as i:
                for n in range(U):
                    write_out(U * i + n, n)
            for j in range(NBLK - NBLK % U, NBLK):
                write_out(j, j % U)
            for v in range(U):
                pool.wait_ge(s_yw[v], 16 * len(range(v, NBLK, U)))

        @block.scalar
        def _(act):
            act.wait_ge(s_w, 16 * len(weights))
            act.activation(tanh_g[:], gate_x, ACT.Tanh).then_inc(s_tanh, 1)
            act.wait_ge(s_ctxT, 1)
            for i in range(2):
                act.copy(ctxT2[:, :, i, :], pb(7)[0:TC, :].rearrange("p (b t) -> p b t", b=B)).then_inc(s_ctxs, 1)
            act.copy(ctxT[:], pb(7)[0:TC, :]).then_inc(s_ctxs, 1)

            def xT_copy(c):
                act.wait_ge(s_xTp, c + 1)
                if c >= 2:
                    act.wait_ge(s_pr, 4 * (c - 1))
                act.copy(xT[:, c % 2], pb(5 * (c % 2))).then_inc(s_xT, 1)

            xT_copy(0)
            act.wait_ge(s_wp, 2)
            for c in range(nchunk):
                if c >= 2:
                    act.wait_ge(s_pw[c - 2], 16 * 6)
                for j in range(3):
                    first, scale = (2, 1.0) if j == 1 else (0, SCALE)
                    act.wait_ge(s_pr, 4 * c + j + 1)
                    act.activation(piece[c % 2][:, j, first, :], pb(1 + j), ACT.Identity, bias=b_col[:, j:j + 1],
                                   scale=scale)
                    if c:
                        act.wait_ge(s_p2, 3 * (c - 1) + j + 1)
                    act.activation(full[:, j, :], pb(1 + j), ACT.Identity, bias=b_col[:, j:j + 1],
                                   scale=scale).then_inc(s_full, 1)
                    if j == 1 and c < nchunk - 1:
                        xT_copy(c + 1)
                act.wait_ge(s_pr, 4 * c + 4)
                act.copy(v_all[:, CT * c:CT * c + CT, :],
                         pb(4).rearrange("p (t c) -> p t c", t=CT)).then_inc(s_v, 1)
                if c == 0:
                    act.wait_ge(s_kcps, 1)
                    act.activation(cfull, pb(6), ACT.Identity, bias=b_col[:, 3:4]).then_inc(s_kcf, 1)

            def exp(b, k):
                act.wait_ge(s_stt, 8 * b + k + 1)
                if not isinstance(b, int) or b >= 1:
                    act.wait_ge(s_pv, 2 * b - 1 + k // 4)
                act.activation(probs[:, k, :], pb(2 + 2 * (k % 2), 2), ACT.Exp).then_inc(s_exp, 1)

            def vc_blocks(hf, b, half):
                if not isinstance(hf, int) or hf >= 2:
                    act.wait_ge(s_pv, hf - 1)
                for hh in range(2):
                    pr = slice(64 * hh, 64 * hh + 64)
                    act.copy(
                        Vcz[pr, half, :, 16 * hh:16 * hh + 8],
                        vc_all[pr, bass.ds(b, 1), 64 * half:64 * half + 64]
                        .rearrange("p o (n s d) -> p (o n) s d", s=2, d=D)[:, :, hh, :])

            def shift1(hf):
                act.wait_ge(s_mt, hf + 1)
                if not isinstance(hf, int) or hf >= 1:
                    act.wait_ge(s_mw, 16 * hf)
                act.activation(shift[:, 0, :], pb(7)[0:32, 0:P], ACT.Copy, scale=-1.0).then_inc(s_n1, 1)

            def o_copy(hf):
                act.wait_ge(s_pv, hf + 1)
                if not isinstance(hf, int) or hf >= 1:
                    act.wait_ge(s_ot, hf)
                act.copy(o_sb[:], pb(6)).then_inc(s_osb, 1)

            def yT_copy(b):
                act.wait_ge(s_yt, b + 1)
                act.copy(yT[:], pb(7)[:, 0:T]).then_inc(s_yts, 1)

            def zT_copy(b):
                act.wait_ge(s_zTp, b + 1)
                act.copy(zT[:], pb(7)[:, 0:T]).then_inc(s_zT, 1)

            def body(b, prev2, prev, cur, m):
                for k in range(NP):
                    if cur:
                        if k == 2:
                            vc_blocks(2 * b, b, 0)
                        if k == 6:
                            vc_blocks(2 * b + 1, b, 1)
                        exp(b, k)
                    if prev and k == 2:
                        o_copy(2 * b - 1)
                    if m and k == 1:
                        shift1(2 * b + 2)
                    if prev2 and k == 2:
                        zT_copy(b - 2)
                    if prev2 and k == 6:
                        gate_exp(b - 2)
                    if m and k == 5:
                        shift1(2 * b + 3)
                    if cur and k == 6:
                        o_copy(2 * b)
                    if prev and k == 6:
                        yT_copy(b - 1)
                    if prev2 and k == 7:
                        xn_norm(b - 2)

            def xn_norm(b):
                act.wait_ge(s_zr, 5 * b + 5)
                if isinstance(b, int) and b == B - 1:
                    act.wait_ge(s_sc[0], 32 * (b - 1))
                elif not isinstance(b, int) or 1 <= b < B - 2:
                    act.wait_ge(s_sc[0], 32 * b)
                for i in range(2):
                    act.activation(rcd[:, buf(b), i, 0:C], z[:, i, :],
                                   ACT.Copy, scale=rs[:, 1, i:i + 1]).then_inc(s_xn, 1)

            def gate_exp(b):
                act.wait_ge(s_rt, NRT * b + 2)
                act.activation(work[:], work[:], ACT.Exp).then_inc(s_ge, 1)

            act.wait_ge(s_zero, 10)
            act.wait_ge(s_vc, 2)
            shift1(0)
            shift1(1)
            body(0, False, False, True, True)
            body(1, False, True, True, True)
            body(2, True, True, True, True)
            with act.Fori(3, 7) as b:
                body(b, True, True, True, True)
            body(7, True, True, True, False)
            body(8, True, True, False, False)
            body(9, True, False, False, False)

            dead_slots(act, range(E // 2, E))

            def block_T(j, v):
                act.wait_ge(s_gT, j + 1)
                if not isinstance(j, int) or j >= 2:
                    act.wait_ge(s_h, j - 1)
                act.activation(xnT[v], pb(6 + v)[:, 0:P], ACT.Identity, bias=ln_b, scale=ln_g).then_inc(s_gTc, 1)

            def copy_weights(j, v):
                e = act.value_load(owner[0:1, bass.ds(j, 1)], min_val=0, max_val=E - 1)
                if not isinstance(j, int) or j >= 2:
                    act.wait_ge(s_h, j - 1)
                    act.sem_inc(s_stand_act, 1)
                act.copy(w1s[v], w1[:, bass.ds(e, 1), :].rearrange("p o f -> p (o f)")).then_inc(s_wc, 1)

            def relu(j, v):
                act.wait_ge(s_hc, j + 1)
                if not isinstance(j, int) or j >= 2:
                    act.wait_ge(s_yp, j - 1)
                act.activation(hidT[v], hid[v], ACT.Relu).then_inc(s_hTc, 1)

            def step(j, n, first, last):
                if not last:
                    block_T(j + 1, (n + 1) % 2)
                    copy_weights(j + 1, (n + 1) % 2)
                if not first:
                    relu(j - 1, (n + 1) % 2)

            act.wait_ge(s_ew, 32)
            act.wait_ge(s_slot, 2)
            copy_weights(0, 0)
            block_T(0, 0)
            for n in range(U):
                step(n, n, n == 0, False)
            with act.Fori(1, NBLK // U) as i:
                for n in range(U):
                    step(U * i + n, n, False, False)
            for j in range(NBLK - NBLK % U, NBLK):
                step(j, j % U, False, j == NBLK - 1)
            relu(NBLK - 1, (NBLK - 1) % 2)

        @block.vector
        def _(dve):
            def pad_keys(b):
                dve.wait_ge(s_ldk, 16 * NLD * (b + 1))
                if not isinstance(b, int) or b >= RING:
                    dve.wait_ge(s_stt, 8 * (b - RING) + 8)
                for h in range(2):
                    dve.tensor_scalar(K[:, bass.ds(b % RING, 1), :, h, :].rearrange("p o n t -> p (o n) t"),
                                       K0[:].rearrange("p (n t) -> p n t", n=NP), own_rows[:, h:h + 1],
                                       one_rows[:, h:h + 1], ALU.mult, ALU.add).then_inc(s_pad, 1)

            def stats(c):
                sl = slice(CT * c, CT * c + CT)
                dve.wait_ge(s_x[c], 16)
                for t in range(CT * c, CT * c + CT):
                    ins = dve.bn_stats(st6[:, t, :], x_sb[:, t, :])
                ins.then_inc(s_st, 1)
                dve.wait_ge(s_st, 3 * c + 1)
                for t in range(CT * c, CT * c + CT):
                    ins = dve.bn_aggr(mv[:, t, :], st6[:, t, :])
                ins.then_inc(s_st, 1)
                dve.wait_ge(s_st, 3 * c + 2)
                dve.tensor_scalar(rstd[:, sl], mv[:, sl, 1], EPS, None, ALU.add).then_inc(s_st, 1)

            def xhat(c):
                dve.wait_ge(s_rstd, c + 1)
                if c >= 2:
                    dve.wait_ge(s_xTp, c - 1)
                for i in range(CT):
                    t = CT * c + i
                    ins = dve.tensor_scalar(xh[:, c % 2, i, :], x_sb[:, t, :], mv[:, t, 0:1], rstd[:, t:t + 1],
                                            ALU.subtract, ALU.mult)
                ins.then_inc(s_xh, 1)

            def split(c, parts=range(3)):
                for j in parts:
                    at = 3 * c + j
                    first = 2 if j == 1 else 0
                    dve.wait_ge(s_full, at + 1)
                    if c:
                        dve.wait_ge(s_p3, at - 2)
                    dve.tensor_tensor(rest[:, j, :], full[:, j, :], piece[c % 2][:, j, first, :],
                                      ALU.subtract).then_inc(s_p2, 1)
                    dve.wait_ge(s_p2, at + 1)
                    if j == 0 and c >= 2:
                        dve.wait_ge(s_pw[c - 2], 16 * 6)
                    dve.tensor_copy(piece[c % 2][:, j, 1, :], rest[:, j, :]).then_inc(s_p2b, 1)

            stats(0)
            dve.wait_ge(s_w, 16 * len(weights))
            dve.tensor_scalar(b_col[:, 0:1], b_col[:, 0:1], SCALE, None, ALU.mult).then_inc(s_wp, 1)
            dve.tensor_scalar(b_col[:, 2:3], b_col[:, 2:3], SCALE, None, ALU.mult).then_inc(s_wp, 1)
            xhat(0)
            stats(1)
            xhat(1)
            dve.wait_ge(s_tanh, 1)
            dve.tensor_tensor(bvs[:], bv_col[:, 0:1], bv_col[:, 1:2], ALU.add).then_inc(s_bvs, 1)
            dve.tensor_scalar(w_p, w_p, tanh_g[:, 0:1], None, ALU.mult).then_inc(s_wp, 1)
            dve.tensor_scalar(bp_bc, bp_bc, tanh_g[:, 0:1], None, ALU.mult).then_inc(s_wp, 1)
            dve.wait_ge(s_bvs, 1)
            dve.tensor_copy(bvs_w[:], bvs[:, 0:1].to_broadcast([P, P])).then_inc(s_bvs, 1)
            stats(2)
            stats(3)
            for c in range(nchunk):
                if c < nchunk - 2:
                    xhat(c + 2)
                if c < nchunk - 1:
                    split(c)
                if c == 0:
                    dve.wait_ge(s_vcps, 1)
                    dve.tensor_copy(vc_all[:, 0:4, :], pb(7).rearrange("p (b c) -> p b c", b=4)).then_inc(s_vc, 1)
                    dve.wait_ge(s_kcf, 1)
                    dve.tensor_copy(cpiece[:, 2, :], cfull).then_inc(s_kcp, 1)
                    dve.wait_ge(s_kcp, 1)
                    dve.tensor_tensor(cfull, cfull, cpiece[:, 2, :], ALU.subtract).then_inc(s_kcp, 1)
                    dve.wait_ge(s_kcp, 2)
                    dve.tensor_copy(cpiece[:, 1, :], cfull).then_inc(s_kcp, 1)
                    dve.wait_ge(s_kcp, 3)
                    dve.tensor_tensor(cpiece[:, 0, :], cfull, cpiece[:, 1, :], ALU.subtract).then_inc(s_kcp, 1)
                if c == 1:
                    dve.wait_ge(s_vcps, 2)
                    dve.tensor_copy(vc_all[:, 4:8, :], pb(6).rearrange("p (b c) -> p b c", b=4)).then_inc(s_vc, 1)
                    dve.wait_ge(s_bmm, 1)
                    dve.tensor_tensor(att_bias[:], pb(7)[:, 0:C], bp_bc, ALU.add).then_inc(s_abias, 1)
                if c == 2:
                    pad_keys(0)
                    dve.wait_ge(s_kcl, 16 * 3)
                    for h in range(2):
                        dve.tensor_scalar(Kc[:, :, h, :], Kc0.rearrange("p (n t) -> p n t", t=TC),
                                          own_rows[:, h:h + 1], one_rows[:, h:h + 1], ALU.mult,
                                          ALU.add).then_inc(s_kcpad, 1)
            def reduce(hf, j):
                g = 4 * hf + j
                at = score_banks(hf, j)[0]
                for i in range(2):
                    dve.wait_ge(s_s, 2 * g + i + 1)
                    dve.tensor_reduce(top[:, j, 8 * i:8 * i + 8], pb(at[i]).rearrange("p (g k) -> p g k", k=64), AX_X,
                                      ALU.max).then_inc(s_red, 1)

            def maxima(hf):
                Mv = M[:, 0:32].rearrange("p (h y n u) -> p y h n u", y=2, h=2, n=4)
                dve.wait_ge(s_red, 8 * hf + 8)
                if not isinstance(hf, int) or hf >= 1:
                    dve.wait_ge(s_mt, hf)
                dve.tensor_reduce(Mv[:, 0, :, :, 1].rearrange("p h n -> p n h"),
                                  top[:, :, 0:8].rearrange("p n (h g) -> p n h g", h=2), AX_X, ALU.max).then_inc(s_m, 1)
                dve.tensor_reduce(Mv[:, 0, :, :, 0].rearrange("p h n -> p n h"),
                                  top[:, :, 8:12].rearrange("p n (h g) -> p n h g", h=2), AX_X, ALU.max).then_inc(s_m, 1)
                for u in range(2):
                    dve.tensor_copy(Mv[:, 1, :, :, u].rearrange("p h n -> p n h"),
                                    top[:, :, 12 + 2 * u:14 + 2 * u]).then_inc(s_m, 1)
                dve.wait_ge(s_m, 4 * hf + 4)

            def shift2(hf):
                dve.wait_ge(s_n1, hf + 1)
                dve.scalar_tensor_tensor(out=shift[:, 1, :], in0=pb(7)[0:32, 0:P], scalar=-1.0,
                                         in1=shift[:, 0, :], op0=ALU.mult, op1=ALU.subtract).then_inc(s_n2, 1)

            def normalise(hf):
                O = pb(7).rearrange("p (g r) -> p g r", r=16)
                dve.wait_ge(s_ot, hf + 1)
                dve.reciprocal(rec[:], O[:, :, 8]).then_inc(s_rec, 1)
                dve.wait_ge(s_rec, hf + 1)
                if not isinstance(hf, int) or hf >= 1:
                    dve.wait_ge(s_y, hf)
                dve.tensor_tensor(yn[:].rearrange("p y u (g d) -> p (y u g) d", d=D), O[:, :, 0:8],
                                  rec[:].unsqueeze(2).to_broadcast([P, 32, D]), ALU.mult).then_inc(s_yn, 1)

            def x1(b):
                dve.wait_ge(s_att, b + 1)
                dve.wait_ge(s_xb, b + 1)
                dve.tensor_tensor(x_sb[:, bass.ds(2 * b, 2), :], pb(7)[:, 0:2 * C]
                                  .rearrange("p (u c) -> p u c", u=2), xb[:], ALU.add).then_inc(s_x1, 1)

            def ffn_stats(b):
                at = 3 * b
                dve.wait_ge(s_x1, b + 1)
                for i in range(2):
                    ins = dve.bn_stats(st6z[:, i, :], x_sb[:, bass.ds(2 * b + i, 1), :].rearrange("p o c -> p (o c)"))
                ins.then_inc(s_zst, 1)
                dve.wait_ge(s_zst, at + 1)
                dve.sem_inc(s_stand_dve, 1)
                for i in range(2):
                    ins = dve.bn_aggr(mvz[:, i, :], st6z[:, i, :])
                ins.then_inc(s_zst, 1)
                dve.wait_ge(s_zst, at + 2)
                dve.tensor_scalar(rs[:, 0, :], mvz[:, :, 1], EPS, None, ALU.add).then_inc(s_zst, 1)

            def z_norm(b):
                dve.wait_ge(s_zr, 5 * b + 1)
                if not isinstance(b, int) or b >= 1:
                    dve.wait_ge(s_xn, 2 * b)
                for i in range(2):
                    dve.tensor_scalar(z[:, i, :], x_sb[:, bass.ds(2 * b + i, 1), :].rearrange("p o c -> p (o c)"),
                                      mvz[:, i, 0:1], rs[:, 0, i:i + 1], ALU.subtract, ALU.mult).then_inc(s_z, 1)

            def logits(b):
                dve.wait_ge(s_lgp, b + 1)
                dve.tensor_tensor(logit[:],
                                  pb(7)[:, 0:2 * E].rearrange("p (t e) -> p t e", t=2),
                                  br_bc.unsqueeze(1).to_broadcast([P, 2, E]), ALU.add).then_inc(s_lg, 1)

            two = lambda v: v.unsqueeze(1).to_broadcast([P, 2, E])
            each = lambda v: v.unsqueeze(2).to_broadcast([P, 2, E])

            def choose(b, n):
                at = NRT * b
                if n == 1:
                    dve.wait_ge(s_lg, b + 1)
                    dve.tensor_reduce(top1[:], logit[:], AX_X, ALU.max).then_inc(s_rt, 1)
                if n == 2:
                    dve.wait_ge(s_rt, at + 1)
                    dve.tensor_tensor(work[:], logit[:], each(top1[:]), ALU.subtract).then_inc(s_rt, 1)
                if n == 3:
                    dve.wait_ge(s_rt, at + 1)
                    dve.tensor_tensor(ties[:], logit[:], each(top1[:]), ALU.is_equal).then_inc(s_rt, 1)
                if n == 4:
                    dve.wait_ge(s_rt, at + 3)
                    dve.tensor_tensor(ties[:], ties[:], two(desc[:]), ALU.mult).then_inc(s_rt, 1)
                if n == 5:
                    dve.wait_ge(s_rt, at + 4)
                    dve.tensor_reduce(last[:], ties[:], AX_X, ALU.max).then_inc(s_rt, 1)
                if n == 6:
                    dve.wait_ge(s_rt, at + 5)
                    dve.tensor_tensor(onehot[:], two(desc[:]), each(last[:]), ALU.is_equal).then_inc(s_rt, 1)

            def place(b, n):
                at = NRT * b
                if n == 7:
                    dve.wait_ge(s_ge, b + 1)
                    dve.tensor_reduce(gate[:], work[:], AX_X, ALU.add).then_inc(s_rt, 1)
                if n == 8:
                    dve.wait_ge(s_rt, at + 7)
                    dve.reciprocal(gate[:], gate[:]).then_inc(s_rt, 1)
                if n == 9:
                    dve.wait_ge(s_rt, at + 8)
                    if isinstance(b, int) and b != B - 2:
                        dve.wait_ge(s_xn, 2 * b + 2)
                    dve.tensor_scalar(rcd[:, buf(b), :, 2 * C], gate[:], tanh_g[:, 1:2], None, ALU.mult).then_inc(s_rt, 1)
                if n == 10:
                    dve.wait_ge(s_rkp, b + 1)
                    dve.tensor_tensor(pos[:], pb(7)[:, P:P + 2 * E].rearrange("p (t e) -> p t e", t=2), two(fill[:]),
                                      ALU.add).then_inc(s_rt, 1)
                if n == 11:
                    dve.wait_ge(s_rt, at + 10)
                    dve.tensor_tensor(fill[:], fill[:], pb(7)[:, P + 2 * E:P + 3 * E], ALU.add).then_inc(s_rt, 1)
                if n == 12:
                    dve.wait_ge(s_rt, at + 10)
                    dve.tensor_tensor(pos[:], pos[:], onehot[:], ALU.mult).then_inc(s_rt, 1)
                if n == 13:
                    dve.wait_ge(s_rt, at + 12)
                    dve.tensor_reduce(slot_f[:], pos[:], AX_X, ALU.add).then_inc(s_rt, 1)
                if n == 14:
                    dve.tensor_copy(rcd[:, buf(b), :, 2 * C + 1].bitcast(I32), tok[:]).then_inc(s_rt, 1)
                if n == 15:
                    dve.wait_ge(s_rt, at + 14)
                    dve.tensor_scalar(tok[:], tok[:], float(T), None, ALU.add).then_inc(s_rt, 1)
                if n == 16:
                    dve.wait_ge(s_rt, at + 13)
                    dve.tensor_copy(slot[:, buf(b)], slot_f[:]).then_inc(s_rt, 1)

            def body(b, prev3, prev2, prev, p1a, p1b):
                for k in range(NP):
                    if prev3:
                        for n in ((7,), (8,), (12,), (13, 14), (15, 16))[k] if k < 5 else ():
                            place(b - 3, n)
                    if (p1a and k < 4) or (p1b and k >= 4):
                        reduce(2 * b + 3 + k // 4, k % 4)
                    if prev and k == 0:
                        normalise(2 * b - 2)
                    if prev2 and k == 0:
                        ffn_stats(b - 2)
                    if prev2 and k == 1:
                        z_norm(b - 2)
                    if p1a and k == 1:
                        shift2(2 * b + 2)
                    if p1b and k == 2:
                        pad_keys(b + 2)
                    if prev and k == 3:
                        normalise(2 * b - 1)
                    if prev2 and k == 4:
                        logits(b - 2)
                    if p1a and k == 5:
                        shift2(2 * b + 3)
                    if prev and k == 7:
                        x1(b - 1)
                    if (p1a and k == 3) or (p1b and k == 7):
                        maxima(2 * b + 3 + k // 4)
                    if prev3 and k == 1:
                        for n in (9, 10, 11):
                            place(b - 3, n)
                        if isinstance(b, int) and b - 3 == B - 1:
                            dve.wait_ge(s_rt, NRT * (b - 3) + 11)
                            dve.tensor_copy(fill_i[:], fill[:]).then_inc(s_slot, 1)
                    if prev2:
                        for n in ((1,), (2, 3), (4,), (5, 6))[k - 4] if k >= 4 else ():
                            choose(b - 2, n)

            for hf in range(3):
                for j in range(4):
                    reduce(hf, j)
                    if hf and j == 2:
                        shift2(hf - 1)
                maxima(hf)
                if hf == 0:
                    pad_keys(1)
                split(nchunk - 1, (hf,))
            dve.wait_ge(s_io, 6)
            dve.tensor_scalar(desc[:], iota[:, 0:E], -1.0, float(E), ALU.mult, ALU.add).then_inc(s_pre, 1)
            dve.tensor_copy(tok[:], tok_i[:]).then_inc(s_pre, 1)
            dve.tensor_copy(region[:], region_i[:]).then_inc(s_pre, 1)
            dve.tensor_copy(fill[:], region_i[:]).then_inc(s_pre, 1)
            dve.tensor_scalar(iota_p[:], iota[:], float(P), None, ALU.mult).then_inc(s_pre, 1)
            dve.wait_ge(s_pre, 5)
            body(0, False, False, False, True, True)
            body(1, False, False, True, True, True)
            body(2, False, True, True, True, True)
            with dve.Fori(3, 6) as b:
                body(b, True, True, True, True, True)
            body(6, True, True, True, True, False)
            body(7, True, True, True, False, False)
            body(8, True, True, True, False, False)
            body(9, True, True, False, False, False)
            body(10, True, False, False, False, False)

            step = [NRT * B]

            def did(ins):
                step[0] += 1
                ins.then_inc(s_rt, 1)
                dve.wait_ge(s_rt, step[0])

            did(dve.tensor_tensor(count[:], fill[:], region[:], ALU.subtract))
            did(dve.tensor_tensor(over[:], count[:].unsqueeze(2).to_broadcast([P, E, NT]),
                                  iota_p[:, 0:NT].unsqueeze(1).to_broadcast([P, E, NT]), ALU.is_gt))
            did(dve.tensor_reduce(nblk[:], over[:], AX_X, ALU.add))
            a_, b_ = nblk, nb[0]
            for sh in (1, 2, 4):
                dve.tensor_copy(b_[:, 0:sh], a_[:, 0:sh]).then_inc(s_rt, 1)
                step[0] += 1
                did(dve.tensor_tensor(b_[:, sh:E], a_[:, sh:E], a_[:, 0:E - sh], ALU.add))
                a_, b_ = b_, nb[1] if b_ is nb[0] else nb[0]
            did(dve.tensor_tensor(passed[:], iota[:, 0:NBLK].unsqueeze(2).to_broadcast([P, NBLK, E]),
                                  a_[:].unsqueeze(1).to_broadcast([P, NBLK, E]), ALU.is_ge))
            did(dve.tensor_reduce(own_f[:], passed[:], AX_X, ALU.add))
            did(dve.tensor_scalar(own_f[:], own_f[:], float(E - 1), None, ALU.min))
            did(dve.tensor_copy(owner[:], own_f[:]))
            did(dve.tensor_scalar(jump[:], nblk[:], -float(P), float(STRIDE), ALU.mult, ALU.add))
            did(dve.tensor_tensor(passed[:], passed[:], jump[:].unsqueeze(1).to_broadcast([P, NBLK, E]), ALU.mult))
            did(dve.tensor_reduce(row_f[:], passed[:], AX_X, ALU.add))
            did(dve.tensor_tensor(row_f[:], row_f[:], iota_p[:, 0:NBLK], ALU.add))
            did(dve.tensor_scalar(row_f[:], row_f[:], float(E * STRIDE), None, ALU.min))
            dve.tensor_copy(row_i[:], row_f[:]).then_inc(s_slot, 1)

            def bias1(j, n):
                e = dve.value_load(owner[0:1, bass.ds(j, 1)], min_val=0, max_val=E - 1)
                dve.wait_ge(s_h, j + 1)
                if not isinstance(j, int) or j >= 2:
                    dve.wait_ge(s_hTc, j - 1)
                dve.tensor_tensor(hid[n % 2].rearrange("p (k t) -> p k t", k=FC),
                                  pb(n % 2).rearrange("p (k t) -> p k t", k=FC),
                                  b1_col[:, bass.ds(e, 1), :].rearrange("p o k -> p (o k)").unsqueeze(2)
                                  .to_broadcast([P, FC, P]), ALU.add).then_inc(s_hc, 1)

            def bias2(j, v, turn):
                e = dve.value_load(owner[0:1, bass.ds(j, 1)], min_val=0, max_val=E - 1)
                dve.wait_ge(s_yp, j + 1)
                dve.tensor_tensor(yb[v % 2], pb(4 + v % 2)[:, 0:C], b2_bc[:, bass.ds(e, 1), :]
                                  .rearrange("p o f -> p (o f)"), ALU.add).then_inc(s_yb, 1)
                if not isinstance(turn, int) or turn >= 1:
                    dve.wait_ge(s_yw[v], 16 * turn)
                dve.tensor_copy(yg[v][:, C:C + 1].bitcast(I32), rx[v][:, XW - 1:XW].bitcast(I32)).then_inc(s_yc, 1)
                dve.wait_ge(s_yb, j + 1)
                dve.scalar_tensor_tensor(out=yg[v][:, 0:C], in0=yb[v % 2], scalar=rx[v][:, 2 * C:2 * C + 1],
                                         in1=rx[v][:, C:2 * C], op0=ALU.mult, op1=ALU.add).then_inc(s_yc, 1)

            dve.wait_ge(s_eb, 16)
            for n in range(U):
                bias1(n, n)
                if n >= 2:
                    bias2(n - 2, n - 2, 0)
            for j in (U, U + 1):
                bias1(j, j % U)
                bias2(j - 2, j - 2, 0)
            last_turn = (NBLK - 2) // U
            with dve.Fori(1, last_turn) as i:
                for n in range(U):
                    bias1(U * i + n + 2, n)
                    bias2(U * i + n, n, i)
            for j in range(U * last_turn, NBLK):
                if j + 2 < NBLK:
                    bias1(j + 2, j % U)
                bias2(j, j % U, last_turn)

        @block.tensor
        def _(pe):
            pe.wait_ge(s_cst, 10)
            pe.wait_ge(s_w, 16 * len(weights))
            for i in range(4):
                ins = pe.transpose(pb(7)[0:TC, P * i:P * i + P], ctx_sb[:, i, :], ident[:])
            ins.then_inc(s_ctxT, 1)

            def transposes(c):
                pe.wait_ge(s_xh, c + 1)
                if c >= 2:
                    pe.wait_ge(s_xT, c - 1)
                for i in range(CT):
                    ins = pe.transpose(pb(5 * (c % 2))[:, P * i:P * i + P], xh[:, c % 2, i, :], ident[:])
                ins.then_inc(s_xTp, 1)

            def context_values(i, bank):
                for j in range(4):
                    ins = pe.matmul(pb(bank)[:, C * j:C * j + C],
                                    ctxT2[:, 4 * i + j].rearrange("p u t -> p (u t)"), w_cv, start=True, stop=True)
                ins.then_inc(s_vcps, 1)

            transposes(0)
            for c in range(nchunk):
                pe.wait_ge(s_xT, c + 1)
                for j in range(3):
                    if c:
                        pe.wait_ge(s_full, 3 * (c - 1) + j + 1)
                    pe.matmul(pb(1 + j), w_q[:, j, :], xT[:, c % 2], start=True, stop=True).then_inc(s_pr, 1)
                    if j == 1 and c < nchunk - 1:
                        transposes(c + 1)
                if c:
                    pe.wait_ge(s_v, c)
                for i in range(CT):
                    ins = pe.matmul(pb(4)[:, C * i:C * i + C], xT[:, c % 2, P * i:P * i + P], w_v, start=True, stop=True)
                ins.then_inc(s_pr, 1)
                if c == 0:
                    pe.wait_ge(s_ctxs, 3)
                    pe.matmul(pb(6), w_ck, ctxT[:], start=True, stop=True).then_inc(s_kcps, 1)
                    context_values(0, 7)
                if c == 1:
                    pe.wait_ge(s_kcf, 1)
                    context_values(1, 6)
                    pe.wait_ge(s_bvs, 2)
                    pe.wait_ge(s_wp, 4)
                    pe.wait_ge(s_vc, 1)
                    pe.matmul(pb(7)[:, 0:C], bvs_w[:], w_p, start=True, stop=True).then_inc(s_bmm, 1)

            def pass1(hf, b, half, j):
                hp = 4 * half + j
                at, before_it = score_banks(hf, j)
                slot = bass.ds(b % RING, 1)
                k2 = K[:, slot, hp].rearrange("p o h t -> p (o h) t")
                q2 = QQ[:, slot, 0, hp].rearrange("p o t -> p (o t)")
                qc2 = QQ[:, slot, 1, hp].rearrange("p o t -> p (o t)")
                kc2 = Kc[:, bass.ds(hp * B + b, 1)].rearrange("p o h t -> p (o h t)")
                mask = causal[:].unsqueeze(1).to_broadcast([P, 2, P])
                b0, b1 = pb(at[0]), pb(at[1])
                if before_it is not None:
                    pe.wait_ge(s_red, 2 * before_it + 1)
                pe.matmul(b0, q2[:, P:T], k2, start=True, stop=True)
                pe.matmul(b0.rearrange("p (h t) -> p h t", h=2)[:, :, P:T], ident_bf[:], mask, start=False, stop=True,
                          skip_group_check=True).then_inc(s_s, 1)
                if before_it is not None:
                    pe.wait_ge(s_red, 2 * before_it + 2)
                pe.matmul(b1[:, 0:256], q2[:, 0:P], k2[:, :, 0:P], start=True, stop=False)
                pe.matmul(b1[:, 0:256].rearrange("p (h t) -> p h t", h=2), ident_bf[:], mask, start=False, stop=True)
                pe.matmul(b1[:, 256:384], qc2[:, 0:P], kc2, start=True, stop=True)
                pe.matmul(b1[:, 384:512], qc2[:, P:T], kc2, start=True, stop=True).then_inc(s_s, 1)

            def pass2(b, k):
                g = 8 * b + k
                if not isinstance(b, int) or g >= 2:
                    pe.wait_ge(s_exp, g - 1)
                else:
                    pe.wait_ge(s_red, 2 * (9 + g) + 2)
                if k % 4 == 0:
                    pe.wait_ge(s_mr, 16 * (2 * b + k // 4 + 1))
                slot = bass.ds(b % RING, 1)
                k2 = K[:, slot, k].rearrange("p o h t -> p (o h) t")
                q2 = QQ[:, slot, 0, k].rearrange("p o t -> p (o t)")
                qc2 = QQ[:, slot, 1, k].rearrange("p o t -> p (o t)")
                b0, b1 = pb(2 + 2 * (k % 2)), pb(3 + 2 * (k % 2))
                for hh in range(2):
                    pe.matmul(b0[:, T * hh:T * hh + T], k2[:, hh, 0:P], q2, start=True, stop=True)
                    pe.matmul(b1[:, T * hh:T * hh + P], k2[:, hh, P:T], q2[:, P:T], start=True, stop=True)
                pe.matmul(b1.rearrange("p (g q) -> p g q", q=256)[:, :, P:256], Kc[:, bass.ds(k * B + b, 1)].rearrange("p o h t -> p (o h t)"),
                          qc2.rearrange("p (g q) -> p g q", q=P), start=True, stop=True).then_inc(s_stt, 1)

            def pv(hf, half, steps):
                if steps[0] == 0:
                    pe.wait_ge(s_sel, 4 * hf + 4)
                O = pb(6)
                for step in steps:
                    for q in range(4):
                        rows = slice(32 * q, 32 * q + 32)
                        pr = probs[:, 4 * half + q, :]
                        hh, kb = ((0, 0), (0, 1), (1, 1), (1, 0), (0, 0))[step]
                        if step == 4:
                            ins = pe.matmul(O[rows, 256:512].rearrange("p (g q) -> p g q", q=P), Vcz[:, half, q, :],
                                            pr[:, 512:1024].rearrange("p (g q) -> p g q", q=256)[:, :, P:256],
                                            start=True, stop=True)
                            continue
                        win = slice(16, 48) if hh == 0 else slice(0, 32)
                        lhs = Vz[:, half, kb, 2 * q + hh, win]
                        if kb == 0:
                            pe.matmul(O[rows, 0:T], lhs, pr[:, T * hh:T * hh + T], start=(hh == 0),
                                      stop=(hh == 1))
                        else:
                            pe.matmul(O[rows, P:T], lhs, pr[:, 512 + T * hh:512 + T * hh + P], start=False,
                                      stop=False)
                if steps[-1] == 4:
                    ins.then_inc(s_pv, 1)

            def max_T(hf):
                pe.wait_ge(s_m, 4 * hf + 4)
                pe.transpose(pb(7)[:, 0:P], M[:], ident[:]).then_inc(s_mt, 1)

            def o_T(hf):
                pe.wait_ge(s_osb, hf + 1)
                for i in range(4):
                    ins = pe.transpose(pb(7)[:, P * i:P * i + P], o_sb[:, P * i:P * i + P], ident[:])
                ins.then_inc(s_ot, 1)

            def y_T(b):
                pe.wait_ge(s_y, 2 * b + 2)
                for i in range(2):
                    ins = pe.transpose(pb(7)[:, P * i:P * i + P], y_sb[:, i, :], ident[:])
                ins.then_inc(s_yt, 1)

            def project(b):
                pe.wait_ge(s_yts, b + 1)
                for i in range(2):
                    ins = pe.matmul(pb(7)[:, C * i:C * i + C], yT[:, P * i:P * i + P], w_p, start=True, stop=True)
                ins.then_inc(s_att, 1)

            def z_T(b):
                pe.wait_ge(s_z, 2 * b + 2)
                for i in range(2):
                    ins = pe.transpose(pb(7)[:, P * i:P * i + P], z[:, i, :], ident[:])
                ins.then_inc(s_zTp, 1)

            def route(b):
                pe.wait_ge(s_zT, b + 1)
                for i in range(2):
                    ins = pe.matmul(pb(7)[:, E * i:E * i + E], zT[:, P * i:P * i + P], w_r, start=True, stop=True)
                ins.then_inc(s_lgp, 1)

            def counts(b):
                pe.wait_ge(s_rt, NRT * b + 6)
                prefix, total = pb(7)[:, P:P + 2 * E], pb(7)[:, P + 2 * E:P + 3 * E]
                pe.matmul(prefix[:, 0:E], before[:], onehot[:, 0, :], start=True, stop=True)
                pe.matmul(prefix[:, E:2 * E], before[:], onehot[:, 1, :], start=True, stop=False)
                pe.matmul(prefix[:, E:2 * E], ones_bf[:], onehot[:, 0, :], start=False, stop=True)
                pe.matmul(total, ones_bf[:], onehot[:, 0, :], start=True, stop=False)
                pe.matmul(total, ones_bf[:], onehot[:, 1, :], start=False, stop=True).then_inc(s_rkp, 1)

            def body(b, prev3, prev2, prev, cur, p1a, p1b):
                for k in range(NP):
                    if cur:
                        pass2(b, k)
                    if p1a and k < 4:
                        pass1(2 * b + 3, b + 1, 1, k)
                    if p1b and k >= 4:
                        if k == 4:
                            pe.wait_ge(s_ldq, 16 * NLD * (b + 3))
                            pe.wait_ge(s_pad, 2 * (b + 3))
                        pass1(2 * b + 4, b + 2, 0, k - 4)
                    if prev and k == 0:
                        if prev2:
                            pe.wait_ge(s_x1, b - 1)
                        o_T(2 * b - 2)
                    if prev and k in (1, 2):
                        pv(2 * b - 1, 1, PARTS[k - 1])
                    if prev and k == 1:
                        pe.wait_ge(s_yn, 2 * b - 1)
                    if prev3 and k == 1:
                        if not prev2:
                            pe.wait_ge(s_lg, b - 2)
                        counts(b - 3)
                    if p1a and k == 1:
                        max_T(2 * b + 2)
                    if prev3 and k == 2:
                        pe.wait_ge(s_rt, NRT * (b - 3) + 11)
                    if prev2 and k == 2:
                        if p1a:
                            pe.wait_ge(s_n2, 2 * b + 3)
                        elif prev:
                            pe.wait_ge(s_yn, 2 * b - 1)
                        else:
                            pe.wait_ge(s_x1, b - 1)
                        z_T(b - 2)
                    if prev and k == 3:
                        if prev2:
                            pe.wait_ge(s_zT, b - 1)
                        elif p1a:
                            pe.wait_ge(s_n2, 2 * b + 3)
                        o_T(2 * b - 1)
                    if prev2 and k == 4:
                        if prev:
                            pe.wait_ge(s_yn, 2 * b)
                        route(b - 2)
                    if p1a and k == 5:
                        if prev2:
                            pe.wait_ge(s_lg, b - 1)
                        elif prev:
                            pe.wait_ge(s_yn, 2 * b)
                        else:
                            pe.wait_ge(s_n2, 3)
                        max_T(2 * b + 3)
                    if cur and k in (5, 6):
                        pv(2 * b, 0, PARTS[k - 5])
                    if prev and k == 6:
                        if p1a:
                            pe.wait_ge(s_n2, 2 * b + 4)
                        else:
                            pe.wait_ge(s_lg, b - 1)
                        y_T(b - 1)
                    if prev and k == 7:
                        project(b - 1)

            pe.wait_ge(s_abias, 1)
            pe.wait_ge(s_vc, 2)
            pe.wait_ge(s_kcpad, 2)
            for hf in range(3):
                if hf % 2 == 0:
                    pe.wait_ge(s_ldq, 16 * NLD * (hf // 2 + 1))
                    pe.wait_ge(s_pad, 2 * (hf // 2 + 1))
                if hf == 1:
                    pe.wait_ge(s_full, 3 * nchunk)
                    pe.wait_ge(s_v, nchunk)
                for j in range(4):
                    pass1(hf, hf // 2, hf % 2, j)
                    if hf and j == 1:
                        if hf == 2:
                            pe.wait_ge(s_n2, 1)
                        max_T(hf - 1)
            pe.wait_ge(s_n2, 2)
            body(0, False, False, False, True, True, True)
            body(1, False, False, True, True, True, True)
            body(2, False, True, True, True, True, True)
            with pe.Fori(3, 6) as b:
                body(b, True, True, True, True, True, True)
            body(6, True, True, True, True, True, False)
            body(7, True, True, True, True, False, False)
            body(8, True, True, True, False, False, False)
            body(9, True, True, False, False, False, False)
            body(10, True, False, False, False, False, False)

            def block_T(j, v, turn):
                pe.wait_ge(s_rx[v], 16 * (turn + 1))
                if not isinstance(j, int) or j >= 2:
                    pe.wait_ge(s_gTc, j - 1)
                pe.transpose(pb(6 + v % 2)[:, 0:P], rx[v][:, 0:C], ident[:]).then_inc(s_gT, 1)

            def expert(j):
                return pe.value_load(owner[0:1, bass.ds(j, 1)], min_val=0, max_val=E - 1)

            def hidden(j, n):
                pe.wait_ge(s_gTc, j + 1)
                pe.wait_ge(s_wc, j + 1)
                if not isinstance(j, int) or j >= 2:
                    pe.wait_ge(s_hc, j - 1)
                for k in range(FC):
                    ins = pe.matmul(pb(n % 2)[:, P * k:P * k + P], w1s[n % 2][:, P * k:P * k + P], xnT[n % 2],
                                    start=True, stop=True)
                ins.then_inc(s_h, 1)

            def outp(j, v, e):
                pe.wait_ge(s_hTc, j + 1)
                if not isinstance(j, int) or j >= 2:
                    pe.wait_ge(s_yb, j - 1)
                for k in range(FC):
                    ins = pe.matmul(pb(4 + v)[:, 0:C], hidT[v][:, P * k:P * k + P],
                                    w2[:, bass.ds(e, 1), k, :].rearrange("p o c -> p (o c)"),
                                    start=(k == 0), stop=(k == FC - 1))
                ins.then_inc(s_yp, 1)

            def step(j, n, turn):
                e = expert(j - 2) if not isinstance(j, int) or j >= 2 else None
                if not isinstance(j, int) or j < NBLK - 1:
                    block_T(j + 1, (n + 1) % U, turn + (n + 1) // U)
                hidden(j, n)
                if not isinstance(j, int) or j >= 2:
                    outp(j - 2, n % 2, e)

            pe.wait_ge(s_ew, 32)
            pe.wait_ge(s_slot, 2)
            block_T(0, 0, 0)
            for n in range(U):
                step(n, n, 0)
            with pe.Fori(1, NBLK // U) as i:
                for n in range(U):
                    step(U * i + n, n, i)
            for j in range(NBLK - NBLK % U, NBLK):
                step(j, j % U, j // U)
            for j in (NBLK - 2, NBLK - 1):
                outp(j, j % 2, expert(j))


def _by_row(w):
    return w.reshape(-1, NP, 2, D).transpose(0, 3, 2, 1).reshape(-1, C)


def kernel(**inputs):
    import numpy as np
    import concourse.bacc as bacc
    from concourse.bass_utils import run_bass_kernel_spmd as run

    inp = {k: np.ascontiguousarray(v) for k, v in inputs.items()}
    att = lambda n: inp["L0_xattn_" + n]
    ffn = lambda n: inp["L0_ffn_" + n]
    col = lambda v: v.reshape(C, 1)
    rows = np.arange(P)
    own = np.stack([rows % 2 == h for h in range(2)], 1).astype(np.float32)
    ones = np.stack([(rows % 2 == h) & (rows >= SHIFT) & (rows < SHIFT + 2 * NS) for h in range(2)], 1).astype(np.float32)
    arrays = {
        "x": inp["x"].reshape(B * T, C), "ctx": inp["ctx_512"].reshape(B * TC, TC),
        "wpack": np.concatenate([_by_row(att("Wq")), _by_row(att("Wk")), _by_row(att("Wcq")), att("Wv"), att("Wp"),
                                 ffn("Wr")], 1),
        "cpack": np.concatenate([_by_row(att("Wck")), att("Wcv")], 1),
        "cols": np.concatenate([col(_by_row(att("bq"))), col(_by_row(att("bk"))), col(_by_row(att("bcq"))),
                                col(_by_row(att("bck"))), col(att("bv")), col(att("bcv")), col(ffn("ln_g")),
                                col(ffn("ln_b")), own, ones,
                                ffn("b1").reshape(E * FC, P).T], 1),
        "rpack": np.concatenate([att("bp"), ffn("br"), inp["g_xattn"].reshape(1), inp["g_ffn"].reshape(1)]),
        "b2": ffn("b2").reshape(-1),
        "w1": ffn("W1"), "w2": ffn("W2"),
    }
    arrays = {k: np.ascontiguousarray(v) for k, v in arrays.items()}
    nc = bacc.Bacc("TRN2", target_bir_lowering=False, num_devices=1)
    aps = {k: nc.dram_tensor("in_" + k, v.shape, mybir.dt.from_np(v.dtype), kind="ExternalInput").ap()
           for k, v in arrays.items()}
    out = nc.dram_tensor("out", [B * T, C], F32, kind="ExternalOutput").ap()
    build(nc, aps, out)
    r = run(nc, [{"in_" + k: v for k, v in arrays.items()}], core_ids=[0])
    return r.results[0]["out"].reshape(B, T, C)
```
